# Optimizing a Trainium2 kernel written in Bass

```python
import numpy as np
import jax
import jax.numpy as jnp

def _softmax(x, axis=-1):
    return jax.nn.softmax(x, axis=axis)

def _gelu(x):
    return jax.nn.gelu(x, approximate=True)

def _silu(x):
    return jax.nn.silu(x)

def _sigmoid(x):
    return jax.nn.sigmoid(x)

def _layernorm(x, axis=-1, eps=1e-05):
    m = jnp.mean(x, axis=axis, keepdims=True)
    v = jnp.var(x, axis=axis, keepdims=True)
    return (x - m) / jnp.sqrt(v + eps)

def _scatter_add(tgt, idx, src, axis=0):
    return tgt.at[idx].add(src)

def _segment_sum(src, seg, n):
    return jax.ops.segment_sum(src, seg, n)
kernel_name = 'mk_seq_preln_d2_jaxref_r8_3889a9'

def setup_inputs(seed: int=0):
    np.random.seed(seed)
    _w = jnp.asarray

    def _L0_attn_setup():
        import jax, jax.numpy as jnp
        import numpy as np
        import math
        D_MODEL = 256
        NUM_HEAD = 16
        HEAD_DIM = D_MODEL // NUM_HEAD

        def _trunc_normal(key, shape, std):
            return jax.random.truncated_normal(key, -3.0, 3.0, shape, dtype=jnp.float32) * std
        key = jax.random.key(seed)
        kx, kp, ko = jax.random.split(key, 3)
        b, s = (4, 256)
        x = jax.random.normal(kx, (b, s, D_MODEL), dtype=jnp.float32)
        sigma_p = math.sqrt(2.0 / (D_MODEL + 3 * D_MODEL))
        w_project = _trunc_normal(kp, (3 * D_MODEL, D_MODEL), sigma_p)
        sigma_o = math.sqrt(2.0 / (D_MODEL + D_MODEL))
        w_out = _trunc_normal(ko, (D_MODEL, D_MODEL), sigma_o)
        return {'x': x, 'w_project': w_project, 'w_out': w_out}
    _L0_attn_in = _L0_attn_setup()

    def _L0_ffn_setup():
        import jax, jax.numpy as jnp
        import numpy as np
        TOP_K = 2
        key = jax.random.key(seed)
        k1, k2, k3, k4, k5 = jax.random.split(key, 5)
        B, S, H, O, E = (2, 128, 256, 256, 8)
        hidden_states = jax.random.normal(k1, (B, S, H), dtype=jnp.float32)
        router_w = jax.random.normal(k2, (O * E, H), dtype=jnp.float32) * 0.02
        router_b = jnp.zeros((O * E,), dtype=jnp.float32)
        expert_w = jax.random.normal(k3, (E, O, H), dtype=jnp.float32) * 0.02
        expert_b = jnp.zeros((E, O), dtype=jnp.float32)
        return {'hidden_states': hidden_states, 'router_w': router_w, 'router_b': router_b, 'expert_w': expert_w, 'expert_b': expert_b}
    _L0_ffn_in = _L0_ffn_setup()

    def _L1_attn_setup():
        import jax, jax.numpy as jnp
        import numpy as np
        NUM_HEADS = 16
        NUM_KV_HEADS = 4
        HEAD_DIM = 128
        HIDDEN = 256
        SEQ = 256
        BATCH = 2
        Q_PER_GROUP = NUM_HEADS // NUM_KV_HEADS
        GROUP_SIZE = (Q_PER_GROUP + 2) * HEAD_DIM
        TOTAL_PROJ = NUM_KV_HEADS * GROUP_SIZE
        key = jax.random.key(seed)
        k1, k2, k3 = jax.random.split(key, 3)
        x = jax.random.normal(k1, (SEQ, BATCH, HIDDEN), dtype=jnp.float32)
        w_qkv = jax.random.normal(k2, (TOTAL_PROJ, HIDDEN), dtype=jnp.float32) * 0.02
        w_proj = jax.random.normal(k3, (HIDDEN, NUM_HEADS * HEAD_DIM), dtype=jnp.float32) * 0.02
        return {'x': x, 'w_qkv': w_qkv, 'w_proj': w_proj}
    _L1_attn_in = _L1_attn_setup()

    def _L1_ffn_setup():
        import jax, jax.numpy as jnp
        import numpy as np
        BLOCK_SIZE = 32
        HIDDEN_SIZE = 256
        MLP_DIM = 2048
        NVFP4_LUT = jnp.array([0.0, 0.5, 1.0, 1.5, 2.0, 3.0, 4.0, 6.0, 0.0, -0.5, -1.0, -1.5, -2.0, -3.0, -4.0, -6.0], dtype=jnp.float32)

        def dequant_nvfp4(W_packed, scales, block=BLOCK_SIZE):
            N = W_packed.shape[0]
            low = W_packed & 15
            high = W_packed >> 4 & 15
            idx = jnp.stack([low, high], axis=-1).reshape(N, -1)
            vals = NVFP4_LUT[idx]
            K = vals.shape[1]
            vals = vals.reshape(N, K // block, block) * scales[:, :, None]
            return vals.reshape(N, K)
        key = jax.random.key(seed)
        ks = jax.random.split(key, 7)
        x = jax.random.normal(ks[0], (4, 32, HIDDEN_SIZE), dtype=jnp.float32)
        gate_W_packed = jax.random.randint(ks[1], (MLP_DIM, HIDDEN_SIZE // 2), 0, 32, dtype=jnp.int32)
        gate_scales = jax.random.uniform(ks[2], (MLP_DIM, HIDDEN_SIZE // BLOCK_SIZE), dtype=jnp.float32) * 0.1 + 0.001
        up_W_packed = jax.random.randint(ks[3], (MLP_DIM, HIDDEN_SIZE // 2), 0, 32, dtype=jnp.int32)
        up_scales = jax.random.uniform(ks[4], (MLP_DIM, HIDDEN_SIZE // BLOCK_SIZE), dtype=jnp.float32) * 0.1 + 0.001
        down_W_packed = jax.random.randint(ks[5], (HIDDEN_SIZE, MLP_DIM // 2), 0, 32, dtype=jnp.int32)
        down_scales = jax.random.uniform(ks[6], (HIDDEN_SIZE, MLP_DIM // BLOCK_SIZE), dtype=jnp.float32) * 0.1 + 0.001
        return {'x': x, 'gate_W_packed': gate_W_packed, 'gate_scales': gate_scales, 'up_W_packed': up_W_packed, 'up_scales': up_scales, 'down_W_packed': down_W_packed, 'down_scales': down_scales}
    _L1_ffn_in = _L1_ffn_setup()
    _d = {'L0_attn_x': _L0_attn_in['x'], 'L0_attn_w_project': _L0_attn_in['w_project'], 'L0_attn_w_out': _L0_attn_in['w_out'], 'L0_ffn_router_w': _L0_ffn_in['router_w'], 'L0_ffn_router_b': _L0_ffn_in['router_b'], 'L0_ffn_expert_w': _L0_ffn_in['expert_w'], 'L0_ffn_expert_b': _L0_ffn_in['expert_b'], 'L1_attn_w_qkv': _L1_attn_in['w_qkv'], 'L1_attn_w_proj': _L1_attn_in['w_proj'], 'L1_ffn_gate_W_packed': _L1_ffn_in['gate_W_packed'], 'L1_ffn_gate_scales': _L1_ffn_in['gate_scales'], 'L1_ffn_up_W_packed': _L1_ffn_in['up_W_packed'], 'L1_ffn_up_scales': _L1_ffn_in['up_scales'], 'L1_ffn_down_W_packed': _L1_ffn_in['down_W_packed'], 'L1_ffn_down_scales': _L1_ffn_in['down_scales']}
    _x0 = _d['L0_attn_x']
    _d['L0_attn_x'] = jax.random.normal(jax.random.fold_in(jax.random.key(seed), 1), (4, 512, 256), dtype=_x0.dtype)
    del _x0
    return _d

def reference(L0_attn_x, L0_attn_w_project, L0_attn_w_out, L0_ffn_router_w, L0_ffn_router_b, L0_ffn_expert_w, L0_ffn_expert_b, L1_attn_w_qkv, L1_attn_w_proj, L1_ffn_gate_W_packed, L1_ffn_gate_scales, L1_ffn_up_W_packed, L1_ffn_up_scales, L1_ffn_down_W_packed, L1_ffn_down_scales):

    def _L0_attn_ref(x, w_project, w_out):
        import jax, jax.numpy as jnp
        import numpy as np
        import math
        D_MODEL = 256
        NUM_HEAD = 16
        HEAD_DIM = D_MODEL // NUM_HEAD

        def _trunc_normal(key, shape, std):
            return jax.random.truncated_normal(key, -3.0, 3.0, shape, dtype=jnp.float32) * std
        b, s, d = x.shape
        qkv = jnp.einsum('bsd,od->bso', x, w_project)
        qkv = qkv.reshape(b, s, 3, NUM_HEAD, HEAD_DIM)
        qkv = jnp.transpose(qkv, (2, 0, 3, 1, 4))
        q, k, v = (qkv[0], qkv[1], qkv[2])
        att = jnp.einsum('bhqd,bhkd->bhqk', q, k) / math.sqrt(HEAD_DIM)
        causal = jnp.triu(jnp.ones((s, s), dtype=bool), k=1)
        att = jnp.where(causal[None, None, :, :], jnp.float32(-1000000000.0), att)
        att = jax.nn.softmax(att, axis=-1)
        out = jnp.einsum('bhqk,bhkd->bhqd', att, v)
        out = jnp.transpose(out, (0, 2, 1, 3)).reshape(b, s, d)
        return jnp.einsum('bsd,od->bso', out, w_out)

    def _L0_ffn_ref(hidden_states, router_w, router_b, expert_w, expert_b):
        import jax, jax.numpy as jnp
        import numpy as np
        TOP_K = 2
        B, S, H = hidden_states.shape
        E, O, _ = expert_w.shape
        T = B * S
        h = hidden_states.reshape(T, H)
        logits = (h @ router_w.T + router_b).reshape(T, O, E)
        probs = jax.nn.softmax(logits.astype(jnp.float32), axis=-1)
        w, sel = jax.lax.top_k(probs, TOP_K)
        w = w / jnp.sum(w, axis=-1, keepdims=True)
        w = w.astype(h.dtype)
        t_idx = jnp.arange(T)[:, None, None]
        c = jnp.zeros((T, E), dtype=h.dtype).at[t_idx, sel].add(w)
        expert_out = jnp.einsum('th,eoh->teo', h, expert_w) + expert_b[None, :, :]
        final = jnp.einsum('te,teo->to', c, expert_out)
        return final.reshape(B, S, O)

    def _L1_attn_ref(x, w_qkv, w_proj):
        import jax, jax.numpy as jnp
        import numpy as np
        NUM_HEADS = 16
        NUM_KV_HEADS = 4
        HEAD_DIM = 128
        HIDDEN = 256
        SEQ = 256
        BATCH = 2
        Q_PER_GROUP = NUM_HEADS // NUM_KV_HEADS
        GROUP_SIZE = (Q_PER_GROUP + 2) * HEAD_DIM
        TOTAL_PROJ = NUM_KV_HEADS * GROUP_SIZE
        s, b, _ = x.shape
        qkv = jnp.einsum('sbh,ph->sbp', x, w_qkv)
        qkv = qkv.reshape(s, b, NUM_KV_HEADS, GROUP_SIZE)
        q = qkv[..., :Q_PER_GROUP * HEAD_DIM].reshape(s, b, NUM_HEADS, HEAD_DIM)
        k = qkv[..., Q_PER_GROUP * HEAD_DIM:(Q_PER_GROUP + 1) * HEAD_DIM]
        v = qkv[..., (Q_PER_GROUP + 1) * HEAD_DIM:]
        q = q.transpose(1, 2, 0, 3)
        k = jnp.repeat(k.transpose(1, 2, 0, 3), Q_PER_GROUP, axis=1)
        v = jnp.repeat(v.transpose(1, 2, 0, 3), Q_PER_GROUP, axis=1)
        scale = 1.0 / jnp.sqrt(jnp.asarray(HEAD_DIM, dtype=x.dtype))
        scores = jnp.einsum('bhsd,bhtd->bhst', q, k) * scale
        attn = jax.nn.softmax(scores, axis=-1)
        out = jnp.einsum('bhst,bhtd->bhsd', attn, v)
        out = out.transpose(2, 0, 1, 3).reshape(s, b, NUM_HEADS * HEAD_DIM)
        return jnp.einsum('sbe,he->sbh', out, w_proj)

    def _L1_ffn_ref(x, gate_W_packed, gate_scales, up_W_packed, up_scales, down_W_packed, down_scales):
        import jax, jax.numpy as jnp
        import numpy as np
        BLOCK_SIZE = 32
        HIDDEN_SIZE = 256
        MLP_DIM = 2048
        NVFP4_LUT = jnp.array([0.0, 0.5, 1.0, 1.5, 2.0, 3.0, 4.0, 6.0, 0.0, -0.5, -1.0, -1.5, -2.0, -3.0, -4.0, -6.0], dtype=jnp.float32)

        def dequant_nvfp4(W_packed, scales, block=BLOCK_SIZE):
            N = W_packed.shape[0]
            low = W_packed & 15
            high = W_packed >> 4 & 15
            idx = jnp.stack([low, high], axis=-1).reshape(N, -1)
            vals = NVFP4_LUT[idx]
            K = vals.shape[1]
            vals = vals.reshape(N, K // block, block) * scales[:, :, None]
            return vals.reshape(N, K)
        B, S, H = x.shape
        xt = x.reshape(B * S, H)
        Wg = dequant_nvfp4(gate_W_packed, gate_scales)
        Wu = dequant_nvfp4(up_W_packed, up_scales)
        Wd = dequant_nvfp4(down_W_packed, down_scales)
        gate = jnp.einsum('th,nh->tn', xt, Wg)
        up = jnp.einsum('th,nh->tn', xt, Wu)
        gelu = jnp.tanh(0.7978845608028654 * (gate + 0.044715 * gate ** 3)) * gate * 0.5 + gate * 0.5
        inter = gelu * up
        out = jnp.einsum('tn,hn->th', inter, Wd)
        return out.reshape(B, S, H)
    x = L0_attn_x
    x = x + _L0_attn_ref(_layernorm(x, axis=-1), L0_attn_w_project, L0_attn_w_out)
    x = x + _L0_ffn_ref(_layernorm(x, axis=-1), L0_ffn_router_w, L0_ffn_router_b, L0_ffn_expert_w, L0_ffn_expert_b)
    x = x + _L1_attn_ref(_layernorm(x, axis=-1), L1_attn_w_qkv, L1_attn_w_proj)
    x = x + _L1_ffn_ref(_layernorm(x, axis=-1), L1_ffn_gate_W_packed, L1_ffn_gate_scales, L1_ffn_up_W_packed, L1_ffn_up_scales, L1_ffn_down_W_packed, L1_ffn_down_scales)
    return x

_drawn_inputs = setup_inputs


def setup_inputs(seed=0):
    import zlib

    import numpy as np

    out = dict(_drawn_inputs(seed))
    spreads = {'L0_ffn_router_b': (0.0, 0.1), 'L0_ffn_expert_b': (0.0, 0.1)}
    factors = {'L1_attn_w_qkv': 8.0, 'L1_attn_w_proj': 8.0}
    for name, (base, spread) in spreads.items():
        noise = np.random.default_rng([zlib.crc32(name.encode()), seed]).standard_normal(out[name].shape)
        drawn = base * np.exp(spread * noise) if base else spread * noise
        out[name] = jnp.asarray(drawn.astype(out[name].dtype))
    for name, factor in factors.items():
        out[name] = (out[name] * factor).astype(out[name].dtype)
    return out
```

```python
from contextlib import ExitStack
from itertools import islice

import numpy as np

import concourse.bass as bass
from concourse import mybir

F32 = mybir.dt.float32
F32R = mybir.dt.float32r
BF16 = mybir.dt.bfloat16
I32 = mybir.dt.int32
ALU = mybir.AluOpType
ACT = mybir.ActivationFunctionType
AX_X = mybir.AxisListType.X

P = 128
B = 4
S = 512
D = 256
KC = D // P
G = S // P
BANK = 512
EPS = 1e-5


class Store:

    def __init__(self, nc, stack):
        self.nc, self.stack = nc, stack

    def sb(self, name, shape, dt):
        return self.stack.enter_context(self.nc.sbuf_tensor(name, shape, dt))

    def sem(self, name):
        return self.stack.enter_context(self.nc.semaphore(name))


def reach(eng, sem, value):
    if not (isinstance(value, int) and value <= 0):
        eng.wait_ge(sem, value)


def wait_alone(eng, sem, value, passed):
    eng.wait_ge(sem, value)
    eng.sem_inc(passed, 1)

H0 = 16
HD0 = D // H0
HG = 4
NG = H0 // HG
HB = 32
STK = 4 * HD0
SHIFT = STK
NEG = -3.0e38


def max_units(pair):
    a, b = 2 * pair, 2 * pair + 1
    return [
        [(a, 3, k) for k in range(4)],
        [(b, 3, k) for k in range(4)],
        [(a, 2, k) for k in range(3)] + [(a, 0, 0)],
        [(b, 2, k) for k in range(3)] + [(b, 0, 0)],
        [(a, 1, 0), (a, 1, 1), (b, 1, 0), (b, 1, 1)],
    ]


def layer0_attention(nc, glob, A):
    X, ps, ident, identb = glob["X"], glob["ps"], glob["ident"], glob["identb"]
    passed_dve, passed_pool, passed_sp = glob["passed"]
    scratch_q, scratch_k = glob["scratch_q"], glob["scratch_k"]
    with ExitStack() as stack:
        st = Store(nc, stack)
        w_f = st.sb("w0_f", [P, KC, 3 * D], F32)
        w_hi = st.sb("w0_hi", [P, KC, 3 * D], BF16)
        w_lo = st.sb("w0_lo", [P, KC, 3 * D], BF16)
        wo = st.sb("wo0", [P, NG, D], F32)
        maskneg = st.sb("maskneg", [P, P], BF16)
        sel = st.sb("sel0", [P, P], F32)
        stats = st.sb("stats0", [P, G, 6], F32)
        mv = st.sb("mv0", [P, G, 2], F32)
        rstd = st.sb("rstd0", [P, G], F32)
        half = st.sb("half0", [P, G], F32)
        xn = st.sb("xn0", [P, G, D], F32)
        xT_hi = st.sb("xT0_hi", [P, KC, S], BF16)
        xT_lo = st.sb("xT0_lo", [P, KC, S], BF16)
        qk_hi = st.sb("qk_hi", [P, 4, S], BF16)
        qk_lo = st.sb("qk_lo", [P, 4, S], BF16)
        qs = st.sb("qs", [STK + 2, H0, S], BF16)
        ks = st.sb("ks", [STK + 2, H0, S], BF16)
        v = st.sb("v0", [P, G, H0, HB], F32)
        bm = st.sb("bm", [P, H0 // 2, 20], F32)
        mx = st.sb("mx", [P, H0, G], F32)
        mt_f = st.sb("mt_f", [HG * G, P], F32)
        mt_hi = st.sb("mt_hi", [HG * G, P], BF16)
        mt_lo = st.sb("mt_lo", [HG * G, P], BF16)
        pt = [st.sb(f"pt{k}", [P, HG, S - P * k], F32) for k in range(G)]
        o_raw = st.sb("o_raw", [P, S], F32)
        rec = st.sb("rec0", [P, S], F32)
        oT = st.sb("oT", [P, NG, S], F32)

        load, load_wo = st.sem("load0"), st.sem("load0_wo")
        const = st.sem("const0")
        wsplit_hi, wsplit_lo = st.sem("wsplit0_hi"), st.sem("wsplit0_lo")
        s_stat, s_mv, s_rstd = st.sem("stat0"), st.sem("mv0s"), st.sem("rstd0s")
        s_xn, s_tp, s_xhi, s_xlo = st.sem("xn0s"), st.sem("tp0"), st.sem("xhi0"), st.sem("xlo0")
        s_qk, s_qkhi, s_qklo = st.sem("qk"), st.sem("qkhi"), st.sem("qklo")
        s_scr, s_stk = st.sem("scr"), st.sem("stk")
        s_v, s_vev = st.sem("v0s"), st.sem("vev0")
        s_mu, s_bm, s_mx = st.sem("max_unit"), st.sem("block_max"), st.sem("row_max")
        s_mt, s_mthi, s_mtlo, s_shift = st.sem("mt"), st.sem("mthi"), st.sem("mtlo"), st.sem("shift")
        s_st, s_exp, s_msk, s_pv = st.sem("scoreT"), st.sem("expd"), st.sem("masked"), st.sem("pv0")
        s_raw, s_den, s_rec, s_oT = st.sem("raw0"), st.sem("den0"), st.sem("rec0s"), st.sem("oT0")
        s_out, s_res = st.sem("out0"), st.sem("res0")


        MAXB, STB, PVB, SELB = (0, 1), (2, 4), 6, 7

        def bank(n, width=BANK, off=0):
            return ps[:, n * BANK + off:n * BANK + off + width]

        ST_UNITS = [(0, (0, 1)), (0, (2, 3)), (1, (0, 1)), (1, (2, 3)), (2, (0, 1, 2, 3)), (3, (0, 1, 2, 3))]

        def st_col(u, n):
            kt, heads = ST_UNITS[u]
            width = S - P * kt
            per = BANK // width
            return STB[u % 2] * BANK + (n // per) * BANK + (n % per) * width, width

        with nc.Block() as block:

            @block.sync
            def _(sp):
                sp.dma_start(w_f[:, :, :], A["w_project"].rearrange("(c p) n -> p c n", p=P)).then_inc(load, 16)
                sp.wait_ge(const, 3)
                for h in range(HG):
                    sp.dma_start(wo[HB * h:HB * h + HD0, :, :],
                                 A["w_out"].rearrange("(g i d) n -> i d g n", i=HG, d=HD0)[h]).then_inc(load_wo, 16)
                with sp.Fori(0, B) as b:
                    for n, (hi_rows, lo_rows) in enumerate((((0, 2), (1, 3)), ((0, 1), (2, 3)))):
                        scr = scratch_q if n == 0 else scratch_k
                        dst = qs if n == 0 else ks
                        for part, (buf, done) in enumerate(((qk_hi, s_qkhi), (qk_lo, s_qklo))):
                            sp.wait_ge(done, 4 * b + 2 * n + 2)
                            sp.dma_start(scr[part].rearrange("(m p) t -> p m t", p=P),
                                         buf[:, 2 * n:2 * n + 2, :]).then_inc(s_scr, 16)
                    wait_alone(sp, s_scr, 64 * b + 64, passed_sp)
                    reach(sp, s_st, 6 * NG * b)
                    for n, (hi_rows, lo_rows) in enumerate((((0, 2), (1, 3)), ((0, 1), (2, 3)))):
                        scr = scratch_q if n == 0 else scratch_k
                        dst = qs if n == 0 else ks
                        for part, rows in enumerate((hi_rows, lo_rows)):
                            for r in rows:
                                sp.dma_start(dst[HD0 * r:HD0 * (r + 1), :, :],
                                             scr[part].rearrange("(h d) t -> d h t", d=HD0)).then_inc(s_stk, 16)
                    for g in range(NG):
                        for part, (buf, done) in enumerate(((mt_hi, s_mthi), (mt_lo, s_mtlo))):
                            sp.wait_ge(done, NG * b + g + 1)
                            sp.dma_start(
                                qs[SHIFT + part:SHIFT + part + 1, HG * g:HG * (g + 1), :].rearrange(
                                    "o h (j q) -> o (h j) q", q=P),
                                buf[:, :]).then_inc(s_shift, 16)
                    wait_alone(sp, s_stk, 128 * b + 128, passed_sp)

            @block.gpsimd
            def _(pool):
                pool.memset(half[:, :], -0.5).then_inc(const, 1)
                pool.memset(maskneg[:, :], 0.0).then_inc(const, 1)
                pool.memset(wo[:, :, :], 0.0).then_inc(const, 1)
                pool.memset(v[:, :, :, :], 0.0).then_inc(const, 1)
                pool.memset(sel[:, :], 0.0).then_inc(const, 1)
                pool.wait_ge(const, 5)
                pool.memset(ks[STK:STK + 2, :, :], 1.0).then_inc(const, 1)
                pool.wait_ge(const, 6)
                pool.affine_select(out=maskneg[:, :], in_=maskneg[:, :], compare_op=ALU.is_ge, fill=NEG, base=0,
                                   pattern=[[-1, P]], channel_multiplier=1).then_inc(const, 1)
                pool.memset(v[:, :, :, HD0:HD0 + 1], 1.0).then_inc(const, 1)
                pool.affine_select(out=sel[:, :].rearrange("p (h r) -> p h r", r=HB),
                                   in_=sel[:, :].rearrange("p (h r) -> p h r", r=HB),
                                   compare_op=ALU.not_equal, fill=1.0, base=-HD0,
                                   pattern=[[-HB, HG], [0, HB]], channel_multiplier=1).then_inc(const, 1)
                with pool.Fori(0, B) as b:
                    wait_alone(pool, s_mv, G * b + G, passed_pool)
                    pool.tensor_scalar(rstd[:, :], mv[:, :, 1], EPS, None, ALU.add).then_inc(s_rstd, 1)
                    wait_alone(pool, s_rstd, 2 * b + 1, passed_pool)
                    pool.tensor_tensor(rstd[:, :], rstd[:, :], half[:, :], ALU.pow).then_inc(s_rstd, 1)
                    for g in range(NG):
                        for u, (kt, heads) in enumerate(ST_UNITS):
                            wait_alone(pool, s_exp, 6 * (NG * b + g) + u + 1, passed_pool)
                            t = pt[kt][:, heads[0]:heads[-1] + 1, 0:P]
                            pool.affine_select(out=t, in_=t, compare_op=ALU.is_ge, fill=0.0, base=0,
                                               pattern=[[0, len(heads)], [1, P]],
                                               channel_multiplier=-1).then_inc(s_msk, 1)

            @block.tensor
            def _(pe):
                pe.wait_ge(wsplit_hi, 1)
                pe.wait_ge(wsplit_lo, 1)
                pe.wait_ge(const, 9)
                pe.wait_ge(load_wo, 16 * HG)

                def three(out, lhs, rhs, last):
                    n = 0
                    for c in range(KC):
                        for a, b_ in ((0, 0), (0, 1), (1, 0)):
                            mm = pe.matmul(out, lhs[a](c), rhs[b_](c), start=(n == 0), stop=(n == 3 * KC - 1))
                            n += 1
                    if last is not None:
                        mm.then_inc(last, 1)

                def max_unit(b, pair, u):
                    n = 5 * pair + u
                    blocks = max_units(pair)[u]
                    o = MAXB[n % 2] * BANK
                    if n >= 2:
                        pe.wait_ge(s_bm, 40 * b + n - 1)
                    else:
                        reach(pe, s_bm, 40 * b)
                    i = 0
                    while i < 4:
                        h, j, k0 = blocks[i]
                        w = 1
                        while i + w < 4 and blocks[i + w][:2] == (h, j):
                            w += 1
                        out = ps[:, o + P * i:o + P * (i + w)]
                        pe.matmul(out, qs[0:STK, h, P * j:P * (j + 1)], ks[0:STK, h, P * k0:P * (k0 + w)],
                                  start=(i == 0), stop=False, skip_group_check=True)
                        i += w
                        mm = pe.matmul(ps[:, o + P * (i - 1):o + P * i], identb[:, :], maskneg[:, :],
                                       start=False, stop=(i == 4), skip_group_check=True)
                    mm.then_inc(s_mu, 1)

                def turn_max(b, g):
                    pe.wait_ge(s_mx, NG * b + g + 1)
                    reach(pe, s_rec, NG * b + g - 1 if g else NG * b)
                    pe.transpose(ps[0:HG * G, SELB * BANK:SELB * BANK + P],
                                 mx[:, HG * g:HG * (g + 1), :].rearrange("p h j -> p (h j)"), ident[:, :]).then_inc(s_mt, 1)

                def score_unit(b, g, u):
                    kt, heads = ST_UNITS[u]
                    n = 6 * (NG * b + g) + u
                    if u == 0:
                        pe.wait_ge(s_shift, 32 * (NG * b + g) + 32)
                    if g or u >= 2:
                        pe.wait_ge(s_exp, n - 1)
                    else:
                        reach(pe, s_exp, 6 * NG * b)
                    for i, h in enumerate(heads):
                        c, w = st_col(u, i)
                        h += HG * g
                        mm = pe.matmul(ps[:, c:c + w], ks[:, h, P * kt:P * (kt + 1)], qs[:, h, P * kt:],
                                       start=True, stop=True, skip_group_check=True)
                    mm.then_inc(s_st, 1)

                def values(b, g, kt):
                    n = NG * b + g
                    pe.wait_ge(s_msk, 6 * n + (2, 4, 5, 6)[kt])
                    if kt == 0:
                        reach(pe, s_raw, n)
                    for h in range(HG):
                        mm = pe.matmul(ps[HB * h:HB * (h + 1), PVB * BANK + P * kt:(PVB + 1) * BANK],
                                       v[:, kt, HG * g + h, :], pt[kt][:, h, :],
                                       start=(kt == 0), stop=(kt == G - 1), skip_group_check=True)
                    mm.then_inc(s_pv, 1)

                def denominators(b, g):
                    n = NG * b + g
                    pe.wait_ge(s_raw, n + 1)
                    nxt = min(g + 2, NG) + NG * b
                    pe.wait_ge(s_mtlo, nxt)
                    reach(pe, s_rec, n)
                    pe.matmul(bank(SELB), sel[:, :], o_raw[:, :], start=True, stop=True).then_inc(s_den, 1)

                with pe.Fori(0, B) as b:
                    pe.wait_ge(s_xn, G * b + G)
                    reach(pe, s_bm, 40 * b)
                    for c in range(KC):
                        for g in range(G):
                            tr = pe.transpose(bank(c, P, P * g), xn[:, g, P * c:P * (c + 1)], ident[:, :])
                        tr.then_inc(s_tp, 1)
                    pe.wait_ge(s_xhi, 2 * b + 2)
                    pe.wait_ge(s_xlo, 2 * b + 2)
                    reach(pe, s_exp, 6 * NG * b)
                    for m in range(4):
                        three(bank(2 + m),
                              [lambda c, m=m: w_hi[:, c, P * m:P * (m + 1)], lambda c, m=m: w_lo[:, c, P * m:P * (m + 1)]],
                              [lambda c: xT_hi[:, c, :], lambda c: xT_lo[:, c, :]], s_qk)
                    reach(pe, s_raw, NG * b)
                    reach(pe, s_res, 2 * b)
                    for t in range(G):
                        three(bank(PVB + t // 2, D, D * (t % 2)),
                              [lambda c, t=t: xT_hi[:, c, P * t:P * (t + 1)], lambda c, t=t: xT_lo[:, c, P * t:P * (t + 1)]],
                              [lambda c: w_hi[:, c, 2 * D:], lambda c: w_lo[:, c, 2 * D:]],
                              s_v if t % 2 else None)
                    pe.wait_ge(s_stk, 128 * b + 128)
                    pe.wait_ge(s_vev, 2 * b + 2)
                    for n in range(10):
                        max_unit(b, n // 5, n % 5)
                    turn_max(b, 0)
                    for n in range(10, 20):
                        max_unit(b, n // 5, n % 5)
                    for g in range(NG):
                        todo = iter(range(10 * (g + 2), min(10 * (g + 3), 40)))

                        def some(k):
                            for n in islice(todo, k):
                                max_unit(b, n // 5, n % 5)
                        if g + 1 < NG:
                            turn_max(b, g + 1)
                        score_unit(b, g, 0)
                        some(1)
                        score_unit(b, g, 1)
                        some(2)
                        score_unit(b, g, 2)
                        some(1)
                        score_unit(b, g, 3)
                        values(b, g, 0)
                        some(2)
                        score_unit(b, g, 4)
                        some(1)
                        values(b, g, 1)
                        score_unit(b, g, 5)
                        some(2)
                        values(b, g, 2)
                        some(9)
                        values(b, g, 3)
                        denominators(b, g)
                    pe.wait_ge(s_oT, NG * b + NG)
                    for t in range(G):
                        for g in range(NG):
                            mm = pe.matmul(bank(PVB + t // 2, D, D * (t % 2)), oT[:, g, P * t:P * (t + 1)], wo[:, g, :],
                                           start=(g == 0), stop=(g == NG - 1))
                        if t % 2:
                            mm.then_inc(s_out, 1)

            @block.scalar
            def _(act):
                act.wait_ge(load, 16)
                act.activation(w_hi[:, :, :], w_f[:, :, :], ACT.Copy).then_inc(wsplit_hi, 1)
                act.wait_ge(const, 9)
                with act.Fori(0, B) as b:
                    for c in range(KC):
                        act.wait_ge(s_tp, 2 * b + c + 1)
                        act.activation(xT_hi[:, c, :], bank(c), ACT.Copy).then_inc(s_xhi, 1)
                    reach(act, s_scr, 64 * b)
                    for m in range(4):
                        act.wait_ge(s_qk, 4 * b + m + 1)
                        act.activation(qk_hi[:, m, :], bank(2 + m), ACT.Copy,
                                       scale=(HD0 ** -0.5 if m < 2 else 1.0)).then_inc(s_qkhi, 1)
                    for t in range(G // 2):
                        act.wait_ge(s_v, 2 * b + t + 1)
                        act.activation(v[:, 2 * t:2 * t + 2, :, 0:HD0],
                                       bank(PVB + t).rearrange("p (t h d) -> p t h d", t=2, d=HD0),
                                       ACT.Copy).then_inc(s_vev, 1)
                    for g in range(NG):
                        for u, (kt, heads) in enumerate(ST_UNITS):
                            act.wait_ge(s_st, 6 * (NG * b + g) + u + 1)
                            reach(act, s_pv, G * (NG * b + g - 1) + kt + 1 if g else G * NG * b)
                            c, w = st_col(u, 0)
                            per = BANK // w
                            src = ps[:, c:c + len(heads) // per * BANK].rearrange(
                                "p (h q) -> p h q", h=len(heads))[:, :, 0:w]
                            act.activation(pt[kt][:, heads[0]:heads[-1] + 1, :], src, ACT.Exp).then_inc(s_exp, 1)
                        act.wait_ge(s_pv, G * (NG * b + g) + G)
                        reach(act, s_oT, NG * b + g)
                        act.activation(o_raw[:, :], bank(PVB), ACT.Copy).then_inc(s_raw, 1)

            @block.vector
            def _(dve):
                dve.wait_ge(load, 16)
                dve.wait_ge(wsplit_hi, 1)
                dve.tensor_tensor(w_lo[:, :, :], w_f[:, :, :], w_hi[:, :, :], ALU.subtract).then_inc(wsplit_lo, 1)

                def take_max(b, n):
                    pair, u = n // 5, n % 5
                    dve.wait_ge(s_mu, 40 * b + n + 1)
                    dve.tensor_reduce(bm[:, pair, 4 * u:4 * u + 4],
                                      bank(MAXB[n % 2]).rearrange("p (k q) -> p k q", k=4), AX_X,
                                      ALU.max).then_inc(s_bm, 1)

                def row_max(b, g):
                    pr = slice(2 * g, 2 * g + 2)
                    dve.wait_ge(s_bm, 40 * b + 10 * g + 10)
                    m4 = mx[:, HG * g:HG * (g + 1), :].rearrange("p (r h) j -> p r h j", h=2)
                    dve.tensor_reduce(m4[:, :, :, 3], bm[:, pr, 0:8].rearrange("p r (h k) -> p r h k", h=2), AX_X, ALU.max)
                    dve.tensor_reduce(m4[:, :, :, 2], bm[:, pr, 8:16].rearrange("p r (h k) -> p r h k", h=2)[:, :, :, 0:3],
                                      AX_X, ALU.max)
                    dve.tensor_reduce(m4[:, :, :, 1], bm[:, pr, 16:20].rearrange("p r (h k) -> p r h k", h=2), AX_X, ALU.max)
                    dve.tensor_copy(m4[:, :, :, 0], bm[:, pr, 8:16].rearrange("p r (h k) -> p r h k", h=2)[:, :, :, 3])\
                       .then_inc(s_mx, 1)

                def shift_rows(b, g):
                    n = NG * b + g
                    mt_ps = ps[0:HG * G, SELB * BANK:SELB * BANK + P]
                    dve.wait_ge(s_mt, n + 1)
                    reach(dve, s_shift, 32 * n)
                    dve.tensor_scalar(mt_hi[:, :], mt_ps, -1.0, None, ALU.mult).then_inc(s_mthi, 1)
                    dve.wait_ge(s_mthi, n + 1)
                    dve.scalar_tensor_tensor(mt_lo[:, :], mt_ps, -1.0, mt_hi[:, :], ALU.mult, ALU.subtract)\
                       .then_inc(s_mtlo, 1)

                def normalise(b, g):
                    n = NG * b + g
                    dve.wait_ge(s_den, n + 1)
                    dve.reciprocal(rec[:, :], bank(SELB)).then_inc(s_rec, 1)
                    dve.wait_ge(s_rec, n + 1)
                    reach(dve, s_out, 2 * b)
                    dve.tensor_tensor(oT[:, g, :], o_raw[:, :], rec[:, :], ALU.mult).then_inc(s_oT, 1)

                with dve.Fori(0, B) as b:
                    for g in range(G):
                        dve.bn_stats(stats[:, g, :], X[:, b, g, :]).then_inc(s_stat, 1)
                    for g in range(G):
                        wait_alone(dve, s_stat, G * b + g + 1, passed_dve)
                        dve.bn_aggr(mv[:, g, :], stats[:, g, :]).then_inc(s_mv, 1)
                    dve.wait_ge(s_rstd, 2 * b + 2)
                    for g in range(G):
                        dve.tensor_scalar(xn[:, g, :], X[:, b, g, :], mv[:, g, 0:1], rstd[:, g:g + 1],
                                          ALU.subtract, ALU.mult).then_inc(s_xn, 1)
                    for c in range(KC):
                        dve.wait_ge(s_xhi, 2 * b + c + 1)
                        dve.tensor_tensor(xT_lo[:, c, :], bank(c), xT_hi[:, c, :], ALU.subtract).then_inc(s_xlo, 1)
                    reach(dve, s_scr, 64 * b)
                    for m in range(4):
                        dve.wait_ge(s_qkhi, 4 * b + m + 1)
                        dve.scalar_tensor_tensor(qk_lo[:, m, :], bank(2 + m), (HD0 ** -0.5 if m < 2 else 1.0),
                                                 qk_hi[:, m, :], ALU.mult, ALU.subtract).then_inc(s_qklo, 1)
                    for n in range(10):
                        take_max(b, n)
                    row_max(b, 0)
                    shift_rows(b, 0)
                    for n in range(10, 20):
                        take_max(b, n)
                    row_max(b, 1)
                    for g in range(NG):
                        if g + 1 < NG:
                            shift_rows(b, g + 1)
                        for n in range(10 * (g + 2), min(10 * (g + 3), 40)):
                            take_max(b, n)
                        if g + 2 < NG:
                            row_max(b, g + 2)
                        normalise(b, g)
                    for t in range(G // 2):
                        dve.wait_ge(s_out, 2 * b + t + 1)
                        xr = X[:, b, 2 * t:2 * t + 2, :]
                        dve.tensor_tensor(xr, bank(PVB + t).rearrange("p (t n) -> p t n", t=2), xr,
                                          ALU.add).then_inc(s_res, 1)


E = 8
EO = E * D
NU = EO // BANK
CAP = 60.0


def normalise_ops(b_of, dve, X, stats, mv, rstd, xn, s_stat, s_mv, s_rstd, s_xn, i, passed):
    for j in range(4):
        dve.bn_stats(stats[:, j, :], b_of(j)).then_inc(s_stat, 1)
    for j in range(4):
        wait_alone(dve, s_stat, 4 * i + j + 1, passed)
        dve.bn_aggr(mv[:, j, :], stats[:, j, :]).then_inc(s_mv, 1)
    dve.wait_ge(s_rstd, 2 * i + 2)
    for j in range(4):
        dve.tensor_scalar(xn[:, j, :], b_of(j), mv[:, j, 0:1], rstd[:, j:j + 1],
                          ALU.subtract, ALU.mult).then_inc(s_xn, 1)


def rstd_ops(pool, mv, rstd, half, s_mv, s_rstd, i, passed):
    wait_alone(pool, s_mv, 4 * i + 4, passed)
    pool.tensor_scalar(rstd[:, :], mv[:, :, 1], EPS, None, ALU.add).then_inc(s_rstd, 1)
    wait_alone(pool, s_rstd, 2 * i + 1, passed)
    pool.tensor_tensor(rstd[:, :], rstd[:, :], half[:, :], ALU.pow).then_inc(s_rstd, 1)


def layer0_mixture(nc, glob, A):
    X, ps, ident = glob["X"], glob["ps"], glob["ident"]
    passed_dve, passed_pool, passed_sp = glob["passed"]
    with ExitStack() as stack:
        st = Store(nc, stack)
        w_in = [st.sb(f"w_in{n}", [P, EO], F32) for n in range(2)]
        rw_hi = st.sb("rw_hi", [P, KC, EO], F32R)
        rw_lo = st.sb("rw_lo", [P, KC, EO], F32R)
        ew_hi = st.sb("ew_hi", [P, KC, EO], BF16)
        ew_lo = st.sb("ew_lo", [P, KC, EO], BF16)
        b_f = st.sb("b_f", [1, 2, EO], F32)
        b_part = st.sb("b_part", [1, 3, 2, EO], BF16)
        b3 = st.sb("b3", [3, 2, EO], BF16)
        ones3 = st.sb("ones3", [3, P], BF16)
        code = st.sb("code", [P, E], I32)
        stats = st.sb("stats1", [P, 4, 6], F32)
        mv = st.sb("mv1", [P, 4, 2], F32)
        rstd = st.sb("rstd1", [P, 4], F32)
        half = st.sb("half1", [P, 4], F32)
        xn = st.sb("xn1", [P, 4, D], F32)
        xr_hi = st.sb("xr_hi", [P, KC, S], F32R)
        xr_lo = st.sb("xr_lo", [P, KC, S], F32R)
        xb_hi = st.sb("xb_hi", [P, KC, S], BF16)
        xb_lo = st.sb("xb_lo", [P, KC, S], BF16)
        lg = [st.sb(f"lg{n}", [P, E, D], F32) for n in range(2)]
        tmp = st.sb("tmp", [P, E, D], F32)
        s4, h4 = st.sb("s4", [P, 4, D], F32), st.sb("h4", [P, 4, D], F32)
        h2, a2, c2 = (st.sb(n, [P, 2, D], F32) for n in ("h2", "a2", "c2"))
        m1, m2, n1, c1 = (st.sb(n, [P, D], F32) for n in ("m1", "m2", "n1", "c1"))
        e1 = st.sb("e1", [P, D], F32)
        cw = [st.sb(f"cw{n}", [P, E], F32) for n in range(2)]

        load_r, load_e, load_b, load_b3 = (st.sem(n) for n in ("load_r", "load_e", "load_b", "load_b3"))
        const, s_whi, s_wlo, s_b = st.sem("const1"), st.sem("w1hi"), st.sem("w1lo"), st.sem("bparts")
        s_stat, s_mv, s_rstd = st.sem("stat1"), st.sem("mv1s"), st.sem("rstd1s")
        s_xn, s_tp, s_xhi, s_xlo = st.sem("xn1s"), st.sem("tp1"), st.sem("xhi1"), st.sem("xlo1")
        s_rt, s_lg, s_dve, s_z, s_ez = st.sem("router"), st.sem("logits"), st.sem("topk"), st.sem("zdist"), st.sem("zexp")
        s_c, s_u = st.sem("cweights"), st.sem("experts")

        def bank(n, width=BANK, off=0):
            return ps[:, n * BANK + off:n * BANK + off + width]

        def over_experts(a):
            return a[:, :].rearrange("p (o n) -> p o n", o=1).to_broadcast([P, E, D])

        TOP, DIST, WEIGHED, DONE = 13, 15, 18, 26

        with nc.Block() as block:

            @block.sync
            def _(sp):
                for c in range(KC):
                    sp.dma_start(w_in[c][:, :], A["router_w"][P * c:P * (c + 1), :]).then_inc(load_r, 16)
                sp.dma_start(b_f[:, 0, :], A["router_b"]).then_inc(load_b, 16)
                sp.dma_start(b_f[:, 1, :], A["expert_b"]).then_inc(load_b, 16)
                sp.wait_ge(s_whi, 2)
                sp.wait_ge(s_wlo, 2)
                for c in range(KC):
                    sp.dma_start(w_in[c][:, :], A["expert_w"][P * c:P * (c + 1), :]).then_inc(load_e, 16)
                sp.wait_ge(s_b, 5)
                for part in range(3):
                    sp.dma_start(b3[part:part + 1, :, :], b_part[:, part, :, :]).then_inc(load_b3, 16)
                sp.wait_ge(load_b3, 48)

            @block.gpsimd
            def _(pool):
                pool.memset(half[:, :], -0.5).then_inc(const, 1)
                pool.memset(ones3[:, :], 1.0).then_inc(const, 1)
                pool.iota(code[:, :], pattern=[[-1, E]], base=E - 1, channel_multiplier=0).then_inc(const, 1)
                with pool.Fori(0, B) as b:
                    rstd_ops(pool, mv, rstd, half, s_mv, s_rstd, b, passed_pool)

            @block.tensor
            def _(pe):
                pe.wait_ge(s_wlo, 4)
                pe.wait_ge(s_whi, 4)
                pe.wait_ge(load_b3, 48)
                pe.wait_ge(const, 3)

                def products(out, x_hi, x_lo, w_hi, w_lo, t, cols, bias):
                    pe.matmul(out, ones3[:, :], bias, start=True, stop=False)
                    tok = slice(P * t, P * (t + 1))
                    for c in range(KC):
                        pe.matmul(out, x_hi[:, c, tok], w_hi[:, c, cols], start=False, stop=False)
                        pe.matmul(out, x_hi[:, c, tok], w_lo[:, c, cols], start=False, stop=False)
                        mm = pe.matmul(out, x_lo[:, c, tok], w_hi[:, c, cols], start=False, stop=(c == KC - 1))
                    return mm

                def router(b, t):
                    for u in range(NU):
                        reach(pe, s_lg, NU * (4 * b + t - 1) + u + 1 if t else NU * 4 * b)
                        cols = slice(BANK * u, BANK * (u + 1))
                        products(bank(u), xr_hi, xr_lo, rw_hi, rw_lo, t, cols, b3[:, 0, cols]).then_inc(s_rt, 1)

                def experts(b, t):
                    for u in range(NU):
                        reach(pe, s_c, E * (4 * b + t - 1) + 2 * (u + 1) if t else E * 4 * b)
                        cols = slice(BANK * u, BANK * (u + 1))
                        products(bank(4 + u), xb_hi, xb_lo, ew_hi, ew_lo, t, cols, b3[:, 1, cols]).then_inc(s_u, 1)

                with pe.Fori(0, B) as b:
                    pe.wait_ge(s_xn, 4 * b + 4)
                    reach(pe, s_lg, NU * 4 * b)
                    for c in range(KC):
                        for t in range(4):
                            tr = pe.transpose(bank(c, P, P * t), xn[:, t, P * c:P * (c + 1)], ident[:, :])
                        tr.then_inc(s_tp, 1)
                    pe.wait_ge(s_xhi, 4 * b + 4)
                    pe.wait_ge(s_xlo, 4 * b + 4)
                    for t in range(4):
                        router(b, t)
                        experts(b, t)

            @block.scalar
            def _(act):
                act.wait_ge(load_r, 32)
                for c in range(KC):
                    act.activation(rw_hi[:, c, :], w_in[c][:, :], ACT.Copy).then_inc(s_whi, 1)
                act.wait_ge(load_e, 32)
                for c in range(KC):
                    act.activation(ew_hi[:, c, :], w_in[c][:, :], ACT.Copy).then_inc(s_whi, 1)
                with act.Fori(0, B) as b:
                    for c in range(KC):
                        act.wait_ge(s_tp, 2 * b + c + 1)
                        act.activation(xr_hi[:, c, :], bank(c), ACT.Copy).then_inc(s_xhi, 1)
                        act.activation(xb_hi[:, c, :], bank(c), ACT.Copy).then_inc(s_xhi, 1)
                    for t in range(4):
                        n = 4 * b + t
                        for u in range(NU):
                            act.wait_ge(s_rt, NU * n + u + 1)
                            if u == 0:
                                reach(act, s_dve, DONE * (n - 1) if t else DONE * 4 * b)
                            act.activation(lg[t % 2][:, 2 * u:2 * u + 2, :],
                                           bank(u).rearrange("p (e o) -> p e o", e=2), ACT.Copy).then_inc(s_lg, 1)
                        act.wait_ge(s_dve, DONE * n + DIST)
                        act.activation(lg[t % 2][:, :, :], tmp[:, :, :], ACT.Exp).then_inc(s_ez, 1)
                        act.activation(e1[:, :], n1[:, :], ACT.Exp).then_inc(s_ez, 1)

            @block.vector
            def _(dve):
                for k, load in ((0, load_r), (2, load_e)):
                    dve.wait_ge(load, 32)
                    for c in range(KC):
                        dve.wait_ge(s_whi, k + c + 1)
                        hi = rw_hi[:, c, :].bitcast(F32) if k == 0 else ew_hi[:, c, :]
                        lo = rw_lo if k == 0 else ew_lo
                        dve.tensor_tensor(lo[:, c, :], w_in[c][:, :], hi, ALU.subtract).then_inc(s_wlo, 1)
                dve.wait_ge(load_b, 32)
                dve.tensor_copy(b_part[:, 0, :, :], b_f[:, :, :]).then_inc(s_b, 1)
                for part in (1, 2):
                    dve.wait_ge(s_b, 2 * part - 1)
                    dve.tensor_tensor(b_f[:, :, :], b_f[:, :, :], b_part[:, part - 1, :, :], ALU.subtract).then_inc(s_b, 1)
                    dve.wait_ge(s_b, 2 * part)
                    dve.tensor_copy(b_part[:, part, :, :], b_f[:, :, :]).then_inc(s_b, 1)
                dve.wait_ge(const, 3)

                with dve.Fori(0, B) as b:
                    normalise_ops(lambda j: X[:, b, j, :], dve, X, stats, mv, rstd, xn,
                                  s_stat, s_mv, s_rstd, s_xn, b, passed_dve)
                    for c in range(KC):
                        dve.wait_ge(s_xhi, 4 * b + 2 * c + 2)
                        dve.tensor_tensor(xr_lo[:, c, :], bank(c), xr_hi[:, c, :].bitcast(F32), ALU.subtract).then_inc(s_xlo, 1)
                        dve.tensor_tensor(xb_lo[:, c, :], bank(c), xb_hi[:, c, :], ALU.subtract).then_inc(s_xlo, 1)
                    for t in range(4):
                        n = 4 * b + t
                        L, c_t = lg[t % 2], cw[t % 2]
                        Li, Ti = L[:, :, :].bitcast(I32), tmp[:, :, :].bitcast(I32)
                        done = [0]

                        def step(ins):
                            done[0] += 1
                            ins.then_inc(s_dve, 1)
                            dve.wait_ge(s_dve, DONE * n + done[0])

                        def free(ins):
                            done[0] += 1
                            ins.then_inc(s_dve, 1)

                        dve.wait_ge(s_lg, NU * n + NU)
                        free(dve.scalar_tensor_tensor(
                            Ti, Li, 31, code[:, :].rearrange("p (e o) -> p e o", o=1).to_broadcast([P, E, D]),
                            ALU.arith_shift_right, ALU.bitwise_xor))
                        step(dve.tensor_scalar(Li, Li, -8, None, ALU.bitwise_and))
                        step(dve.scalar_tensor_tensor(Li, Ti, 7, Li, ALU.bitwise_and, ALU.bitwise_or))
                        free(dve.tensor_tensor(h4[:, :, :], L[:, 0:4, :], L[:, 4:8, :], ALU.max))
                        step(dve.tensor_tensor(s4[:, :, :], L[:, 0:4, :], L[:, 4:8, :], ALU.min))
                        free(dve.tensor_tensor(h2[:, :, :], h4[:, 0:2, :], h4[:, 2:4, :], ALU.max))
                        free(dve.tensor_tensor(a2[:, :, :], h4[:, 0:2, :], h4[:, 2:4, :], ALU.min))
                        step(dve.tensor_tensor(c2[:, :, :], s4[:, 0:2, :], s4[:, 2:4, :], ALU.max))
                        step(dve.tensor_tensor(a2[:, :, :], a2[:, :, :], c2[:, :, :], ALU.max))
                        free(dve.tensor_tensor(m1[:, :], h2[:, 0, :], h2[:, 1, :], ALU.max))
                        free(dve.tensor_tensor(n1[:, :], h2[:, 0, :], h2[:, 1, :], ALU.min))
                        step(dve.tensor_tensor(c1[:, :], a2[:, 0, :], a2[:, 1, :], ALU.max))
                        step(dve.tensor_tensor(m2[:, :], n1[:, :], c1[:, :], ALU.max))
                        assert done[0] == TOP
                        step(dve.scalar_tensor_tensor(m2[:, :], m1[:, :], -CAP, m2[:, :], ALU.add, ALU.max))
                        dve.tensor_tensor(n1[:, :], m1[:, :], m2[:, :], ALU.subtract)
                        free(dve.tensor_tensor(tmp[:, :, :], L[:, :, :], over_experts(m2), ALU.subtract))
                        assert done[0] == DIST
                        dve.wait_ge(s_ez, 2 * n + 2)
                        step(dve.tensor_scalar(e1[:, :], e1[:, :], 1.0, None, ALU.add))
                        free(dve.reciprocal(n1[:, :], e1[:, :]))
                        step(dve.scalar_tensor_tensor(L[:, :, :], tmp[:, :, :], 0.0, L[:, :, :], ALU.is_ge, ALU.mult))
                        assert done[0] == WEIGHED
                        for e in range(E):
                            free(dve.tensor_tensor_reduce(out=tmp[:, e, :], in0=L[:, e, :], in1=n1[:, :], scale=1.0,
                                                          scalar=0.0, op0=ALU.mult, op1=ALU.add,
                                                          accum_out=c_t[:, e:e + 1]))
                        assert done[0] == DONE
                        dve.wait_ge(s_dve, DONE * n + DONE)
                        for u in range(NU):
                            dve.wait_ge(s_u, NU * n + u + 1)
                            for e in (0, 1):
                                x = X[:, b, t, :]
                                dve.scalar_tensor_tensor(x, bank(4 + u, D, D * e), c_t[:, 2 * u + e:2 * u + e + 1], x,
                                                         ALU.mult, ALU.add).then_inc(s_c, 1)
                                dve.wait_ge(s_c, E * n + 2 * u + e + 1)


H1 = 16
KV = 4
HQ = H1 // KV
HD1 = 128
GROUP = (HQ + 2) * HD1
T8 = 32
OC = 4
NB = S // P
SCALE1 = HD1 ** -0.5


def layer1_attention(nc, glob, A):
    X, ps, ident = glob["X"], glob["ps"], glob["ident"]
    passed_dve, passed_pool, passed_sp = glob["passed"]
    with ExitStack() as stack:
        st = Store(nc, stack)
        NW = KV * GROUP
        w_in = st.sb("w2_in", [P, NW], F32)
        wq_hi = st.sb("wq_hi", [P, KC, NW], BF16)
        wq_lo = st.sb("wq_lo", [P, KC, NW], BF16)
        wp_hi = st.sb("wp_hi", [P, H1, D], BF16)
        wp_lo = st.sb("wp_lo", [P, H1, D], BF16)
        stats = st.sb("stats2", [P, 4, 6], F32)
        mv = st.sb("mv2", [P, 4, 2], F32)
        rstd = st.sb("rstd2", [P, 4], F32)
        half = st.sb("half2", [P, 4], F32)
        xn = st.sb("xn2", [P, 4, D], F32)
        xT_hi = st.sb("xT2_hi", [P, KC, S], BF16)
        xT_lo = st.sb("xT2_lo", [P, KC, S], BF16)
        qk_hi = st.sb("qk1_hi", [P, KV, HQ + 1, S], BF16)
        qk_lo = st.sb("qk1_lo", [P, KV, HQ + 1, S], BF16)
        v = st.sb("v1", [P, NB, KV, HD1], F32)
        mask = st.sb("mask1", [P, T8], F32)
        sc = [st.sb(f"sc{n}", [P, H1, T8], F32) for n in range(2)]
        mx = [st.sb(f"mx1_{n}", [P, H1], F32) for n in range(2)]
        sm = [st.sb(f"sm1_{n}", [P, H1], F32) for n in range(2)]
        pT = [st.sb(f"pT{n}", [P, KV, OC, HQ * T8], F32) for n in range(2)]
        oT_hi = st.sb("oT1_hi", [P, H1, S], BF16)
        oT_lo = st.sb("oT1_lo", [P, H1, S], BF16)

        load_q = [st.sem(f"load_q{c}") for c in range(KC)]
        load_p = st.sem("load_p")
        const, const_v, s_whi, s_wlo = st.sem("const2"), st.sem("const2v"), st.sem("w2hi"), st.sem("w2lo")
        s_stat, s_mv, s_rstd = st.sem("stat2"), st.sem("mv2s"), st.sem("rstd2s")
        s_xn, s_tp, s_xhi, s_xlo = st.sem("xn2s"), st.sem("tp2"), st.sem("xhi2"), st.sem("xlo2")
        s_qk, s_qkhi, s_qklo = st.sem("qk1"), st.sem("qk1hi"), st.sem("qk1lo")
        s_v, s_vev, s_sc, s_sma, s_smb, s_ex = (
            st.sem(n) for n in ("v1s", "v1ev", "sc1", "shifted1", "softmax1", "exp1"))
        s_pv, s_ohi, s_olo, s_out, s_res = (st.sem(n) for n in ("pv1", "o1hi", "o1lo", "out1", "res1"))
        NM = KV * (HQ + 1)
        SMA, SMB = 4, 7
        TURNED, MASKED, MAXED, SHIFTED = 1, 2, 3, SMA

        def bank(n, width=BANK, off=0):
            return ps[:, n * BANK + off:n * BANK + off + width]

        def o_tile(a, j, k):
            return a[:, HQ * k:HQ * (k + 1), :].rearrange("p h (b t) -> p (h b) t", b=B)[:, :, T8 * j:T8 * (j + 1)]

        with nc.Block() as block:

            @block.sync
            def _(sp):
                for c in range(KC):
                    if c:
                        sp.wait_ge(s_wlo, c)
                    sp.dma_start(w_in[:, :], A["w_qkv"][P * c:P * (c + 1), :]).then_inc(load_q[c], 16)
                for n in range(2):
                    sp.wait_ge(s_wlo, KC + n)
                    sp.dma_start(w_in[:, 0:H1 // 2 * D].rearrange("p (h n) -> p h n", n=D),
                                 A["w_proj"].rearrange("(h p) n -> p h n", p=P)[:, H1 // 2 * n:H1 // 2 * (n + 1), :]
                                 ).then_inc(load_p, 16)
                    sp.wait_ge(load_p, 16 * (n + 1))

            @block.gpsimd
            def _(pool):
                pool.memset(half[:, :], -0.5).then_inc(const, 1)
                pool.memset(mask[:, :], -1.0e30).then_inc(const, 1)
                for m in range(P // 8):
                    pool.wait_ge(const, 2 + m)
                    mk = mask[:, :].rearrange("p (b q) -> p b q", q=8)
                    pool.affine_select(out=mk, in_=mk, compare_op=ALU.not_equal, fill=0.0, base=-8 * m,
                                       pattern=[[0, 4], [-1, 8]], channel_multiplier=1).then_inc(const, 1)
                with pool.Fori(0, G) as g:
                    rstd_ops(pool, mv, rstd, half, s_mv, s_rstd, g, passed_pool)

            @block.tensor
            def _(pe):
                pe.wait_ge(s_wlo, KC + 2)
                pe.wait_ge(s_whi, KC + 2)
                pe.wait_ge(const, 2 + P // 8)
                pe.wait_ge(const_v, 2)

                def three(out, lhs, rhs, chunks, **kw):
                    n = 0
                    for c in range(chunks):
                        for a, b_ in ((0, 0), (0, 1), (1, 0)):
                            mm = pe.matmul(out, lhs[a](c), rhs[b_](c), start=(n == 0), stop=(n == 3 * chunks - 1), **kw)
                            n += 1
                    return mm

                def turn(g):
                    pe.wait_ge(s_xn, 4 * g + 4)
                    reach(pe, s_res, 2 * g)
                    for c in range(KC):
                        for b in range(B):
                            tr = pe.transpose(bank(4 + c, P, P * b), xn[:, b, P * c:P * (c + 1)], ident[:, :])
                        tr.then_inc(s_tp, 1)

                def queries_keys(g):
                    pe.wait_ge(s_xhi, 2 * g + 2)
                    pe.wait_ge(s_xlo, 2 * g + 2)
                    for m in range(NM):
                        if m >= 4:
                            pe.wait_ge(s_qklo, NM * g + m - 3)
                        else:
                            reach(pe, s_qklo, NM * g)
                        w = GROUP * (m // (HQ + 1)) + HD1 * (m % (HQ + 1))
                        three(bank(4 + m % 4),
                              [lambda c: wq_hi[:, c, w:w + P], lambda c: wq_lo[:, c, w:w + P]],
                              [lambda c: xT_hi[:, c, :], lambda c: xT_lo[:, c, :]], KC).then_inc(s_qk, 1)

                def values(g):
                    pe.wait_ge(s_qklo, NM * g + NM)
                    for j in range(NB):
                        wv = [w[:, :, :].rearrange("p c (k n) -> p c k n", k=KV)[:, :, :, (HQ + 1) * HD1:]
                              for w in (wq_hi, wq_lo)]
                        three(bank(4 + j).rearrange("p (k n) -> p k n", k=KV),
                              [lambda c: xT_hi[:, c, P * j:P * (j + 1)], lambda c: xT_lo[:, c, P * j:P * (j + 1)]],
                              [lambda c: wv[0][:, c, :, :], lambda c: wv[1][:, c, :, :]], KC).then_inc(s_v, 1)

                def scores(g):
                    pe.wait_ge(s_qklo, NM * g + NM)
                    for j in range(NB):
                        for k in range(KV):
                            for i, (a, b_) in enumerate(((qk_hi, qk_hi), (qk_hi, qk_lo), (qk_lo, qk_hi))):
                                for o in range(OC):
                                    t = P * j + T8 * o
                                    mm = pe.matmul(
                                        ps[T8 * o:T8 * (o + 1), BANK * j + P * k:BANK * j + P * (k + 1)]
                                        .rearrange("p (h q) -> p h q", q=T8),
                                        a[:, k, HQ, t:t + T8], b_[:, k, 0:HQ, t:t + T8],
                                        start=(i == 0), stop=(i == 2), skip_group_check=True)
                        mm.then_inc(s_sc, 1)

                def outputs(g):
                    pe.wait_ge(s_vev, NB * g + NB)
                    for j in range(NB):
                        n = NB * g + j
                        pe.wait_ge(s_smb, SMB * n + SMB)
                        for k in range(KV):
                            if j:
                                pe.wait_ge(s_olo, KV * (n - 1) + k + 1)
                            pe.matmul(bank(4 + k).rearrange("p (n o q) -> p n o q", o=OC, q=8), v[:, j, k, :],
                                      pT[j % 2][:, k, :, :].rearrange("p o (n q) -> p n o q", q=8),
                                      start=True, stop=True).then_inc(s_pv, 1)

                def project(g):
                    pe.wait_ge(s_olo, NB * KV * (g + 1))
                    pe.wait_ge(s_ohi, NB * KV * (g + 1))
                    pe.wait_ge(s_vev, NB * g + NB)
                    for b in range(B):
                        def o_of(a):
                            return lambda h: a[:, h, P * b:P * (b + 1)]
                        mm = three(bank(4 + b // 2, D, D * (b % 2)), [o_of(oT_hi), o_of(oT_lo)],
                                   [lambda h: wp_hi[:, h, :], lambda h: wp_lo[:, h, :]], H1)
                        if b % 2:
                            mm.then_inc(s_out, 1)

                with pe.Fori(0, G) as g:
                    turn(g)
                    queries_keys(g)
                    scores(g)
                    values(g)
                    outputs(g)
                    project(g)

            @block.scalar
            def _(act):
                for c in range(KC):
                    act.wait_ge(load_q[c], 16)
                    act.activation(wq_hi[:, c, :], w_in[:, :], ACT.Copy).then_inc(s_whi, 1)
                for n in range(2):
                    act.wait_ge(load_p, 16 * (n + 1))
                    hs = slice(H1 // 2 * n, H1 // 2 * (n + 1))
                    act.activation(wp_hi[:, hs, :], w_in[:, 0:H1 // 2 * D].rearrange("p (h n) -> p h n", n=D),
                                   ACT.Copy).then_inc(s_whi, 1)

                with act.Fori(0, G) as g:
                    for c in range(KC):
                        act.wait_ge(s_tp, 2 * g + c + 1)
                        act.activation(xT_hi[:, c, :].rearrange("p (o b q) -> p b o q", b=B, q=8),
                                       bank(4 + c).rearrange("p (b o q) -> p b o q", b=B, q=8),
                                       ACT.Copy).then_inc(s_xhi, 1)
                    for m in range(NM):
                        act.wait_ge(s_qk, NM * g + m + 1)
                        act.activation(qk_hi[:, m // (HQ + 1), m % (HQ + 1), :], bank(4 + m % 4),
                                       ACT.Copy).then_inc(s_qkhi, 1)
                    for j in range(NB):
                        act.wait_ge(s_v, NB * g + j + 1)
                        act.activation(v[:, j, :, :], bank(4 + j).rearrange("p (k n) -> p k n", k=KV),
                                       ACT.Copy).then_inc(s_vev, 1)
                    def exponentials(j):
                        n = NB * g + j
                        act.wait_ge(s_sma, SMA * n + SHIFTED)
                        act.activation(sc[j % 2][:, :, :], sc[j % 2][:, :, :], ACT.Exp, scale=SCALE1).then_inc(s_ex, 1)

                    def outputs_hi(j):
                        n = NB * g + j
                        for k in range(KV):
                            act.wait_ge(s_pv, KV * n + k + 1)
                            act.activation(o_tile(oT_hi, j, k), bank(4 + k).rearrange("p (n q) -> p n q", q=T8),
                                           ACT.Copy).then_inc(s_ohi, 1)

                    exponentials(0)
                    for j in range(NB):
                        if j + 1 < NB:
                            exponentials(j + 1)
                        if j:
                            outputs_hi(j - 1)
                    outputs_hi(NB - 1)

            @block.vector
            def _(dve):
                for n in range(2):
                    dve.memset(pT[n][:, :, :, :], 0.0).then_inc(const_v, 1)
                for c in range(KC):
                    dve.wait_ge(s_whi, c + 1)
                    dve.tensor_tensor(wq_lo[:, c, :], w_in[:, :], wq_hi[:, c, :], ALU.subtract).then_inc(s_wlo, 1)
                for n in range(2):
                    dve.wait_ge(s_whi, KC + n + 1)
                    hs = slice(H1 // 2 * n, H1 // 2 * (n + 1))
                    dve.tensor_tensor(wp_lo[:, hs, :], w_in[:, 0:H1 // 2 * D].rearrange("p (h n) -> p h n", n=D),
                                      wp_hi[:, hs, :], ALU.subtract).then_inc(s_wlo, 1)
                dve.wait_ge(const_v, 2)

                def softmax_a(g, j):
                    n, s, m = NB * g + j, sc[j % 2], mx[j % 2]
                    dve.wait_ge(s_sc, n + 1)
                    reach(dve, s_smb, SMB * (n - 1) if j >= 2 else SMB * NB * g)
                    dve.transpose(s[:, :, :].rearrange("p h q -> p (h q)"), bank(j)).then_inc(s_sma, 1)
                    dve.wait_ge(s_sma, SMA * n + TURNED)
                    dve.tensor_tensor(s[:, :, :], s[:, :, :],
                                      mask[:, :].rearrange("p (o q) -> p o q", o=1).to_broadcast([P, H1, T8]),
                                      ALU.add).then_inc(s_sma, 1)
                    dve.wait_ge(s_sma, SMA * n + MASKED)
                    dve.tensor_reduce(m[:, :], s[:, :, :], AX_X, ALU.max).then_inc(s_sma, 1)
                    dve.wait_ge(s_sma, SMA * n + MAXED)
                    dve.tensor_tensor(s[:, :, :], s[:, :, :],
                                      m[:, :].rearrange("p (h o) -> p h o", o=1).to_broadcast([P, H1, T8]),
                                      ALU.subtract).then_inc(s_sma, 1)

                def softmax_b(g, j):
                    n, s, z = NB * g + j, sc[j % 2], sm[j % 2]
                    dve.wait_ge(s_ex, n + 1)
                    dve.tensor_reduce(z[:, :], s[:, :, :], AX_X, ALU.add).then_inc(s_smb, 1)
                    dve.wait_ge(s_smb, SMB * n + 1)
                    dve.reciprocal(z[:, :], z[:, :]).then_inc(s_smb, 1)
                    dve.wait_ge(s_smb, SMB * n + 2)
                    dve.tensor_tensor(s[:, :, :], s[:, :, :],
                                      z[:, :].rearrange("p (h o) -> p h o", o=1).to_broadcast([P, H1, T8]),
                                      ALU.mult).then_inc(s_smb, 1)
                    dve.wait_ge(s_smb, SMB * n + 3)
                    if j >= 2:
                        dve.wait_ge(s_pv, KV * (n - 1))
                    else:
                        reach(dve, s_pv, KV * NB * g)
                    for o in range(OC):
                        rows = slice(T8 * o, T8 * (o + 1))
                        dve.transpose(pT[j % 2][rows, :, o, :],
                                      s[rows, :, :].rearrange("p (k h) q -> p k (h q)", k=KV)).then_inc(s_smb, 1)

                def outputs_lo(g, j):
                    n = NB * g + j
                    for k in range(KV):
                        dve.wait_ge(s_ohi, KV * n + k + 1)
                        dve.tensor_tensor(o_tile(oT_lo, j, k), bank(4 + k).rearrange("p (n q) -> p n q", q=T8),
                                          o_tile(oT_hi, j, k), ALU.subtract).then_inc(s_olo, 1)

                with dve.Fori(0, G) as g:
                    normalise_ops(lambda b: X[:, b, g, :], dve, X, stats, mv, rstd, xn,
                                  s_stat, s_mv, s_rstd, s_xn, g, passed_dve)
                    for c in range(KC):
                        dve.wait_ge(s_xhi, 2 * g + c + 1)
                        dve.tensor_tensor(xT_lo[:, c, :].rearrange("p (o b q) -> p b o q", b=B, q=8),
                                          bank(4 + c).rearrange("p (b o q) -> p b o q", b=B, q=8),
                                          xT_hi[:, c, :].rearrange("p (o b q) -> p b o q", b=B, q=8),
                                          ALU.subtract).then_inc(s_xlo, 1)
                    for m in range(NM):
                        dve.wait_ge(s_qkhi, NM * g + m + 1)
                        k, h = m // (HQ + 1), m % (HQ + 1)
                        dve.tensor_tensor(qk_lo[:, k, h, :], bank(4 + m % 4), qk_hi[:, k, h, :],
                                          ALU.subtract).then_inc(s_qklo, 1)
                    softmax_a(g, 0)
                    for j in range(NB):
                        if j + 1 < NB:
                            softmax_a(g, j + 1)
                        softmax_b(g, j)
                        if j:
                            outputs_lo(g, j - 1)
                    outputs_lo(g, NB - 1)
                    for t in range(2):
                        dve.wait_ge(s_out, 2 * g + t + 1)
                        xr = X[:, 2 * t:2 * t + 2, g, :]
                        dve.tensor_tensor(xr, bank(4 + t).rearrange("p (b n) -> p b n", b=2), xr,
                                          ALU.add).then_inc(s_res, 1)


FF = 2048
MT = FF // P
GELU_C = 0.7978845608028654
GELU_A = 0.044715


def layer1_mlp(nc, glob, A):
    X, ps, ident = glob["X"], glob["ps"], glob["ident"]
    passed_dve, passed_pool, passed_sp = glob["passed"]
    with ExitStack() as stack:
        st = Store(nc, stack)
        NAMES = ("gate", "up", "down")
        packed = [st.sb(f"packed{n}", [P, FF], I32) for n in range(2)]
        scales = [st.sb(f"scales{n}", [P, FF], F32) for n in range(2)]
        sign = st.sb("sign", [P, FF], I32)
        code = st.sb("codes", [P, FF], I32)
        mag = st.sb("mag", [P, FF], F32)
        w_hi = [st.sb(f"w_{n}_hi", [P, 2, FF], BF16) for n in NAMES]
        w_lo = [st.sb(f"w_{n}_lo", [P, 2, FF], BF16) for n in NAMES]
        stats = st.sb("stats3", [P, 4, 6], F32)
        mv = st.sb("mv3", [P, 4, 2], F32)
        rstd = st.sb("rstd3", [P, 4], F32)
        half = st.sb("half3", [P, 4], F32)
        xn = st.sb("xn3", [P, 4, D], F32)
        xT_hi = st.sb("xT3_hi", [P, 2, S], BF16)
        xT_lo = st.sb("xT3_lo", [P, 2, S], BF16)
        g2 = [st.sb(f"g2_{n}", [P, S], F32) for n in range(2)]
        th = [st.sb(f"th_{n}", [P, S], F32) for n in range(2)]
        it = [st.sb(f"it_{n}", [P, S], F32) for n in range(2)]
        it_hi = [st.sb(f"it_hi{n}", [P, S], BF16) for n in range(2)]
        it_lo = [st.sb(f"it_lo{n}", [P, S], BF16) for n in range(2)]

        load = [st.sem(f"load_{n}") for n in NAMES]
        const, s_dq, s_whi = st.sem("const3"), st.sem("dequant"), st.sem("w3hi")
        s_stat, s_mv, s_rstd = st.sem("stat3"), st.sem("mv3s"), st.sem("rstd3s")
        s_xn, s_tp, s_xhi, s_xlo = st.sem("xn3s"), st.sem("tp3"), st.sem("xhi3"), st.sem("xlo3")
        s_gu, s_sq, s_in, s_th, s_it, s_ihi, s_ilo, s_dn, s_gate, s_res = (
            st.sem(n) for n in ("gateup", "square", "inner", "tanh", "inter", "interhi", "interlo", "down", "gelu", "res3"))
        DQ = 8

        def bank(n, width=BANK, off=0):
            return ps[:, n * BANK + off:n * BANK + off + width]

        with nc.Block() as block:

            @block.sync
            def _(sp):
                for n, name in enumerate(NAMES):
                    if n == 2:
                        sp.wait_ge(s_dq, 2 * DQ)
                    w, s = A[f"{name}_W"], A[f"{name}_s"]
                    if name == "down":
                        w = w.rearrange("(c p) n -> p c n", p=P)
                        sp.dma_start(packed[n % 2][:, :].rearrange("p (c n) -> p c n", n=D), w).then_inc(load[n], 16)
                        for k in range(8):
                            sp.dma_start(scales[n % 2][16 * k:16 * (k + 1), :].rearrange("p (c n) -> p c n", n=D),
                                         s.rearrange("(c k) n -> k c n", k=8)[k:k + 1, :, :].to_broadcast([16, 8, D])
                                         ).then_inc(load[n], 16)
                    else:
                        sp.dma_start(packed[n % 2][:, :], w).then_inc(load[n], 16)
                        for k in range(8):
                            sp.dma_start(scales[n % 2][16 * k:16 * (k + 1), :],
                                         s[k:k + 1, :].to_broadcast([16, FF])).then_inc(load[n], 16)

            @block.gpsimd
            def _(pool):
                pool.memset(half[:, :], -0.5).then_inc(const, 1)
                with pool.Fori(0, B) as b:
                    rstd_ops(pool, mv, rstd, half, s_mv, s_rstd, b, passed_pool)

            @block.tensor
            def _(pe):
                pe.wait_ge(s_dq, 6 * DQ)
                pe.wait_ge(const, 1)

                def turn(b):
                    pe.wait_ge(s_xn, 4 * b + 4)
                    reach(pe, s_it, MT * b)
                    for c in range(2):
                        for t in range(4):
                            tr = pe.transpose(bank(c, P, P * t), xn[:, t, c:D:2], ident[:, :])
                        tr.then_inc(s_tp, 1)

                def gate_up(b, m):
                    if m >= 3:
                        pe.wait_ge(s_it, MT * b + m - 2)
                    else:
                        reach(pe, s_it, MT * b)
                    for k in range(2):
                        n = 0
                        for c in range(2):
                            for w, x in ((w_hi, xT_hi), (w_hi, xT_lo), (w_lo, xT_hi)):
                                mm = pe.matmul(bank(2 * (m % 3) + k), w[k][:, c, P * m:P * (m + 1)], x[:, c, :],
                                               start=(n == 0), stop=(n == 5))
                                n += 1
                        mm.then_inc(s_gu, 1)

                def down(b, m):
                    pe.wait_ge(s_ilo, MT * b + m + 1)
                    pe.wait_ge(s_ihi, MT * b + m + 1)
                    if m == 0:
                        reach(pe, s_res, 2 * b)
                    for t in range(4):
                        n = 0
                        for a, w in ((it_hi, w_hi), (it_hi, w_lo), (it_lo, w_hi)):
                            mm = pe.matmul(bank(6 + t // 2, D, D * (t % 2)), a[m % 2][:, P * t:P * (t + 1)],
                                           w[2][:, m % 2, D * (m // 2):D * (m // 2 + 1)],
                                           start=(m == 0 and n == 0 and t % 2 == 0), stop=(m == MT - 1 and n == 2),
                                           skip_group_check=True)
                            n += 1
                    mm.then_inc(s_dn, 1)

                with pe.Fori(0, B) as b:
                    turn(b)
                    pe.wait_ge(s_xhi, 2 * b + 2)
                    pe.wait_ge(s_xlo, 2 * b + 2)
                    for m in range(MT + 2):
                        if m < MT:
                            gate_up(b, m)
                        if m >= 2:
                            down(b, m - 2)

            @block.scalar
            def _(act):
                for n in range(3):
                    for c in range(2):
                        act.wait_ge(s_dq, DQ * (2 * n + c) + DQ - 1)
                        act.activation(w_hi[n][:, c, :], mag[:, :], ACT.Copy, scale=0.5).then_inc(s_whi, 1)
                with act.Fori(0, B) as b:
                    for c in range(2):
                        act.wait_ge(s_tp, 2 * b + c + 1)
                        act.activation(xT_hi[:, c, :], bank(c), ACT.Copy).then_inc(s_xhi, 1)

                    def square(m):
                        n = MT * b + m
                        act.wait_ge(s_gu, 2 * n + 2)
                        reach(act, s_in, n - 1 if m >= 2 else MT * b)
                        act.activation(g2[m % 2][:, :], bank(2 * (m % 3)), ACT.Square, scale=GELU_A ** 0.5).then_inc(s_sq, 1)

                    def tanh(m):
                        n = MT * b + m
                        act.wait_ge(s_in, n + 1)
                        reach(act, s_it, n - 1 if m >= 2 else MT * b)
                        act.activation(th[m % 2][:, :], g2[m % 2][:, :], ACT.Tanh, scale=GELU_C).then_inc(s_th, 1)

                    def high(m):
                        n = MT * b + m
                        act.wait_ge(s_it, n + 1)
                        reach(act, s_dn, n - 1 if m >= 2 else MT * b)
                        act.activation(it_hi[m % 2][:, :], it[m % 2][:, :], ACT.Copy).then_inc(s_ihi, 1)

                    square(0)
                    for m in range(MT):
                        tanh(m)
                        if m + 1 < MT:
                            square(m + 1)
                        high(m)

            @block.vector
            def _(dve):
                for n in range(3):
                    dve.wait_ge(load[n], 16 * 9)
                    p, s = packed[n % 2], scales[n % 2]
                    for c in range(2):
                        k = DQ * (2 * n + c)

                        def step(ins, ready):
                            ins.then_inc(s_dq, 1)
                            dve.wait_ge(s_dq, k + ready)

                        step(dve.tensor_scalar(sign[:, :], p[:, :], 28 - 4 * c, -2 ** 31,
                                               ALU.logical_shift_left, ALU.bitwise_and), 1)
                        step(dve.tensor_scalar(code[:, :], p[:, :], 4 * c, 7,
                                               ALU.logical_shift_right, ALU.bitwise_and), 2)
                        step(dve.scalar_tensor_tensor(mag[:, :], code[:, :], 4.0, code[:, :], ALU.max, ALU.add), 3)
                        step(dve.scalar_tensor_tensor(mag[:, :], code[:, :], 6.0, mag[:, :], ALU.max, ALU.add), 4)
                        step(dve.scalar_tensor_tensor(mag[:, :], code[:, :], 6.0, mag[:, :], ALU.max, ALU.add), 5)
                        step(dve.scalar_tensor_tensor(mag[:, :], mag[:, :], -16.0, s[:, :], ALU.add, ALU.mult), 6)
                        step(dve.tensor_tensor(mag[:, :].bitcast(I32), mag[:, :].bitcast(I32), sign[:, :], ALU.bitwise_xor), 7)
                        dve.wait_ge(s_whi, 2 * n + c + 1)
                        step(dve.scalar_tensor_tensor(w_lo[n][:, c, :], mag[:, :], 0.5, w_hi[n][:, c, :],
                                                      ALU.mult, ALU.subtract), 8)
                with dve.Fori(0, B) as b:
                    normalise_ops(lambda t: X[:, b, t, :], dve, X, stats, mv, rstd, xn,
                                  s_stat, s_mv, s_rstd, s_xn, b, passed_dve)
                    for c in range(2):
                        dve.wait_ge(s_xhi, 2 * b + c + 1)
                        dve.tensor_tensor(xT_lo[:, c, :], bank(c), xT_hi[:, c, :], ALU.subtract).then_inc(s_xlo, 1)

                    def inner(m):
                        n = MT * b + m
                        dve.wait_ge(s_sq, n + 1)
                        dve.scalar_tensor_tensor(g2[m % 2][:, :], g2[m % 2][:, :], 1.0, bank(2 * (m % 3)),
                                                 ALU.add, ALU.mult).then_inc(s_in, 1)

                    def inter(m):
                        n = MT * b + m
                        dve.wait_ge(s_th, n + 1)
                        dve.scalar_tensor_tensor(th[m % 2][:, :], th[m % 2][:, :], 1.0, bank(2 * (m % 3)),
                                                 ALU.add, ALU.mult).then_inc(s_gate, 1)
                        dve.wait_ge(s_gate, n + 1)
                        dve.scalar_tensor_tensor(it[m % 2][:, :], th[m % 2][:, :], 0.5, bank(2 * (m % 3) + 1),
                                                 ALU.mult, ALU.mult).then_inc(s_it, 1)

                    def low(m):
                        n = MT * b + m
                        dve.wait_ge(s_ihi, n + 1)
                        reach(dve, s_dn, n - 1 if m >= 2 else MT * b)
                        dve.tensor_tensor(it_lo[m % 2][:, :], it[m % 2][:, :], it_hi[m % 2][:, :], ALU.subtract).then_inc(s_ilo, 1)

                    inner(0)
                    for m in range(MT):
                        inter(m)
                        if m + 1 < MT:
                            inner(m + 1)
                        low(m)
                    for t in range(2):
                        dve.wait_ge(s_dn, MT * b + MT)
                        xr = X[:, b, 2 * t:2 * t + 2, :]
                        dve.tensor_tensor(xr, bank(6 + t).rearrange("p (t n) -> p t n", t=2), xr,
                                          ALU.add).then_inc(s_res, 1)


def build(nc, A, out, phases=(1, 2, 3, 4)):
    with ExitStack() as stack:
        st = Store(nc, stack)
        X = st.sb("X", [P, B, G, D], F32)
        ident = st.sb("ident", [P, P], F32)
        identb = st.sb("identb", [P, P], BF16)
        ps = stack.enter_context(nc.psum_tensor("ps", [P, 8 * BANK], F32))
        x_in, made = st.sem("x_in"), st.sem("made")
        glob = {
            "passed": [st.sem(f"passed_{n}") for n in ("dve", "pool", "sp")],
            "X": X, "ps": ps, "ident": ident, "identb": identb,
            "scratch_q": nc.dram_tensor("scratch_q", [2, D, S], BF16, kind="Internal").ap(),
            "scratch_k": nc.dram_tensor("scratch_k", [2, D, S], BF16, kind="Internal").ap(),
        }
        with nc.Block() as block:

            @block.sync
            def _(sp):
                for b in range(B):
                    sp.dma_start(X[:, b, :, :], A["x"][b].rearrange("(g p) d -> p g d", p=P)).then_inc(x_in, 16)
                sp.wait_ge(x_in, 16 * B)

            @block.gpsimd
            def _(pool):
                pool.memset(ident[:, :], 0.0).then_inc(made, 1)
                pool.wait_ge(made, 1)
                pool.affine_select(out=ident[:, :], in_=ident[:, :], compare_op=ALU.not_equal, fill=1.0, base=0,
                                   pattern=[[-1, P]], channel_multiplier=1).then_inc(made, 1)
                pool.wait_ge(made, 2)
                pool.tensor_copy(identb[:, :], ident[:, :]).then_inc(made, 1)

        if 1 in phases:
            layer0_attention(nc, glob, A)
        if 2 in phases:
            layer0_mixture(nc, glob, A)
        if 3 in phases:
            layer1_attention(nc, glob, A)
        if 4 in phases:
            layer1_mlp(nc, glob, A)

        stored = st.sem("stored")
        with nc.Block() as block:

            @block.sync
            def _(sp):
                for b in range(B):
                    sp.dma_start(out[b].rearrange("(g p) d -> p g d", p=P), X[:, b, :, :]).then_inc(stored, 16)
                sp.wait_ge(stored, 16 * B)


def layouts(L0_attn_x, L0_attn_w_project, L0_attn_w_out, L0_ffn_router_w, L0_ffn_router_b, L0_ffn_expert_w,
            L0_ffn_expert_b, L1_attn_w_qkv, L1_attn_w_proj, L1_ffn_gate_W_packed, L1_ffn_gate_scales,
            L1_ffn_up_W_packed, L1_ffn_up_scales, L1_ffn_down_W_packed, L1_ffn_down_scales):
    E, O = L0_ffn_expert_b.shape
    return {
        "x": L0_attn_x,
        "w_project": L0_attn_w_project.T,
        "w_out": L0_attn_w_out.T,
        "router_w": L0_ffn_router_w.reshape(O, E, D).transpose(2, 1, 0).reshape(D, E * O),
        "router_b": L0_ffn_router_b.reshape(O, E).T.reshape(1, E * O),
        "expert_w": L0_ffn_expert_w.transpose(2, 0, 1).reshape(D, E * O),
        "expert_b": L0_ffn_expert_b.reshape(1, E * O),
        "w_qkv": L1_attn_w_qkv.T,
        "w_proj": L1_attn_w_proj.T,
        "gate_W": hidden_order(L1_ffn_gate_W_packed).T,
        "gate_s": hidden_order(L1_ffn_gate_scales).T,
        "up_W": hidden_order(L1_ffn_up_W_packed).T,
        "up_s": hidden_order(L1_ffn_up_scales).T,
        "down_W": L1_ffn_down_W_packed.T,
        "down_s": L1_ffn_down_scales.T,
    }


def hidden_order(a):
    n, k = a.shape
    return a.reshape(n // 256, 128, 2, k).transpose(0, 2, 1, 3).reshape(n, k)


def kernel(**inputs):
    import concourse.bacc as bacc
    from concourse.bass_utils import run_bass_kernel_spmd

    arrays = {name: np.ascontiguousarray(a) for name, a in layouts(**{k: np.asarray(v) for k, v in inputs.items()}).items()}
    nc = bacc.Bacc("TRN2", target_bir_lowering=False, num_devices=1)
    A = {name: nc.dram_tensor(f"in_{name}", a.shape, mybir.dt.from_np(a.dtype), kind="ExternalInput").ap()
         for name, a in arrays.items()}
    out = nc.dram_tensor("out", arrays["x"].shape, F32, kind="ExternalOutput").ap()
    build(nc, A, out)
    r = run_bass_kernel_spmd(nc, [{f"in_{name}": a for name, a in arrays.items()}], core_ids=[0])
    return r.results[0]["out"]
```

```python
from contextlib import ExitStack
from itertools import islice

import numpy as np

import concourse.bass as bass
from concourse import mybir

F32 = mybir.dt.float32
F32R = mybir.dt.float32r
BF16 = mybir.dt.bfloat16
I32 = mybir.dt.int32
ALU = mybir.AluOpType
ACT = mybir.ActivationFunctionType
AX_X = mybir.AxisListType.X

P = 128
B = 4
S = 512
D = 256
KC = D // P
G = S // P
BANK = 512
EPS = 1e-5


class Store:

    def __init__(self, nc, stack):
        self.nc, self.stack = nc, stack

    def sb(self, name, shape, dt, side="left"):
        return self.stack.enter_context(self.nc.sbuf_tensor(name, shape, dt, side=side))

    def sem(self, name):
        return self.stack.enter_context(self.nc.semaphore(name))


def reach(eng, sem, value):
    if not (isinstance(value, int) and value <= 0):
        eng.wait_ge(sem, value)


def wait_alone(eng, sem, value, passed):
    eng.wait_ge(sem, value)
    eng.sem_inc(passed, 1)



def work_between(pieces):
    todo = iter(pieces)

    def some(k=1):
        for piece in islice(todo, k):
            piece()
    return some


E = 8
EO = E * D
H1 = 16
KV = 4
HQ = H1 // KV
HD1 = 128
GROUP = (HQ + 2) * HD1
NW = KV * GROUP


FF = 2048
UC = 256
NC = FF // UC
DQ = 10


def unit_columns(a, parities=False):
    return a[:, :, :].rearrange("p c (u n) -> p u c n", n=UC) if parities else a[:, :].rearrange("p (u n) -> p u n", n=UC)


class Dequant:

    def __init__(self, st, stage, passed_sp, tag):
        self.passed_sp = passed_sp
        words = stage[:, :, :].rearrange("p a n -> p (a n)").bitcast(I32)
        self.packed = [words[:, UC * n:UC * (n + 1)] for n in (0, 1)]
        self.scales = [words[:, UC * n:UC * (n + 1)].bitcast(F32) for n in (2, 3)]
        self.sign = words[:, 4 * UC:6 * UC].rearrange("p (c n) -> p c n", c=2)
        self.code = words[:, 6 * UC:8 * UC].rearrange("p (c n) -> p c n", c=2)
        self.mag = st.sb(f"mag_{tag}", [P, 2, UC], F32)
        self.load = [st.sem(f"load_unit{n}_{tag}") for n in (0, 1)]
        self.step, self.high = st.sem(f"dequant_{tag}"), st.sem(f"dequant_hi_{tag}")

    def fetch(self, sp, n, parity, w, s):
        if not isinstance(n, int) or n >= 2:
            wait_alone(sp, self.step, DQ * (n - 1), self.passed_sp)
        sp.dma_start(self.packed[parity], w).then_inc(self.load[parity], 16)
        for k in range(8):
            rows = self.scales[parity][16 * k:16 * (k + 1), :]
            sp.dma_start(rows, s[k:k + 1, :].to_broadcast([16, UC])).then_inc(self.load[parity], 16)

    def pieces(self, dve, n, parity, use, w_lo, w_hi):
        p, mag, code = self.packed[parity], self.mag[:, :, :], self.code
        s = self.scales[parity].rearrange("p (o n) -> p o n", o=1).to_broadcast([P, 2, UC])

        def made(k, ins):
            def piece():
                reach(dve, self.step, DQ * n + k)
                if k == 0:
                    dve.wait_ge(self.load[parity], 16 * 9 * (use + 1))
                if k == DQ - 1:
                    dve.wait_ge(self.high, n + 1)
                ins().then_inc(self.step, 1)
            return piece
        i32 = mag.bitcast(I32)
        return [made(k, ins) for k, ins in enumerate([
            lambda: dve.tensor_scalar(self.sign[:, 0, :], p, 28, -2 ** 31, ALU.logical_shift_left, ALU.bitwise_and),
            lambda: dve.tensor_scalar(self.sign[:, 1, :], p, 24, -2 ** 31, ALU.logical_shift_left, ALU.bitwise_and),
            lambda: dve.tensor_scalar(code[:, 0, :], p, 7, None, ALU.bitwise_and),
            lambda: dve.tensor_scalar(code[:, 1, :], p, 4, 7, ALU.logical_shift_right, ALU.bitwise_and),
            lambda: dve.scalar_tensor_tensor(mag, code, 4.0, code, ALU.max, ALU.add),
            lambda: dve.scalar_tensor_tensor(mag, code, 6.0, mag, ALU.max, ALU.add),
            lambda: dve.scalar_tensor_tensor(mag, code, 6.0, mag, ALU.max, ALU.add),
            lambda: dve.scalar_tensor_tensor(mag, mag, -16.0, s, ALU.add, ALU.mult),
            lambda: dve.tensor_tensor(i32, i32, self.sign, ALU.bitwise_xor),
            lambda: dve.scalar_tensor_tensor(w_lo, mag, 0.5, w_hi, ALU.mult, ALU.subtract),
        ])]

    def make_high(self, act, n, w_hi):
        act.wait_ge(self.step, DQ * n + DQ - 1)
        act.activation(w_hi, self.mag[:, :, :], ACT.Copy, scale=0.5).then_inc(self.high, 1)

H0 = 16
HD0 = D // H0
HG = 4
NG = H0 // HG
HB = 32
STK = 4 * HD0
SHIFT = 96
NEG = -3.0e38


def max_units(pair):
    a, b = 2 * pair, 2 * pair + 1
    return [
        [(a, 3, k) for k in range(4)],
        [(b, 3, k) for k in range(4)],
        [(a, 2, k) for k in range(3)] + [(a, 0, 0)],
        [(b, 2, k) for k in range(3)] + [(b, 0, 0)],
        [(a, 1, 0), (a, 1, 1), (b, 1, 0), (b, 1, 1)],
    ]


def max_work(g):
    return [("max", (g, n)) for n in range(10)]


PREPARE = [("xT", 0), ("xT", 1), ("qk", 0), ("qk", 1), ("qk", 2), ("qk", 3)]
START = PREPARE + max_work(0) + max_work(1)[:2] + [("turn", 0)] + max_work(1)[2:]


def bank_work(first, last):
    def behind_turn(g, work):
        return work[:1] + [("turn", g)] + work[1:]
    m = max_work(2)
    prepared = m[:2] + PREPARE[:2] + m[2:3] + PREPARE[2:4] + m[3:4] + PREPARE[4:] + m[4:]
    return [
        [("v", 0), ("v", 1), ("turn", 1)] + (m if last else prepared) + ([] if first else [("proj", 0), ("proj", 1)]),
        behind_turn(2, max_work(3)),
        [("turn", 3)] if last else behind_turn(3, max_work(0)),
        [] if last else behind_turn(0, max_work(1)),
    ]


def in_group(work, den):
    cut = [0] + [round(len(work) * f) for f in (.1, .3, .4, .6, .7, .9, 1)]
    w = [[("work", x) for x in work[a:b]] for a, b in zip(cut, cut[1:])]
    norm = [[("norm", q)] * den for q in range(G)]
    return ([("score", 0)] + w[0] + [("score", 1)] + [("den", 0)] * den + w[1] + [("score", 2)] + w[2] + norm[0]
            + [("score", 3)] + w[3][:1] + norm[1] + w[3][1:] + norm[2] + [("values", 0), ("score", 4)] + w[4] + norm[3]
            + [("values", 1), ("score", 5)] + w[5] + [("values", 2)] + w[6] + [("values", 3)])


def layer0_attention(nc, glob, A):
    X, ps, ident, identb = glob["X"], glob["ps"], glob["ident"], glob["identb"]
    passed_dve, passed_pool, passed_sp = glob["passed"]
    scratch_q, scratch_k = glob["scratch_q"], glob["scratch_k"]
    with ExitStack() as stack:
        st = Store(nc, stack)
        w_f = st.sb("w0_f", [P, KC, 3 * D], F32)
        w_hi = st.sb("w0_hi", [P, KC, 3 * D], BF16)
        w_lo = st.sb("w0_lo", [P, KC, 3 * D], BF16)
        wo = st.sb("wo0", [P, NG, D], F32)
        maskneg = st.sb("maskneg", [P, P], BF16)
        sel = st.sb("sel0", [P, P], F32)
        stats = st.sb("stats0", [P, G, 6], F32)
        mv = st.sb("mv0", [P, G, 2], F32)
        rstd = st.sb("rstd0", [P, G], F32)
        half = st.sb("half0", [P, G], F32)
        xn = st.sb("xn0", [P, G, D], F32)
        xT_hi = st.sb("xT0_hi", [P, KC, S], BF16)
        xT_lo = st.sb("xT0_lo", [P, KC, S], BF16)
        qk_hi = st.sb("qk_hi", [P, 4, S], BF16)
        qk_lo = st.sb("qk_lo", [P, 4, S], BF16)
        qs = st.sb("qs", [SHIFT + 2, H0, S], BF16)
        ks = st.sb("ks", [SHIFT + 2, H0, S], BF16)
        v = st.sb("v0", [P, G, H0, HB], F32)
        bm = st.sb("bm", [P, H0 // 2, 20], F32)
        mx = st.sb("mx", [P, H0, G], F32)
        mt_f = st.sb("mt_f", [HG * G, P], F32)
        mt_hi = st.sb("mt_hi", [HG * G, P], BF16)
        mt_lo = st.sb("mt_lo", [HG * G, P], BF16)
        pt = [st.sb(f"pt{k}", [P, HG, S - P * k], F32) for k in range(G)]
        o_raw = st.sb("o_raw", [P, S], F32)
        rec = st.sb("rec0", [P, S], F32)
        oT = st.sb("oT", [P, NG, S], F32)

        EQ = EO // B
        w_next = st.sb("w_next0", [P, 2, KC, EQ], F32)
        b_next = st.sb("b_next", [2, EQ], F32)
        b_part = st.sb("b_part", [2, 3, EQ], BF16)
        quarters = [(w[:, :, :].rearrange("p c (q n) -> p q c n", q=B)) for w in
                    (glob["rw_hi"], glob["rw_lo"], glob["ew_hi"], glob["ew_lo"])]
        b3_q = glob["stage"][:, :, :].rearrange("r m (q n) -> r q m n", q=B)

        load_next, load_b, s_next, s_b3 = st.sem("load_next0"), st.sem("load_b0"), st.sem("next0"), st.sem("b3")
        NEXT = 9
        STACKED = 16 * 8
        x_first, x_rest = st.sem("x_first"), st.sem("x_rest")
        load, load_wo = st.sem("load0"), st.sem("load0_wo")
        const, const_v = st.sem("const0"), st.sem("const0v")
        wsplit_hi, wsplit_lo = st.sem("wsplit0_hi"), st.sem("wsplit0_lo")
        s_stat, s_mv, s_rstd = st.sem("stat0"), st.sem("mv0s"), st.sem("rstd0s")
        s_xn, s_xhi, s_xlo, s_qkhi = st.sem("xn0s"), st.sem("xhi0"), st.sem("xlo0"), st.sem("qkhi")
        s_scr, s_stk = st.sem("scr"), [st.sem(f"stack{g}") for g in range(NG)]
        s_work, s_taken, s_mx = st.sem("bank_work"), st.sem("bank_taken"), st.sem("row_max")
        s_mthi, s_shift = st.sem("mthi"), st.sem("shift")
        s_st, s_exp, s_msk, s_pv = st.sem("scoreT"), st.sem("expd"), st.sem("masked"), st.sem("pv0")
        s_raw, s_den, s_rec, s_oT = st.sem("raw0"), st.sem("den0"), st.sem("rec0s"), st.sem("oT0")

        MAXB, STB, PVB, SELB = (0, 1), (2, 4), 6, 7
        BATCH_WORK = sum(map(len, bank_work(False, False)))

        def bank(n, width=BANK, off=0):
            return ps[:, n * BANK + off:n * BANK + off + width]

        ST_UNITS = [(0, (0, 1)), (0, (2, 3)), (1, (0, 1)), (1, (2, 3)), (2, (0, 1, 2, 3)), (3, (0, 1, 2, 3))]

        def st_col(u, n):
            kt, heads = ST_UNITS[u]
            width = S - P * kt
            per = BANK // width
            return STB[u % 2] * BANK + (n // per) * BANK + (n % per) * width, width

        def schedule(b, first, last):
            n = len(START) if first else len(START) - 2 + BATCH_WORK * b
            odd = len(START) % 2
            for g, work in enumerate(bank_work(first, last)):
                yield g, in_group(work, not (first and g == 0)), n, odd
                n, odd = n + len(work), (odd + len(work)) % 2

        LAST_WORK = len(START) - 2 + BATCH_WORK * (B - 1) + sum(map(len, bank_work(False, True)))
        assert BATCH_WORK % 2 == 0, "a batch's work starts in the same bank"

        def all_batches(eng, batch):
            batch(0, True, False)
            with eng.Fori(1, B - 1) as b:
                batch(b, False, False)
            batch(B - 1, False, True)

        with nc.Block() as block:

            @block.sync
            def _(sp):
                for b in range(B):
                    sp.dma_start(X[:, b, :, :], A["x"][b].rearrange("(g p) d -> p g d", p=P)).then_inc(
                        x_rest if b else x_first, 16)
                    if b:
                        continue
                    sp.dma_start(w_f[:, :, :], A["w_project"].rearrange("(c p) n -> p c n", p=P)).then_inc(load, 16)
                sp.wait_ge(const_v, 1)
                for h in range(HG):
                    sp.dma_start(wo[HB * h:HB * h + HD0, :, :],
                                 A["w_out"].rearrange("(g i d) n -> i d g n", i=HG, d=HD0)[h]).then_inc(load_wo, 16)

                def copy_parts(b, qk_work):
                    for g in range(NG):
                        if not (isinstance(b, int) and b == 0):
                            wait_alone(sp, s_stk[g], STACKED * b, passed_sp)
                    for n, scr in enumerate((scratch_q, scratch_k)):
                        for part, buf in enumerate((qk_hi, qk_lo)):
                            sp.wait_ge(s_taken, qk_work[2 * n + 1] + 1)
                            sp.dma_start(scr[part].rearrange("(m p) t -> p m t", p=P),
                                         buf[:, 2 * n:2 * n + 2, :]).then_inc(s_scr, 16)
                    wait_alone(sp, s_scr, 64 * b + 64, passed_sp)

                def stack_group(b, g):
                    reach(sp, s_st, 6 * (NG * (b - 1) + g + 1))
                    heads = slice(HG * g, HG * (g + 1))
                    for scr, dst, hi_lo_rows in ((scratch_q, qs, ((0, 2), (1, 3))), (scratch_k, ks, ((0, 1), (2, 3)))):
                        for part, rows in enumerate(hi_lo_rows):
                            for r in rows:
                                sp.dma_start(dst[HD0 * r:HD0 * (r + 1), heads, :],
                                             scr[part].rearrange("(h d) t -> d h t", d=HD0)[:, heads, :]
                                             ).then_inc(s_stk[g], 16)

                def shift_group(t, g, turned):
                    for part, (buf, done, count) in enumerate(((mt_hi, s_mthi, t + 1), (mt_lo, s_taken, turned + 1))):
                        sp.wait_ge(done, count)
                        sp.dma_start(
                            qs[SHIFT + part:SHIFT + part + 1, HG * g:HG * (g + 1), :].rearrange(
                                "o h (j q) -> o (h j) q", q=P),
                            buf[:, :]).then_inc(s_shift, 16)

                copy_parts(0, [START.index(("qk", m)) for m in range(4)])
                for g in range(NG):
                    stack_group(0, g)
                shift_group(0, 0, START.index(("turn", 0)))

                def batch(b, first, last):
                    reach(sp, s_next, NEXT * b)
                    for n, name in enumerate(("router_w", "expert_w")):
                        sp.dma_start(w_next[:, n, :, :], A[name].rearrange("(c p) (q n) -> q p c n", p=P, q=B)[b]
                                     ).then_inc(load_next, 16)
                    for n, name in enumerate(("router_b", "expert_b")):
                        sp.dma_start(b_next[n:n + 1, :], A[name].rearrange("o (q n) -> q o n", q=B)[b]
                                     ).then_inc(load_b, 16)
                    for g, order, n, odd in schedule(b, first, last):
                        work = [x for kind, x in order if kind == "work"]
                        if not (last and g == NG - 1):
                            g_next = (g + 1) % NG
                            shift_group(NG * b + g + 1, g_next, n + work.index(("turn", g_next)))
                        if not last:
                            if g == 0:
                                copy_parts(b + 1, [n + work.index(("qk", m)) for m in range(4)])
                            stack_group(b + 1, g)
                    wait_alone(sp, s_next, NEXT * b + NEXT, passed_sp)
                    for part in range(3):
                        for m in range(2):
                            sp.dma_start(b3_q[part:part + 1, b, m, :], b_part[m:m + 1, part, :]).then_inc(s_b3, 16)

                all_batches(sp, batch)
                sp.wait_ge(s_b3, 96 * B)

            @block.gpsimd
            def _(pool):
                pool.memset(half[:, :], -0.5).then_inc(const, 1)
                pool.memset(maskneg[:, :], 0.0).then_inc(const, 1)
                pool.memset(sel[:, :], 0.0).then_inc(const, 1)
                pool.wait_ge(const, 3)
                pool.affine_select(out=maskneg[:, :], in_=maskneg[:, :], compare_op=ALU.is_ge, fill=NEG, base=0,
                                   pattern=[[-1, P]], channel_multiplier=1).then_inc(const, 1)
                pool.affine_select(out=sel[:, :].rearrange("p (h r) -> p h r", r=HB),
                                   in_=sel[:, :].rearrange("p (h r) -> p h r", r=HB),
                                   compare_op=ALU.not_equal, fill=1.0, base=-HD0,
                                   pattern=[[-HB, HG], [0, HB]], channel_multiplier=1).then_inc(const, 1)

                def split_next(b):
                    def after(n, ins):
                        def piece():
                            if n is not None:
                                wait_alone(pool, s_next, NEXT * b + n, passed_pool)
                            ins().then_inc(s_next, 1)
                        return piece
                    r_hi, r_lo, e_hi, e_lo = (q[:, b] for q in quarters)

                    def first():
                        wait_alone(pool, load_next, 32 * b + 32, passed_pool)
                        pool.tensor_copy(r_hi, w_next[:, 0, :, :]).then_inc(s_next, 1)

                    def first_bias():
                        wait_alone(pool, load_b, 32 * b + 32, passed_pool)
                        if not (isinstance(b, int) and b == 0):
                            wait_alone(pool, s_b3, 96 * b, passed_pool)
                        pool.tensor_copy(b_part[:, 0, :], b_next[:, :]).then_inc(s_next, 1)
                    return [
                        first,
                        after(None, lambda: pool.tensor_copy(e_hi, w_next[:, 1, :, :])),
                        first_bias,
                        after(1, lambda: pool.tensor_tensor(r_lo, w_next[:, 0, :, :], r_hi.bitcast(F32), ALU.subtract)),
                        after(2, lambda: pool.tensor_tensor(e_lo, w_next[:, 1, :, :], e_hi, ALU.subtract)),
                        after(3, lambda: pool.tensor_tensor(b_next[:, :], b_next[:, :], b_part[:, 0, :], ALU.subtract)),
                        after(6, lambda: pool.tensor_copy(b_part[:, 1, :], b_next[:, :])),
                        after(7, lambda: pool.tensor_tensor(b_next[:, :], b_next[:, :], b_part[:, 1, :], ALU.subtract)),
                        after(8, lambda: pool.tensor_copy(b_part[:, 2, :], b_next[:, :])),
                    ]

                def root(b):
                    wait_alone(pool, s_mv, G * b + G, passed_pool)
                    pool.tensor_scalar(rstd[:, :], mv[:, :, 1], EPS, None, ALU.add).then_inc(s_rstd, 1)
                    wait_alone(pool, s_rstd, 2 * b + 1, passed_pool)
                    pool.tensor_tensor(rstd[:, :], rstd[:, :], half[:, :], ALU.pow).then_inc(s_rstd, 1)

                root(0)
                pool.wait_ge(s_rstd, 2)
                pool.memset(ks[SHIFT:SHIFT + 2, :, :], 1.0).then_inc(const, 1)
                pool.wait_ge(const, 6)
                pool.memset(ks[STK:SHIFT, :, :], 0.0).then_inc(const, 1)
                pool.wait_ge(const, 7)
                pool.memset(qs[STK:SHIFT, :, :], 0.0).then_inc(const, 1)

                def batch(b, first, last):
                    more = work_between(split_next(b))
                    if not last:
                        root(b + 1)
                    for g in range(NG):
                        for u, (kt, heads) in enumerate(ST_UNITS):
                            wait_alone(pool, s_exp, 6 * (NG * b + g) + u + 1, passed_pool)
                            t = pt[kt][:, heads[0]:heads[-1] + 1, 0:P]
                            pool.affine_select(out=t, in_=t, compare_op=ALU.is_ge, fill=0.0, base=0,
                                               pattern=[[0, len(heads)], [1, P]],
                                               channel_multiplier=-1).then_inc(s_msk, 1)
                            if g and u % 2:
                                more()

                all_batches(pool, batch)

            @block.tensor
            def _(pe):
                pe.wait_ge(wsplit_hi, 1)
                pe.wait_ge(wsplit_lo, 1)
                pe.wait_ge(const, 5)
                pe.wait_ge(const_v, 3)
                pe.wait_ge(load_wo, 16 * HG)

                def three(out, lhs, rhs):
                    n = 0
                    for c in range(KC):
                        for a, b_ in ((0, 0), (0, 1), (1, 0)):
                            mm = pe.matmul(out, lhs[a](c), rhs[b_](c), start=(n == 0), stop=(n == 3 * KC - 1))
                            n += 1
                    return mm

                def x_transposed(b, c, out):
                    pe.wait_ge(s_xn, G * b + G)
                    for g in range(G):
                        mm = pe.transpose(out(P, P * g), xn[:, g, P * c:P * (c + 1)], ident[:, :])
                    return mm

                def queries_keys(b, m, out):
                    pe.wait_ge(s_xhi, 2 * b + 2)
                    pe.wait_ge(s_xlo, 2 * b + 2)
                    return three(out(), [lambda c: w_hi[:, c, P * m:P * (m + 1)], lambda c: w_lo[:, c, P * m:P * (m + 1)]],
                                 [lambda c: xT_hi[:, c, :], lambda c: xT_lo[:, c, :]])

                def value_rows(half_, out):
                    for t in (2 * half_, 2 * half_ + 1):
                        mm = three(out(D, D * (t % 2)),
                                   [lambda c: xT_hi[:, c, P * t:P * (t + 1)], lambda c: xT_lo[:, c, P * t:P * (t + 1)]],
                                   [lambda c: w_hi[:, c, 2 * D:], lambda c: w_lo[:, c, 2 * D:]])
                    return mm

                def max_scores(b, g, i, o):
                    if i == 0:
                        pe.wait_ge(s_stk[g], STACKED * (b + 1))
                    blocks = max_units(2 * g + i // 5)[i % 5]
                    i = 0
                    while i < 4:
                        h, j, k0 = blocks[i]
                        w = 1
                        while i + w < 4 and blocks[i + w][:2] == (h, j):
                            w += 1
                        pe.matmul(ps[:, o + P * i:o + P * (i + w)], qs[0:SHIFT, h, P * j:P * (j + 1)],
                                  ks[0:SHIFT, h, P * k0:P * (k0 + w)], start=(i == 0), stop=False, skip_group_check=True)
                        i += w
                        mm = pe.matmul(ps[:, o + P * (i - 1):o + P * i], identb[:, :], maskneg[:, :],
                                       start=False, stop=(i == 4), skip_group_check=True)
                    return mm

                def projection(b, half_, out):
                    pe.wait_ge(s_oT, NG * b + NG)
                    for t in (2 * half_, 2 * half_ + 1):
                        for g in range(NG):
                            mm = pe.matmul(out(D, D * (t % 2)), oT[:, g, P * t:P * (t + 1)], wo[:, g, :],
                                           start=(g == 0), stop=(g == NG - 1))
                    return mm

                def turn_max(t, g, out):
                    pe.wait_ge(s_mx, t + 1)
                    return pe.transpose(out(P)[0:HG * G, :],
                                        mx[:, HG * g:HG * (g + 1), :].rearrange("p h j -> p (h j)"), ident[:, :])

                def work(b, n, parity, kind, arg, ahead, t_next=0):
                    reach(pe, s_taken, n - 1)

                    def out(width=BANK, off=0):
                        return bank(MAXB[parity], width, off)
                    mm = {
                        "xT": lambda: x_transposed(ahead, arg, out),
                        "qk": lambda: queries_keys(ahead, arg, out),
                        "v": lambda: value_rows(arg, out),
                        "max": lambda: max_scores(b if arg[0] >= 2 else ahead, arg[0], arg[1], MAXB[parity] * BANK),
                        "turn": lambda: turn_max(t_next, arg, out),
                        "proj": lambda: projection(b - 1, arg, out),
                    }[kind]()
                    mm.then_inc(s_work, 1)

                def score_unit(b, g, u, first):
                    kt, heads = ST_UNITS[u]
                    t = NG * b + g
                    if u == 0:
                        pe.wait_ge(s_shift, 32 * t + 32)
                    reach(pe, s_exp, 6 * t + u - 1)
                    for i, h in enumerate(heads):
                        c, w = st_col(u, i)
                        h += HG * g
                        mm = pe.matmul(ps[:, c:c + w], ks[:, h, P * kt:P * (kt + 1)], qs[:, h, P * kt:],
                                       start=True, stop=True, skip_group_check=True)
                    mm.then_inc(s_st, 1)

                def values(b, g, kt, values_taken):
                    t = NG * b + g
                    pe.wait_ge(s_msk, 6 * t + (2, 4, 5, 6)[kt])
                    if kt == 0:
                        reach(pe, s_raw, t)
                        if g == 0:
                            pe.wait_ge(s_taken, values_taken)
                    for h in range(HG):
                        mm = pe.matmul(ps[HB * h:HB * (h + 1), PVB * BANK + P * kt:(PVB + 1) * BANK],
                                       v[:, kt, HG * g + h, :], pt[kt][:, h, :],
                                       start=(kt == 0), stop=(kt == G - 1), skip_group_check=True)
                    mm.then_inc(s_pv, 1)

                def denominators(t):
                    pe.wait_ge(s_raw, t + 1)
                    reach(pe, s_rec, G * t)
                    pe.matmul(bank(SELB), sel[:, :], o_raw[:, :], start=True, stop=True).then_inc(s_den, 1)

                for n, (kind, arg) in enumerate(START):
                    if n == len(PREPARE):
                        pe.wait_ge(const, 8)
                    work(0, n, n % 2, kind, arg, 0)

                def batch(b, first, last):
                    for g, order, n, odd in schedule(b, first, last):
                        t, i, first_n = NG * b + g, 0, n
                        for kind, arg in order:
                            if kind == "score":
                                score_unit(b, g, arg, first)
                            elif kind == "den":
                                denominators(t - 1)
                            elif kind == "values":
                                values(b, g, arg, first_n + 2)
                            elif kind == "work":
                                work(b, n + i, (odd + i) % 2, *arg, b + 1, t + 1)
                                i += 1

                all_batches(pe, batch)
                denominators(NG * B - 1)
                for t in range(2):
                    work(B, LAST_WORK + t, (LAST_WORK + t) % 2, "proj", t, None)

            @block.scalar
            def _(act):
                act.wait_ge(load, 16)
                act.activation(w_hi[:, :, :], w_f[:, :, :], ACT.Copy).then_inc(wsplit_hi, 1)
                act.wait_ge(const_v, 3)
                def take(b, n, parity, kind, arg):
                    if kind == "xT":
                        act.wait_ge(s_work, n + 1)
                        act.activation(xT_hi[:, arg, :], bank(MAXB[parity]), ACT.Copy).then_inc(s_xhi, 1)
                    if kind == "qk":
                        act.wait_ge(s_work, n + 1)
                        reach(act, s_scr, 64 * b)
                        act.activation(qk_hi[:, arg, :], bank(MAXB[parity]), ACT.Copy,
                                       scale=(HD0 ** -0.5 if arg < 2 else 1.0)).then_inc(s_qkhi, 1)

                for n, (kind, arg) in enumerate(START):
                    take(0, n, n % 2, kind, arg)

                def exponentials(b, g, u):
                    t, (kt, heads) = NG * b + g, ST_UNITS[u]
                    act.wait_ge(s_st, 6 * t + u + 1)
                    reach(act, s_pv, G * (t - 1) + kt + 1)
                    c, w = st_col(u, 0)
                    per = BANK // w
                    src = ps[:, c:c + len(heads) // per * BANK].rearrange(
                        "p (h q) -> p h q", h=len(heads))[:, :, 0:w]
                    act.activation(pt[kt][:, heads[0]:heads[-1] + 1, :], src, ACT.Exp).then_inc(s_exp, 1)

                def batch(b, first, last):
                    for g, order, n, odd in schedule(b, first, last):
                        i = 0
                        for kind, arg in order:
                            if kind == "score":
                                exponentials(b, g, arg)
                            elif kind == "work":
                                take(b + 1, n + i, (odd + i) % 2, *arg)
                                i += 1
                        t = NG * b + g
                        act.wait_ge(s_pv, G * t + G)
                        reach(act, s_oT, t)
                        act.activation(o_raw[:, :], bank(PVB), ACT.Copy).then_inc(s_raw, 1)

                all_batches(act, batch)

            @block.vector
            def _(dve):
                def statistics(b):
                    dve.wait_ge(*((x_first, 16) if isinstance(b, int) and b == 0 else (x_rest, 16 * (B - 1))))
                    for g in range(G):
                        dve.bn_stats(stats[:, g, :], X[:, b, g, :]).then_inc(s_stat, 1)
                    for g in range(G):
                        wait_alone(dve, s_stat, G * b + g + 1, passed_dve)
                        dve.bn_aggr(mv[:, g, :], stats[:, g, :]).then_inc(s_mv, 1)

                dve.memset(wo[:, :, :], 0.0).then_inc(const_v, 1)
                dve.memset(v[:, :, :, :], 0.0).then_inc(const_v, 1)
                dve.wait_ge(const_v, 2)
                dve.memset(v[:, :, :, HD0:HD0 + 1], 1.0).then_inc(const_v, 1)
                statistics(0)
                dve.wait_ge(load, 16)
                dve.wait_ge(wsplit_hi, 1)
                dve.tensor_tensor(w_lo[:, :, :], w_f[:, :, :], w_hi[:, :, :], ALU.subtract).then_inc(wsplit_lo, 1)

                def normalised(b):
                    dve.wait_ge(s_rstd, 2 * b + 2)
                    for g in range(G):
                        dve.tensor_scalar(xn[:, g, :], X[:, b, g, :], mv[:, g, 0:1], rstd[:, g:g + 1],
                                          ALU.subtract, ALU.mult).then_inc(s_xn, 1)

                def take(b, n, parity, kind, arg, ahead, t_next=0):
                    src = bank(MAXB[parity])
                    if kind == "xT":
                        dve.wait_ge(s_xhi, 2 * ahead + arg + 1)
                        ins = dve.tensor_tensor(xT_lo[:, arg, :], src, xT_hi[:, arg, :], ALU.subtract)
                    elif kind == "qk":
                        dve.wait_ge(s_qkhi, 4 * ahead + arg + 1)
                        reach(dve, s_scr, 64 * ahead)
                        ins = dve.scalar_tensor_tensor(qk_lo[:, arg, :], src, (HD0 ** -0.5 if arg < 2 else 1.0),
                                                       qk_hi[:, arg, :], ALU.mult, ALU.subtract)
                    elif kind == "v":
                        dve.wait_ge(s_work, n + 1)
                        ins = dve.tensor_copy(v[:, 2 * arg:2 * arg + 2, :, 0:HD0],
                                              src.rearrange("p (t h d) -> p t h d", t=2, d=HD0))
                    elif kind == "turn":
                        dve.wait_ge(s_work, n + 1)
                        reach(dve, s_shift, 32 * t_next)
                        dve.tensor_scalar(mt_hi[:, :], src[0:HG * G, 0:P], -1.0, None, ALU.mult).then_inc(s_mthi, 1)
                        dve.wait_ge(s_mthi, t_next + 1)
                        ins = dve.scalar_tensor_tensor(mt_lo[:, :], src[0:HG * G, 0:P], -1.0, mt_hi[:, :], ALU.mult,
                                                       ALU.subtract)
                    elif kind == "proj":
                        dve.wait_ge(s_work, n + 1)
                        xr = X[:, b - 1, 2 * arg:2 * arg + 2, :]
                        ins = dve.tensor_tensor(xr, src.rearrange("p (t n) -> p t n", t=2), xr, ALU.add)
                    else:
                        g, i = arg
                        dve.wait_ge(s_work, n + 1)
                        ins = dve.tensor_reduce(bm[:, 2 * g + i // 5, 4 * (i % 5):4 * (i % 5) + 4],
                                                src.rearrange("p (k q) -> p k q", k=4), AX_X, ALU.max)
                    ins.then_inc(s_taken, 1)
                    if kind == "xT":
                        dve.wait_ge(s_taken, n + 1)
                        dve.sem_inc(s_xlo, 1)
                    if kind == "max" and arg[1] == 9:
                        row_max(arg[0], n)

                def row_max(g, n):
                    pr = slice(2 * g, 2 * g + 2)
                    dve.wait_ge(s_taken, n + 1)
                    m4 = mx[:, HG * g:HG * (g + 1), :].rearrange("p (r h) j -> p r h j", h=2)
                    dve.tensor_reduce(m4[:, :, :, 3], bm[:, pr, 0:8].rearrange("p r (h k) -> p r h k", h=2), AX_X, ALU.max)
                    dve.tensor_reduce(m4[:, :, :, 2], bm[:, pr, 8:16].rearrange("p r (h k) -> p r h k", h=2)[:, :, :, 0:3],
                                      AX_X, ALU.max)
                    dve.tensor_reduce(m4[:, :, :, 1], bm[:, pr, 16:20].rearrange("p r (h k) -> p r h k", h=2), AX_X, ALU.max)
                    dve.tensor_copy(m4[:, :, :, 0], bm[:, pr, 8:16].rearrange("p r (h k) -> p r h k", h=2)[:, :, :, 3])\
                       .then_inc(s_mx, 1)

                def normalise(t, g, q):
                    dve.wait_ge(s_den, t + 1)
                    dve.reciprocal(rec[:, P * q:P * (q + 1)], bank(SELB, P, P * q)).then_inc(s_rec, 1)
                    if q == G - 1:
                        dve.wait_ge(s_rec, G * (t + 1))
                        dve.tensor_tensor(oT[:, g, :], o_raw[:, :], rec[:, :], ALU.mult).then_inc(s_oT, 1)

                normalised(0)
                for n, (kind, arg) in enumerate(START):
                    take(0, n, n % 2, kind, arg, 0)

                def batch(b, first, last):
                    if not last:
                        statistics(b + 1)
                    for g, order, n, odd in schedule(b, first, last):
                        i = 0
                        for kind, arg in order:
                            if kind == "norm":
                                normalise(NG * b + g - 1, (g - 1) % NG, arg)
                            elif kind == "work":
                                take(b, n + i, (odd + i) % 2, *arg, b + 1, NG * b + g + 1)
                                i += 1
                                if g == 0 and i == 4 and not last:
                                    normalised(b + 1)

                all_batches(dve, batch)
                for q in range(G):
                    normalise(NG * B - 1, NG - 1, q)
                for t in range(2):
                    take(B, LAST_WORK + t, (LAST_WORK + t) % 2, "proj", t, None)


NU = EO // BANK
CAP = 60.0


def normalise_ops(b_of, dve, X, stats, mv, rstd, xn, s_stat, s_mv, s_rstd, s_xn, i, passed):
    for j in range(4):
        dve.bn_stats(stats[:, j, :], b_of(j)).then_inc(s_stat, 1)
    for j in range(4):
        wait_alone(dve, s_stat, 4 * i + j + 1, passed)
        dve.bn_aggr(mv[:, j, :], stats[:, j, :]).then_inc(s_mv, 1)
    dve.wait_ge(s_rstd, 2 * i + 2)
    for j in range(4):
        dve.tensor_scalar(xn[:, j, :], b_of(j), mv[:, j, 0:1], rstd[:, j:j + 1],
                          ALU.subtract, ALU.mult).then_inc(s_xn, 1)


def rstd_ops(pool, mv, rstd, half, s_mv, s_rstd, i, passed):
    wait_alone(pool, s_mv, 4 * i + 4, passed)
    pool.tensor_scalar(rstd[:, :], mv[:, :, 1], EPS, None, ALU.add).then_inc(s_rstd, 1)
    wait_alone(pool, s_rstd, 2 * i + 1, passed)
    pool.tensor_tensor(rstd[:, :], rstd[:, :], half[:, :], ALU.pow).then_inc(s_rstd, 1)


def layer0_mixture(nc, glob, A):
    X, ps, ident = glob["X"], glob["ps"], glob["ident"]
    passed_dve, passed_pool, passed_sp = glob["passed"]
    with ExitStack() as stack:
        st = Store(nc, stack)
        rw_hi, rw_lo, ew_hi, ew_lo = (glob[n] for n in ("rw_hi", "rw_lo", "ew_hi", "ew_lo"))
        b3 = glob["stage"][0:3, :, :]
        q_next = st.sb("q_next", [P, KC, NW // B], F32)
        p_next = st.sb("p_next", [P, H1 // B, D], F32)
        wq_q = [w[:, :, :].rearrange("p c (q n) -> p q c n", q=B) for w in (glob["wq_hi"], glob["wq_lo"])]
        wp_q = [w[:, :, :].rearrange("p (q h) n -> p q h n", q=B) for w in (glob["wp_hi"], glob["wp_lo"])]
        ones3 = st.sb("ones3", [3, P], BF16)
        code = st.sb("code", [P, E], I32)
        stats = st.sb("stats1", [P, 4, 6], F32)
        mv = st.sb("mv1", [P, 4, 2], F32)
        rstd = st.sb("rstd1", [P, 4], F32)
        half = st.sb("half1", [P, 4], F32)
        xn = st.sb("xn1", [P, 4, D], F32)
        xr_hi = st.sb("xr_hi", [P, KC, S], F32R)
        xr_lo = st.sb("xr_lo", [P, KC, S], F32R)
        xb_hi = st.sb("xb_hi", [P, KC, S], BF16)
        xb_lo = st.sb("xb_lo", [P, KC, S], BF16)
        lg = [st.sb(f"lg{n}", [P, E, D], F32) for n in range(2)]
        tmp = st.sb("tmp", [P, E, D], F32)
        s4, h4 = st.sb("s4", [P, 4, D], F32), st.sb("h4", [P, 4, D], F32)
        h2, a2, c2 = (st.sb(n, [P, 2, D], F32) for n in ("h2", "a2", "c2"))
        m1, m2, n1, c1 = (st.sb(n, [P, D], F32) for n in ("m1", "m2", "n1", "c1"))
        e1 = st.sb("e1", [P, D], F32)
        cw = [st.sb(f"cw{n}", [P, E], F32) for n in range(2)]

        load_next, s_next, const = st.sem("load_next1"), st.sem("next1"), st.sem("const1")
        NEXT = 4
        s_stat, s_mv, s_rstd = st.sem("stat1"), st.sem("mv1s"), st.sem("rstd1s")
        s_xn, s_tp, s_xhi, s_xlo = st.sem("xn1s"), st.sem("tp1"), st.sem("xhi1"), st.sem("xlo1")
        s_rt, s_lg, s_dve, s_z, s_ez = st.sem("router"), st.sem("logits"), st.sem("topk"), st.sem("zdist"), st.sem("zexp")
        s_c, s_u = st.sem("cweights"), st.sem("experts")

        def bank(n, width=BANK, off=0):
            return ps[:, n * BANK + off:n * BANK + off + width]

        def over_experts(a):
            return a[:, :].rearrange("p (o n) -> p o n", o=1).to_broadcast([P, E, D])

        TOP, DIST, WEIGHED, DONE = 13, 15, 18, 26

        with nc.Block() as block:

            @block.sync
            def _(sp):
                with sp.Fori(0, B) as b:
                    reach(sp, s_next, NEXT * b)
                    sp.dma_start(q_next[:, :, :], A["w_qkv"].rearrange("(c p) (q n) -> q p c n", p=P, q=B)[b]
                                 ).then_inc(load_next, 16)
                    sp.dma_start(p_next[:, :, :], A["w_proj"].rearrange("(q h p) n -> q p h n", p=P, q=B)[b]
                                 ).then_inc(load_next, 16)

            @block.gpsimd
            def _(pool):
                pool.memset(half[:, :], -0.5).then_inc(const, 1)
                pool.memset(ones3[:, :], 1.0).then_inc(const, 1)
                pool.iota(code[:, :], pattern=[[-1, E]], base=E - 1, channel_multiplier=0).then_inc(const, 1)
                with pool.Fori(0, B) as b:
                    rstd_ops(pool, mv, rstd, half, s_mv, s_rstd, b, passed_pool)
                    wait_alone(pool, load_next, 32 * b + 32, passed_pool)
                    pool.tensor_copy(wq_q[0][:, b], q_next[:, :, :]).then_inc(s_next, 1)
                    pool.tensor_copy(wp_q[0][:, b], p_next[:, :, :]).then_inc(s_next, 1)
                    wait_alone(pool, s_next, NEXT * b + 1, passed_pool)
                    pool.tensor_tensor(wq_q[1][:, b], q_next[:, :, :], wq_q[0][:, b], ALU.subtract).then_inc(s_next, 1)
                    wait_alone(pool, s_next, NEXT * b + 2, passed_pool)
                    pool.tensor_tensor(wp_q[1][:, b], p_next[:, :, :], wp_q[0][:, b], ALU.subtract).then_inc(s_next, 1)

            @block.tensor
            def _(pe):
                pe.wait_ge(const, 3)

                def products(out, x_hi, x_lo, w_hi, w_lo, t, cols, bias):
                    pe.matmul(out, ones3[:, :], bias, start=True, stop=False)
                    tok = slice(P * t, P * (t + 1))
                    for c in range(KC):
                        pe.matmul(out, x_hi[:, c, tok], w_hi[:, c, cols], start=False, stop=False)
                        pe.matmul(out, x_hi[:, c, tok], w_lo[:, c, cols], start=False, stop=False)
                        mm = pe.matmul(out, x_lo[:, c, tok], w_hi[:, c, cols], start=False, stop=(c == KC - 1))
                    return mm

                def router(b, t):
                    for u in range(NU):
                        reach(pe, s_lg, NU * (4 * b + t - 1) + u + 1 if t else NU * 4 * b)
                        cols = slice(BANK * u, BANK * (u + 1))
                        products(bank(u), xr_hi, xr_lo, rw_hi, rw_lo, t, cols, b3[:, 0, cols]).then_inc(s_rt, 1)

                def experts(b, t):
                    for u in range(NU):
                        reach(pe, s_c, E * (4 * b + t - 1) + 2 * (u + 1) if t else E * 4 * b)
                        cols = slice(BANK * u, BANK * (u + 1))
                        products(bank(4 + u), xb_hi, xb_lo, ew_hi, ew_lo, t, cols, b3[:, 1, cols]).then_inc(s_u, 1)

                with pe.Fori(0, B) as b:
                    pe.wait_ge(s_xn, 4 * b + 4)
                    reach(pe, s_lg, NU * 4 * b)
                    for c in range(KC):
                        for t in range(4):
                            tr = pe.transpose(bank(c, P, P * t), xn[:, t, P * c:P * (c + 1)], ident[:, :])
                        tr.then_inc(s_tp, 1)
                    pe.wait_ge(s_xhi, 4 * b + 4)
                    pe.wait_ge(s_xlo, 4 * b + 4)
                    for t in range(4):
                        router(b, t)
                        experts(b, t)

            @block.scalar
            def _(act):
                with act.Fori(0, B) as b:
                    for c in range(KC):
                        act.wait_ge(s_tp, 2 * b + c + 1)
                        act.activation(xr_hi[:, c, :], bank(c), ACT.Copy).then_inc(s_xhi, 1)
                        act.activation(xb_hi[:, c, :], bank(c), ACT.Copy).then_inc(s_xhi, 1)
                    for t in range(4):
                        n = 4 * b + t
                        for u in range(NU):
                            act.wait_ge(s_rt, NU * n + u + 1)
                            if u == 0:
                                reach(act, s_dve, DONE * (n - 1) if t else DONE * 4 * b)
                            act.activation(lg[t % 2][:, 2 * u:2 * u + 2, :],
                                           bank(u).rearrange("p (e o) -> p e o", e=2), ACT.Copy).then_inc(s_lg, 1)
                        act.wait_ge(s_dve, DONE * n + DIST)
                        act.activation(lg[t % 2][:, :, :], tmp[:, :, :], ACT.Exp).then_inc(s_ez, 1)
                        act.activation(e1[:, :], n1[:, :], ACT.Exp).then_inc(s_ez, 1)

            @block.vector
            def _(dve):
                dve.wait_ge(const, 3)

                with dve.Fori(0, B) as b:
                    normalise_ops(lambda j: X[:, b, j, :], dve, X, stats, mv, rstd, xn,
                                  s_stat, s_mv, s_rstd, s_xn, b, passed_dve)
                    for c in range(KC):
                        dve.wait_ge(s_xhi, 4 * b + 2 * c + 2)
                        dve.tensor_tensor(xr_lo[:, c, :], bank(c), xr_hi[:, c, :].bitcast(F32), ALU.subtract).then_inc(s_xlo, 1)
                        dve.tensor_tensor(xb_lo[:, c, :], bank(c), xb_hi[:, c, :], ALU.subtract).then_inc(s_xlo, 1)
                    for t in range(4):
                        n = 4 * b + t
                        L, c_t = lg[t % 2], cw[t % 2]
                        Li, Ti = L[:, :, :].bitcast(I32), tmp[:, :, :].bitcast(I32)
                        done = [0]

                        def step(ins):
                            done[0] += 1
                            ins.then_inc(s_dve, 1)
                            dve.wait_ge(s_dve, DONE * n + done[0])

                        def free(ins):
                            done[0] += 1
                            ins.then_inc(s_dve, 1)

                        dve.wait_ge(s_lg, NU * n + NU)
                        free(dve.scalar_tensor_tensor(
                            Ti, Li, 31, code[:, :].rearrange("p (e o) -> p e o", o=1).to_broadcast([P, E, D]),
                            ALU.arith_shift_right, ALU.bitwise_xor))
                        step(dve.tensor_scalar(Li, Li, -8, None, ALU.bitwise_and))
                        step(dve.scalar_tensor_tensor(Li, Ti, 7, Li, ALU.bitwise_and, ALU.bitwise_or))
                        free(dve.tensor_tensor(h4[:, :, :], L[:, 0:4, :], L[:, 4:8, :], ALU.max))
                        step(dve.tensor_tensor(s4[:, :, :], L[:, 0:4, :], L[:, 4:8, :], ALU.min))
                        free(dve.tensor_tensor(h2[:, :, :], h4[:, 0:2, :], h4[:, 2:4, :], ALU.max))
                        free(dve.tensor_tensor(a2[:, :, :], h4[:, 0:2, :], h4[:, 2:4, :], ALU.min))
                        step(dve.tensor_tensor(c2[:, :, :], s4[:, 0:2, :], s4[:, 2:4, :], ALU.max))
                        step(dve.tensor_tensor(a2[:, :, :], a2[:, :, :], c2[:, :, :], ALU.max))
                        free(dve.tensor_tensor(m1[:, :], h2[:, 0, :], h2[:, 1, :], ALU.max))
                        free(dve.tensor_tensor(n1[:, :], h2[:, 0, :], h2[:, 1, :], ALU.min))
                        step(dve.tensor_tensor(c1[:, :], a2[:, 0, :], a2[:, 1, :], ALU.max))
                        step(dve.tensor_tensor(m2[:, :], n1[:, :], c1[:, :], ALU.max))
                        assert done[0] == TOP
                        step(dve.scalar_tensor_tensor(m2[:, :], m1[:, :], -CAP, m2[:, :], ALU.add, ALU.max))
                        dve.tensor_tensor(n1[:, :], m1[:, :], m2[:, :], ALU.subtract)
                        free(dve.tensor_tensor(tmp[:, :, :], L[:, :, :], over_experts(m2), ALU.subtract))
                        assert done[0] == DIST
                        dve.wait_ge(s_ez, 2 * n + 2)
                        step(dve.tensor_scalar(e1[:, :], e1[:, :], 1.0, None, ALU.add))
                        free(dve.reciprocal(n1[:, :], e1[:, :]))
                        step(dve.scalar_tensor_tensor(L[:, :, :], tmp[:, :, :], 0.0, L[:, :, :], ALU.is_ge, ALU.mult))
                        assert done[0] == WEIGHED
                        for e in range(E):
                            free(dve.tensor_tensor_reduce(out=tmp[:, e, :], in0=L[:, e, :], in1=n1[:, :], scale=1.0,
                                                          scalar=0.0, op0=ALU.mult, op1=ALU.add,
                                                          accum_out=c_t[:, e:e + 1]))
                        assert done[0] == DONE
                        dve.wait_ge(s_dve, DONE * n + DONE)
                        for u in range(NU):
                            dve.wait_ge(s_u, NU * n + u + 1)
                            for e in (0, 1):
                                x = X[:, b, t, :]
                                dve.scalar_tensor_tensor(x, bank(4 + u, D, D * e), c_t[:, 2 * u + e:2 * u + e + 1], x,
                                                         ALU.mult, ALU.add).then_inc(s_c, 1)
                                dve.wait_ge(s_c, E * n + 2 * u + e + 1)


T8 = 32
OC = 4
NB = S // P
SCALE1 = HD1 ** -0.5


def layer1_attention(nc, glob, A):
    X, ps, ident = glob["X"], glob["ps"], glob["ident"]
    passed_dve, passed_pool, passed_sp = glob["passed"]
    with ExitStack() as stack:
        st = Store(nc, stack)
        wq_hi, wq_lo, wp_hi, wp_lo = (glob[n] for n in ("wq_hi", "wq_lo", "wp_hi", "wp_lo"))
        stats = st.sb("stats2", [P, 4, 6], F32)
        mv = st.sb("mv2", [P, 4, 2], F32)
        rstd = st.sb("rstd2", [P, 4], F32)
        half = st.sb("half2", [P, 4], F32)
        xn = st.sb("xn2", [P, 4, D], F32)
        xT_hi = st.sb("xT2_hi", [P, KC, S], BF16)
        xT_lo = st.sb("xT2_lo", [P, KC, S], BF16)
        qk_hi = st.sb("qk1_hi", [P, KV, HQ + 1, S], BF16)
        qk_lo = st.sb("qk1_lo", [P, KV, HQ + 1, S], BF16)
        v = st.sb("v1", [P, NB, KV, HD1], F32)
        mask = st.sb("mask1", [P, T8], F32)
        sc = [st.sb(f"sc{n}", [P, H1, T8], F32) for n in range(2)]
        mx = [st.sb(f"mx1_{n}", [P, H1], F32) for n in range(2)]
        sm = [st.sb(f"sm1_{n}", [P, H1], F32) for n in range(2)]
        pT = [glob[n][:, :, :].rearrange("p c n -> p (c n)").bitcast(F32).rearrange("p (k o n) -> p k o n", k=KV, o=OC)
              for n in ("ew_hi", "ew_lo")]
        oT_hi = st.sb("oT1_hi", [P, H1, S], BF16)
        oT_lo = st.sb("oT1_lo", [P, H1, S], BF16)
        dq = Dequant(st, glob["stage"], passed_sp, "gu")
        UNITS = [(name, k) for k in range(NC // G) for name in ("gate", "up")]
        NU2 = len(UNITS)

        def unit_of(name, g, k, a):
            return a.rearrange("x (g k n) -> g k x n", g=G, n=UC)[g, k]

        def made_of(name, g, k, part):
            return glob[f"{name}_{part}"][:, :, :].rearrange("p c (g k n) -> p g k c n", g=G, n=UC)[:, g, k]

        def unit_pieces(dve, g, units):
            for i in units:
                name, k = UNITS[i]
                yield from dq.pieces(dve, NU2 * g + i, i % 2, NU2 // 2 * g + i // 2,
                                     made_of(name, g, k, "lo"), made_of(name, g, k, "hi"))

        def unit_high(act, g, i):
            dq.make_high(act, NU2 * g + i, made_of(*UNITS[i][:1], g, UNITS[i][1], "hi"))

        const, const_v = st.sem("const2"), st.sem("const2v")
        s_stat, s_mv, s_rstd = st.sem("stat2"), st.sem("mv2s"), st.sem("rstd2s")
        s_xn, s_tp, s_xhi, s_xlo = st.sem("xn2s"), st.sem("tp2"), st.sem("xhi2"), st.sem("xlo2")
        s_qk, s_qkhi, s_qklo = st.sem("qk1"), st.sem("qk1hi"), st.sem("qk1lo")
        s_v, s_vev, s_sc, s_sma, s_smb, s_ex = (
            st.sem(n) for n in ("v1s", "v1ev", "sc1", "shifted1", "softmax1", "exp1"))
        s_pv, s_ohi, s_olo, s_out, s_res = (st.sem(n) for n in ("pv1", "o1hi", "o1lo", "out1", "res1"))
        NM = KV * (HQ + 1)
        SMA, SMB = 4, 7
        TURNED, MASKED, MAXED, SHIFTED = 1, 2, 3, SMA

        def bank(n, width=BANK, off=0):
            return ps[:, n * BANK + off:n * BANK + off + width]

        def o_tile(a, j, k):
            return a[:, HQ * k:HQ * (k + 1), :].rearrange("p h (b t) -> p (h b) t", b=B)[:, :, T8 * j:T8 * (j + 1)]

        with nc.Block() as block:

            @block.sync
            def _(sp):
                def fetch(g, units):
                    for i in units:
                        name, k = UNITS[i]
                        dq.fetch(sp, NU2 * g + i, i % 2, unit_of(name, g, k, A[f"{name}_W"]), unit_of(name, g, k, A[f"{name}_s"]))
                fetch(0, range(NU2))
                with sp.Fori(1, G) as g:
                    fetch(g, range(NU2))

            @block.gpsimd
            def _(pool):
                pool.memset(half[:, :], -0.5).then_inc(const, 1)
                pool.memset(mask[:, :], -1.0e30).then_inc(const, 1)
                for m in range(P // 8):
                    pool.wait_ge(const, 2 + m)
                    mk = mask[:, :].rearrange("p (b q) -> p b q", q=8)
                    pool.affine_select(out=mk, in_=mk, compare_op=ALU.not_equal, fill=0.0, base=-8 * m,
                                       pattern=[[0, 4], [-1, 8]], channel_multiplier=1).then_inc(const, 1)
                with pool.Fori(0, G) as g:
                    rstd_ops(pool, mv, rstd, half, s_mv, s_rstd, g, passed_pool)

            @block.tensor
            def _(pe):
                pe.wait_ge(const, 2 + P // 8)
                pe.wait_ge(const_v, 2)

                def three(out, lhs, rhs, chunks, **kw):
                    n = 0
                    for c in range(chunks):
                        for a, b_ in ((0, 0), (0, 1), (1, 0)):
                            mm = pe.matmul(out, lhs[a](c), rhs[b_](c), start=(n == 0), stop=(n == 3 * chunks - 1), **kw)
                            n += 1
                    return mm

                def turn(g):
                    pe.wait_ge(s_xn, 4 * g + 4)
                    reach(pe, s_res, 2 * g)
                    for c in range(KC):
                        for b in range(B):
                            tr = pe.transpose(bank(4 + c, P, P * b), xn[:, b, P * c:P * (c + 1)], ident[:, :])
                        tr.then_inc(s_tp, 1)

                def queries_keys(g):
                    pe.wait_ge(s_xhi, 2 * g + 2)
                    pe.wait_ge(s_xlo, 2 * g + 2)
                    for m in range(NM):
                        if m >= 4:
                            pe.wait_ge(s_qklo, NM * g + m - 3)
                        else:
                            reach(pe, s_qklo, NM * g)
                        w = GROUP * (m // (HQ + 1)) + HD1 * (m % (HQ + 1))
                        three(bank(4 + m % 4),
                              [lambda c: wq_hi[:, c, w:w + P], lambda c: wq_lo[:, c, w:w + P]],
                              [lambda c: xT_hi[:, c, :], lambda c: xT_lo[:, c, :]], KC).then_inc(s_qk, 1)

                def values(g):
                    pe.wait_ge(s_qklo, NM * g + NM)
                    for j in range(NB):
                        wv = [w[:, :, :].rearrange("p c (k n) -> p c k n", k=KV)[:, :, :, (HQ + 1) * HD1:]
                              for w in (wq_hi, wq_lo)]
                        three(bank(4 + j).rearrange("p (k n) -> p k n", k=KV),
                              [lambda c: xT_hi[:, c, P * j:P * (j + 1)], lambda c: xT_lo[:, c, P * j:P * (j + 1)]],
                              [lambda c: wv[0][:, c, :, :], lambda c: wv[1][:, c, :, :]], KC).then_inc(s_v, 1)

                def scores(g):
                    pe.wait_ge(s_qklo, NM * g + NM)
                    for j in range(NB):
                        for k in range(KV):
                            for i, (a, b_) in enumerate(((qk_hi, qk_hi), (qk_hi, qk_lo), (qk_lo, qk_hi))):
                                for o in range(OC):
                                    t = P * j + T8 * o
                                    mm = pe.matmul(
                                        ps[T8 * o:T8 * (o + 1), BANK * j + P * k:BANK * j + P * (k + 1)]
                                        .rearrange("p (h q) -> p h q", q=T8),
                                        a[:, k, HQ, t:t + T8], b_[:, k, 0:HQ, t:t + T8],
                                        start=(i == 0), stop=(i == 2), skip_group_check=True)
                        mm.then_inc(s_sc, 1)

                def outputs(g):
                    pe.wait_ge(s_vev, NB * g + NB)
                    for j in range(NB):
                        n = NB * g + j
                        pe.wait_ge(s_smb, SMB * n + SMB)
                        for k in range(KV):
                            if j:
                                pe.wait_ge(s_olo, KV * (n - 1) + k + 1)
                            pe.matmul(bank(4 + k).rearrange("p (n o q) -> p n o q", o=OC, q=8), v[:, j, k, :],
                                      pT[j % 2][:, k, :, :].rearrange("p o (n q) -> p n o q", q=8),
                                      start=True, stop=True).then_inc(s_pv, 1)

                def project(g):
                    pe.wait_ge(s_olo, NB * KV * (g + 1))
                    pe.wait_ge(s_ohi, NB * KV * (g + 1))
                    pe.wait_ge(s_vev, NB * g + NB)
                    for b in range(B):
                        def o_of(a):
                            return lambda h: a[:, h, P * b:P * (b + 1)]
                        mm = three(bank(4 + b // 2, D, D * (b % 2)), [o_of(oT_hi), o_of(oT_lo)],
                                   [lambda h: wp_hi[:, h, :], lambda h: wp_lo[:, h, :]], H1)
                        if b % 2:
                            mm.then_inc(s_out, 1)

                with pe.Fori(0, G) as g:
                    turn(g)
                    queries_keys(g)
                    scores(g)
                    values(g)
                    outputs(g)
                    project(g)

            @block.scalar
            def _(act):
                with act.Fori(0, G) as g:
                    for c in range(KC):
                        act.wait_ge(s_tp, 2 * g + c + 1)
                        act.activation(xT_hi[:, c, :].rearrange("p (o b q) -> p b o q", b=B, q=8),
                                       bank(4 + c).rearrange("p (b o q) -> p b o q", b=B, q=8),
                                       ACT.Copy).then_inc(s_xhi, 1)
                    for m in range(NM):
                        act.wait_ge(s_qk, NM * g + m + 1)
                        act.activation(qk_hi[:, m // (HQ + 1), m % (HQ + 1), :], bank(4 + m % 4),
                                       ACT.Copy).then_inc(s_qkhi, 1)
                        if m % DQ == DQ - 1:
                            unit_high(act, g, m // DQ)
                    for j in range(NB):
                        act.wait_ge(s_v, NB * g + j + 1)
                        act.activation(v[:, j, :, :], bank(4 + j).rearrange("p (k n) -> p k n", k=KV),
                                       ACT.Copy).then_inc(s_vev, 1)
                    def exponentials(j):
                        n = NB * g + j
                        act.wait_ge(s_sma, SMA * n + SHIFTED)
                        act.activation(sc[j % 2][:, :, :], sc[j % 2][:, :, :], ACT.Exp, scale=SCALE1).then_inc(s_ex, 1)

                    def outputs_hi(j):
                        n = NB * g + j
                        for k in range(KV):
                            act.wait_ge(s_pv, KV * n + k + 1)
                            act.activation(o_tile(oT_hi, j, k), bank(4 + k).rearrange("p (n q) -> p n q", q=T8),
                                           ACT.Copy).then_inc(s_ohi, 1)

                    exponentials(0)
                    for j in range(NB):
                        if j + 1 < NB:
                            exponentials(j + 1)
                        if j:
                            outputs_hi(j - 1)
                    outputs_hi(NB - 1)
                    for i in range(NM // DQ, NU2):
                        unit_high(act, g, i)

            @block.vector
            def _(dve):
                for n in range(2):
                    dve.memset(pT[n][:, :, :, :], 0.0).then_inc(const_v, 1)
                dve.wait_ge(const_v, 2)

                def softmax_a(g, j):
                    n, s, m = NB * g + j, sc[j % 2], mx[j % 2]
                    dve.wait_ge(s_sc, n + 1)
                    reach(dve, s_smb, SMB * (n - 1) if j >= 2 else SMB * NB * g)
                    dve.transpose(s[:, :, :].rearrange("p h q -> p (h q)"), bank(j)).then_inc(s_sma, 1)
                    dve.wait_ge(s_sma, SMA * n + TURNED)
                    dve.tensor_tensor(s[:, :, :], s[:, :, :],
                                      mask[:, :].rearrange("p (o q) -> p o q", o=1).to_broadcast([P, H1, T8]),
                                      ALU.add).then_inc(s_sma, 1)
                    dve.wait_ge(s_sma, SMA * n + MASKED)
                    dve.tensor_reduce(m[:, :], s[:, :, :], AX_X, ALU.max).then_inc(s_sma, 1)
                    dve.wait_ge(s_sma, SMA * n + MAXED)
                    dve.tensor_tensor(s[:, :, :], s[:, :, :],
                                      m[:, :].rearrange("p (h o) -> p h o", o=1).to_broadcast([P, H1, T8]),
                                      ALU.subtract).then_inc(s_sma, 1)

                def softmax_b(g, j):
                    n, s, z = NB * g + j, sc[j % 2], sm[j % 2]
                    dve.wait_ge(s_ex, n + 1)
                    dve.tensor_reduce(z[:, :], s[:, :, :], AX_X, ALU.add).then_inc(s_smb, 1)
                    dve.wait_ge(s_smb, SMB * n + 1)
                    dve.reciprocal(z[:, :], z[:, :]).then_inc(s_smb, 1)
                    dve.wait_ge(s_smb, SMB * n + 2)
                    dve.tensor_tensor(s[:, :, :], s[:, :, :],
                                      z[:, :].rearrange("p (h o) -> p h o", o=1).to_broadcast([P, H1, T8]),
                                      ALU.mult).then_inc(s_smb, 1)
                    dve.wait_ge(s_smb, SMB * n + 3)
                    if j >= 2:
                        dve.wait_ge(s_pv, KV * (n - 1))
                    else:
                        reach(dve, s_pv, KV * NB * g)
                    for o in range(OC):
                        rows = slice(T8 * o, T8 * (o + 1))
                        dve.transpose(pT[j % 2][rows, :, o, :],
                                      s[rows, :, :].rearrange("p (k h) q -> p k (h q)", k=KV)).then_inc(s_smb, 1)

                def outputs_lo(g, j):
                    n = NB * g + j
                    for k in range(KV):
                        dve.wait_ge(s_ohi, KV * n + k + 1)
                        dve.tensor_tensor(o_tile(oT_lo, j, k), bank(4 + k).rearrange("p (n q) -> p n q", q=T8),
                                          o_tile(oT_hi, j, k), ALU.subtract).then_inc(s_olo, 1)

                with dve.Fori(0, G) as g:
                    normalise_ops(lambda b: X[:, b, g, :], dve, X, stats, mv, rstd, xn,
                                  s_stat, s_mv, s_rstd, s_xn, g, passed_dve)
                    for c in range(KC):
                        dve.wait_ge(s_xhi, 2 * g + c + 1)
                        dve.tensor_tensor(xT_lo[:, c, :].rearrange("p (o b q) -> p b o q", b=B, q=8),
                                          bank(4 + c).rearrange("p (b o q) -> p b o q", b=B, q=8),
                                          xT_hi[:, c, :].rearrange("p (o b q) -> p b o q", b=B, q=8),
                                          ALU.subtract).then_inc(s_xlo, 1)
                    more = work_between(unit_pieces(dve, g, range(NU2)))
                    for m in range(NM):
                        dve.wait_ge(s_qkhi, NM * g + m + 1)
                        k, h = m // (HQ + 1), m % (HQ + 1)
                        dve.tensor_tensor(qk_lo[:, k, h, :], bank(4 + m % 4), qk_hi[:, k, h, :],
                                          ALU.subtract).then_inc(s_qklo, 1)
                        more()
                    softmax_a(g, 0)
                    for j in range(NB):
                        if j + 1 < NB:
                            softmax_a(g, j + 1)
                        softmax_b(g, j)
                        if j:
                            outputs_lo(g, j - 1)
                    outputs_lo(g, NB - 1)
                    more(DQ * NU2 - NM)
                    for t in range(2):
                        dve.wait_ge(s_out, 2 * g + t + 1)
                        xr = X[:, 2 * t:2 * t + 2, g, :]
                        dve.tensor_tensor(xr, bank(4 + t).rearrange("p (b n) -> p b n", b=2), xr,
                                          ALU.add).then_inc(s_res, 1)


MT = FF // P
GELU_C = 0.7978845608028654
GELU_A = 0.044715


def layer1_mlp(nc, glob, A):
    X, ps, ident = glob["X"], glob["ps"], glob["ident"]
    passed_dve, passed_pool, passed_sp = glob["passed"]
    with ExitStack() as stack:
        st = Store(nc, stack)
        w_hi = [glob[n] for n in ("gate_hi", "up_hi", "ew_hi")]
        w_lo = [glob[n] for n in ("gate_lo", "up_lo", "ew_lo")]
        dq = Dequant(st, glob["stage"], passed_sp, "down")
        down_hi, down_lo = (w[:, :, :].rearrange("p c (u n) -> p u c n", n=UC) for w in (w_hi[2], w_lo[2]))
        stats = st.sb("stats3", [P, 4, 6], F32)
        mv = st.sb("mv3", [P, 4, 2], F32)
        rstd = st.sb("rstd3", [P, 4], F32)
        half = st.sb("half3", [P, 4], F32)
        xn = st.sb("xn3", [P, 4, D], F32)
        xT_hi = st.sb("xT3_hi", [P, 2, S], BF16)
        xT_lo = st.sb("xT3_lo", [P, 2, S], BF16)
        g2 = [st.sb(f"g2_{n}", [P, S], F32) for n in range(2)]
        th = [st.sb(f"th_{n}", [P, S], F32) for n in range(2)]
        it = [st.sb(f"it_{n}", [P, S], F32) for n in range(2)]
        it_hi = [st.sb(f"it_hi{n}", [P, S], BF16) for n in range(2)]
        it_lo = [st.sb(f"it_lo{n}", [P, S], BF16) for n in range(2)]

        const = st.sem("const3")
        s_stat, s_mv, s_rstd = st.sem("stat3"), st.sem("mv3s"), st.sem("rstd3s")
        s_xn, s_tp, s_xhi, s_xlo = st.sem("xn3s"), st.sem("tp3"), st.sem("xhi3"), st.sem("xlo3")
        s_gu, s_sq, s_in, s_th, s_it, s_ihi, s_ilo, s_dn, s_gate, s_res = (
            st.sem(n) for n in ("gateup", "square", "inner", "tanh", "inter", "interhi", "interlo", "down", "gelu", "res3"))

        def bank(n, width=BANK, off=0):
            return ps[:, n * BANK + off:n * BANK + off + width]

        with nc.Block() as block:

            @block.sync
            def _(sp):
                for u in range(NC):
                    dq.fetch(sp, u, u % 2, A["down_W"][P * u:P * (u + 1), :], A["down_s"][8 * u:8 * (u + 1), :])

            @block.gpsimd
            def _(pool):
                pool.memset(half[:, :], -0.5).then_inc(const, 1)
                with pool.Fori(0, B) as b:
                    rstd_ops(pool, mv, rstd, half, s_mv, s_rstd, b, passed_pool)

            @block.tensor
            def _(pe):
                pe.wait_ge(const, 1)

                def turn(b):
                    pe.wait_ge(s_xn, 4 * b + 4)
                    reach(pe, s_it, MT * b)
                    for c in range(2):
                        for t in range(4):
                            tr = pe.transpose(bank(c, P, P * t), xn[:, t, c:D:2], ident[:, :])
                        tr.then_inc(s_tp, 1)

                def gate_up(b, m):
                    if m >= 3:
                        pe.wait_ge(s_it, MT * b + m - 2)
                    else:
                        reach(pe, s_it, MT * b)
                    for k in range(2):
                        n = 0
                        for c in range(2):
                            for w, x in ((w_hi, xT_hi), (w_hi, xT_lo), (w_lo, xT_hi)):
                                mm = pe.matmul(bank(2 * (m % 3) + k), w[k][:, c, P * m:P * (m + 1)], x[:, c, :],
                                               start=(n == 0), stop=(n == 5))
                                n += 1
                        mm.then_inc(s_gu, 1)

                def down(b, m):
                    pe.wait_ge(s_ilo, MT * b + m + 1)
                    pe.wait_ge(s_ihi, MT * b + m + 1)
                    pe.wait_ge(dq.step, DQ * (m // 2 + 1))
                    if m == 0:
                        reach(pe, s_res, 2 * b)
                    for t in range(4):
                        n = 0
                        for a, w in ((it_hi, w_hi), (it_hi, w_lo), (it_lo, w_hi)):
                            mm = pe.matmul(bank(6 + t // 2, D, D * (t % 2)), a[m % 2][:, P * t:P * (t + 1)],
                                           w[2][:, m % 2, D * (m // 2):D * (m // 2 + 1)],
                                           start=(m == 0 and n == 0 and t % 2 == 0), stop=(m == MT - 1 and n == 2),
                                           skip_group_check=True)
                            n += 1
                    mm.then_inc(s_dn, 1)

                with pe.Fori(0, B) as b:
                    turn(b)
                    pe.wait_ge(s_xhi, 2 * b + 2)
                    pe.wait_ge(s_xlo, 2 * b + 2)
                    for m in range(MT + 2):
                        if m < MT:
                            gate_up(b, m)
                        if m >= 2:
                            down(b, m - 2)

            @block.scalar
            def _(act):
                def batch(b, first):
                    for c in range(2):
                        act.wait_ge(s_tp, 2 * b + c + 1)
                        act.activation(xT_hi[:, c, :], bank(c), ACT.Copy).then_inc(s_xhi, 1)

                    def square(m):
                        n = MT * b + m
                        act.wait_ge(s_gu, 2 * n + 2)
                        reach(act, s_in, n - 1 if m >= 2 else MT * b)
                        act.activation(g2[m % 2][:, :], bank(2 * (m % 3)), ACT.Square, scale=GELU_A ** 0.5).then_inc(s_sq, 1)

                    def tanh(m):
                        n = MT * b + m
                        act.wait_ge(s_in, n + 1)
                        reach(act, s_it, n - 1 if m >= 2 else MT * b)
                        act.activation(th[m % 2][:, :], g2[m % 2][:, :], ACT.Tanh, scale=GELU_C).then_inc(s_th, 1)

                    def high(m):
                        n = MT * b + m
                        act.wait_ge(s_it, n + 1)
                        reach(act, s_dn, n - 1 if m >= 2 else MT * b)
                        act.activation(it_hi[m % 2][:, :], it[m % 2][:, :], ACT.Copy).then_inc(s_ihi, 1)

                    square(0)
                    if first:
                        dq.make_high(act, 0, down_hi[:, 0])
                    for m in range(MT):
                        tanh(m)
                        if m + 1 < MT:
                            square(m + 1)
                        high(m)
                        if first and m % 2 and m + 1 < MT:
                            dq.make_high(act, (m + 1) // 2, down_hi[:, (m + 1) // 2])

                batch(0, True)
                with act.Fori(1, B) as b:
                    batch(b, False)

            @block.vector
            def _(dve):
                def batch(b, first):
                    normalise_ops(lambda t: X[:, b, t, :], dve, X, stats, mv, rstd, xn,
                                  s_stat, s_mv, s_rstd, s_xn, b, passed_dve)
                    for c in range(2):
                        dve.wait_ge(s_xhi, 2 * b + c + 1)
                        dve.tensor_tensor(xT_lo[:, c, :], bank(c), xT_hi[:, c, :], ALU.subtract).then_inc(s_xlo, 1)

                    def inner(m):
                        n = MT * b + m
                        dve.wait_ge(s_sq, n + 1)
                        dve.scalar_tensor_tensor(g2[m % 2][:, :], g2[m % 2][:, :], 1.0, bank(2 * (m % 3)),
                                                 ALU.add, ALU.mult).then_inc(s_in, 1)

                    def inter(m):
                        n = MT * b + m
                        dve.wait_ge(s_th, n + 1)
                        dve.scalar_tensor_tensor(th[m % 2][:, :], th[m % 2][:, :], 1.0, bank(2 * (m % 3)),
                                                 ALU.add, ALU.mult).then_inc(s_gate, 1)
                        dve.wait_ge(s_gate, n + 1)
                        dve.scalar_tensor_tensor(it[m % 2][:, :], th[m % 2][:, :], 0.5, bank(2 * (m % 3) + 1),
                                                 ALU.mult, ALU.mult).then_inc(s_it, 1)

                    def low(m):
                        n = MT * b + m
                        dve.wait_ge(s_ihi, n + 1)
                        reach(dve, s_dn, n - 1 if m >= 2 else MT * b)
                        dve.tensor_tensor(it_lo[m % 2][:, :], it[m % 2][:, :], it_hi[m % 2][:, :], ALU.subtract).then_inc(s_ilo, 1)

                    more = work_between(piece for u in range(NC) for piece in dq.pieces(
                        dve, u, u % 2, u // 2, down_lo[:, u], down_hi[:, u]) if first)
                    inner(0)
                    more(DQ)
                    for m in range(MT):
                        inter(m)
                        more(DQ // 2)
                        if m + 1 < MT:
                            inner(m + 1)
                        low(m)
                    for t in range(2):
                        dve.wait_ge(s_dn, MT * b + MT)
                        xr = X[:, b, 2 * t:2 * t + 2, :]
                        dve.tensor_tensor(xr, bank(6 + t).rearrange("p (t n) -> p t n", t=2), xr,
                                          ALU.add).then_inc(s_res, 1)

                batch(0, True)
                with dve.Fori(1, B) as b:
                    batch(b, False)


def build(nc, A, out, phases=(1, 2, 3, 4)):
    with ExitStack() as stack:
        st = Store(nc, stack)
        X = st.sb("X", [P, B, G, D], F32)
        ident = st.sb("ident", [P, P], F32)
        identb = st.sb("identb", [P, P], BF16)
        ps = stack.enter_context(nc.psum_tensor("ps", [P, 8 * BANK], F32))
        made = st.sem("made")
        layer0_stack = stack.enter_context(ExitStack())
        layer0 = Store(nc, layer0_stack)
        glob = {
            "passed": [st.sem(f"passed_{n}") for n in ("dve", "pool", "sp")],
            "rw_hi": layer0.sb("rw_hi", [P, KC, EO], F32R, "right"), "rw_lo": layer0.sb("rw_lo", [P, KC, EO], F32R, "right"),
            "ew_hi": st.sb("ew_hi", [P, KC, EO], BF16), "ew_lo": st.sb("ew_lo", [P, KC, EO], BF16),
            "stage": st.sb("stage", [P, 2, EO], BF16),
            "X": X, "ps": ps, "ident": ident, "identb": identb,
            "scratch_q": nc.dram_tensor("scratch_q", [2, D, S], BF16, kind="Internal").ap(),
            "scratch_k": nc.dram_tensor("scratch_k", [2, D, S], BF16, kind="Internal").ap(),
        }
        with nc.Block() as block:

            @block.gpsimd
            def _(pool):
                pool.memset(ident[:, :], 0.0).then_inc(made, 1)
                pool.wait_ge(made, 1)
                pool.affine_select(out=ident[:, :], in_=ident[:, :], compare_op=ALU.not_equal, fill=1.0, base=0,
                                   pattern=[[-1, P]], channel_multiplier=1).then_inc(made, 1)
                pool.wait_ge(made, 2)
                pool.tensor_copy(identb[:, :], ident[:, :]).then_inc(made, 1)

        if 1 in phases:
            layer0_attention(nc, glob, A)
        glob |= {
            "wq_hi": st.sb("wq_hi", [P, KC, NW], BF16), "wq_lo": st.sb("wq_lo", [P, KC, NW], BF16),
            "wp_hi": st.sb("wp_hi", [P, H1, D], BF16), "wp_lo": st.sb("wp_lo", [P, H1, D], BF16),
        }
        if 2 in phases:
            layer0_mixture(nc, glob, A)
        glob |= {f"{n}_{part}": st.sb(f"{n}_{part}", [P, 2, FF], BF16) for n in ("gate", "up") for part in ("hi", "lo")}
        layer0_stack.close()
        if 3 in phases:
            layer1_attention(nc, glob, A)
        if 4 in phases:
            layer1_mlp(nc, glob, A)

        stored = st.sem("stored")
        with nc.Block() as block:

            @block.sync
            def _(sp):
                for b in range(B):
                    sp.dma_start(out[b].rearrange("(g p) d -> p g d", p=P), X[:, b, :, :]).then_inc(stored, 16)
                sp.wait_ge(stored, 16 * B)


def layouts(L0_attn_x, L0_attn_w_project, L0_attn_w_out, L0_ffn_router_w, L0_ffn_router_b, L0_ffn_expert_w,
            L0_ffn_expert_b, L1_attn_w_qkv, L1_attn_w_proj, L1_ffn_gate_W_packed, L1_ffn_gate_scales,
            L1_ffn_up_W_packed, L1_ffn_up_scales, L1_ffn_down_W_packed, L1_ffn_down_scales):
    E, O = L0_ffn_expert_b.shape
    return {
        "x": L0_attn_x,
        "w_project": L0_attn_w_project.T,
        "w_out": L0_attn_w_out.T,
        "router_w": L0_ffn_router_w.reshape(O, E, D).transpose(2, 1, 0).reshape(D, E * O),
        "router_b": L0_ffn_router_b.reshape(O, E).T.reshape(1, E * O),
        "expert_w": L0_ffn_expert_w.transpose(2, 0, 1).reshape(D, E * O),
        "expert_b": L0_ffn_expert_b.reshape(1, E * O),
        "w_qkv": L1_attn_w_qkv.T,
        "w_proj": L1_attn_w_proj.T,
        "gate_W": hidden_order(L1_ffn_gate_W_packed).T,
        "gate_s": hidden_order(L1_ffn_gate_scales).T,
        "up_W": hidden_order(L1_ffn_up_W_packed).T,
        "up_s": hidden_order(L1_ffn_up_scales).T,
        "down_W": L1_ffn_down_W_packed.T,
        "down_s": L1_ffn_down_scales.T,
    }


def hidden_order(a):
    n, k = a.shape
    return a.reshape(n // 256, 128, 2, k).transpose(0, 2, 1, 3).reshape(n, k)


def kernel(**inputs):
    import concourse.bacc as bacc
    from concourse.bass_utils import run_bass_kernel_spmd

    arrays = {name: np.ascontiguousarray(a) for name, a in layouts(**{k: np.asarray(v) for k, v in inputs.items()}).items()}
    nc = bacc.Bacc("TRN2", target_bir_lowering=False, num_devices=1)
    A = {name: nc.dram_tensor(f"in_{name}", a.shape, mybir.dt.from_np(a.dtype), kind="ExternalInput").ap()
         for name, a in arrays.items()}
    out = nc.dram_tensor("out", arrays["x"].shape, F32, kind="ExternalOutput").ap()
    build(nc, A, out)
    r = run_bass_kernel_spmd(nc, [{f"in_{name}": a for name, a in arrays.items()}], core_ids=[0])
    return r.results[0]["out"]
```

```python
from contextlib import ExitStack
from itertools import chain, islice

import numpy as np

import concourse.bass as bass
from concourse import mybir

F32 = mybir.dt.float32
F32R = mybir.dt.float32r
BF16 = mybir.dt.bfloat16
I32 = mybir.dt.int32
ALU = mybir.AluOpType
ACT = mybir.ActivationFunctionType
AX_X = mybir.AxisListType.X

P = 128
B = 4
S = 512
D = 256
KC = D // P
G = S // P
BANK = 512
EPS = 1e-5


class Store:

    def __init__(self, nc, stack):
        self.nc, self.stack = nc, stack

    def sb(self, name, shape, dt, side="left"):
        return self.stack.enter_context(self.nc.sbuf_tensor(name, shape, dt, side=side))

    def sem(self, name):
        return self.stack.enter_context(self.nc.semaphore(name))


def reach(eng, sem, value):
    if not (isinstance(value, int) and value <= 0):
        eng.wait_ge(sem, value)


def wait_alone(eng, sem, value, passed):
    eng.wait_ge(sem, value)
    eng.sem_inc(passed, 1)



def work_between(pieces):
    todo = iter(pieces)

    def some(k=1):
        for piece in islice(todo, k):
            piece()
    return some


def interleave(main, n_main, extra, n_extra):
    done = 0
    for i in range(n_main):
        next(main)
        while done * n_main < (i + 1) * n_extra:
            next(extra)
            done += 1


E = 8
EO = E * D
H1 = 16
KV = 4
HQ = H1 // KV
HD1 = 128
GROUP = (HQ + 2) * HD1
NW = KV * GROUP


FF = 2048
UC = 256
NC = FF // UC
DQ = 10


def unit_columns(a, parities=False):
    return a[:, :, :].rearrange("p c (u n) -> p u c n", n=UC) if parities else a[:, :].rearrange("p (u n) -> p u n", n=UC)


class Dequant:

    def __init__(self, st, stage, passed_sp, tag):
        self.passed_sp = passed_sp
        words = stage[:, :, :].rearrange("p a n -> p (a n)").bitcast(I32)
        self.packed = [words[:, UC * n:UC * (n + 1)] for n in (0, 1)]
        self.scales = [words[:, UC * n:UC * (n + 1)].bitcast(F32) for n in (2, 3)]
        self.sign = words[:, 4 * UC:6 * UC].rearrange("p (c n) -> p c n", c=2)
        self.code = words[:, 6 * UC:8 * UC].rearrange("p (c n) -> p c n", c=2)
        self.mag = st.sb(f"mag_{tag}", [P, 2, UC], F32)
        self.load = [st.sem(f"load_unit{n}_{tag}") for n in (0, 1)]
        self.step, self.high = st.sem(f"dequant_{tag}"), st.sem(f"dequant_hi_{tag}")

    def fetch(self, sp, n, parity, w, s):
        if not isinstance(n, int) or n >= 2:
            wait_alone(sp, self.step, DQ * (n - 1), self.passed_sp)
        sp.dma_start(self.packed[parity], w).then_inc(self.load[parity], 16)
        for k in range(8):
            rows = self.scales[parity][16 * k:16 * (k + 1), :]
            sp.dma_start(rows, s[k:k + 1, :].to_broadcast([16, UC])).then_inc(self.load[parity], 16)

    def pieces(self, dve, n, parity, use, w_lo, w_hi):
        p, mag, code = self.packed[parity], self.mag[:, :, :], self.code
        s = self.scales[parity].rearrange("p (o n) -> p o n", o=1).to_broadcast([P, 2, UC])

        def made(k, ins):
            def piece():
                reach(dve, self.step, DQ * n + k)
                if k == 0:
                    dve.wait_ge(self.load[parity], 16 * 9 * (use + 1))
                if k == DQ - 1:
                    dve.wait_ge(self.high, n + 1)
                ins().then_inc(self.step, 1)
            return piece
        i32 = mag.bitcast(I32)
        return [made(k, ins) for k, ins in enumerate([
            lambda: dve.tensor_scalar(self.sign[:, 0, :], p, 28, -2 ** 31, ALU.logical_shift_left, ALU.bitwise_and),
            lambda: dve.tensor_scalar(self.sign[:, 1, :], p, 24, -2 ** 31, ALU.logical_shift_left, ALU.bitwise_and),
            lambda: dve.tensor_scalar(code[:, 0, :], p, 7, None, ALU.bitwise_and),
            lambda: dve.tensor_scalar(code[:, 1, :], p, 4, 7, ALU.logical_shift_right, ALU.bitwise_and),
            lambda: dve.scalar_tensor_tensor(mag, code, 4.0, code, ALU.max, ALU.add),
            lambda: dve.scalar_tensor_tensor(mag, code, 6.0, mag, ALU.max, ALU.add),
            lambda: dve.scalar_tensor_tensor(mag, code, 6.0, mag, ALU.max, ALU.add),
            lambda: dve.scalar_tensor_tensor(mag, mag, -16.0, s, ALU.add, ALU.mult),
            lambda: dve.tensor_tensor(i32, i32, self.sign, ALU.bitwise_xor),
            lambda: dve.scalar_tensor_tensor(w_lo, mag, 0.5, w_hi, ALU.mult, ALU.subtract),
        ])]

    def make_high(self, act, n, w_hi):
        act.wait_ge(self.step, DQ * n + DQ - 1)
        act.activation(w_hi, self.mag[:, :, :], ACT.Copy, scale=0.5).then_inc(self.high, 1)

H0 = 16
HD0 = D // H0
HG = 4
NG = H0 // HG
HB = 32
STK = 4 * HD0
SHIFT = 96
NEG = -3.0e38


def max_units(pair):
    a, b = 2 * pair, 2 * pair + 1
    return [
        [(a, 3, k) for k in range(4)],
        [(b, 3, k) for k in range(4)],
        [(a, 2, k) for k in range(3)] + [(a, 0, 0)],
        [(b, 2, k) for k in range(3)] + [(b, 0, 0)],
        [(a, 1, 0), (a, 1, 1), (b, 1, 0), (b, 1, 1)],
    ]


def max_work(g):
    return [("max", (g, n)) for n in range(10)]


PREPARE = [("xT", 0), ("xT", 1), ("qk", 0), ("qk", 1), ("qk", 2), ("qk", 3)]
START = PREPARE + max_work(0) + max_work(1)[:2] + [("turn", 0)] + max_work(1)[2:]


def bank_work(first, last):
    def behind_turn(g, work):
        return work[:1] + [("turn", g)] + work[1:]
    m = max_work(2)
    prepared = m[:2] + PREPARE[:2] + m[2:3] + PREPARE[2:4] + m[3:4] + PREPARE[4:] + m[4:]
    return [
        [("v", 0), ("v", 1), ("turn", 1)] + (m if last else prepared) + ([] if first else [("proj", 0), ("proj", 1)]),
        behind_turn(2, max_work(3)),
        [("turn", 3)] if last else behind_turn(3, max_work(0)),
        [] if last else behind_turn(0, max_work(1)),
    ]


def in_group(work, den):
    cut = [0] + [round(len(work) * f) for f in (.1, .3, .4, .6, .7, .9, 1)]
    w = [[("work", x) for x in work[a:b]] for a, b in zip(cut, cut[1:])]
    norm = [[("norm", q)] * den for q in range(G)]
    return ([("score", 0)] + w[0] + [("score", 1)] + [("den", 0)] * den + w[1] + [("score", 2)] + w[2] + norm[0]
            + [("score", 3)] + w[3][:1] + norm[1] + w[3][1:] + norm[2] + [("values", 0), ("score", 4)] + w[4] + norm[3]
            + [("values", 1), ("score", 5)] + w[5] + [("values", 2)] + w[6] + [("values", 3)])


def layer0_attention(nc, glob, A):
    X, ps, ident, identb = glob["X"], glob["ps"], glob["ident"], glob["identb"]
    passed_dve, passed_pool, passed_sp = glob["passed"]
    scratch_q, scratch_k = glob["scratch_q"], glob["scratch_k"]
    with ExitStack() as stack:
        st = Store(nc, stack)
        w_f = st.sb("w0_f", [P, KC, 3 * D], F32)
        w_hi = st.sb("w0_hi", [P, KC, 3 * D], BF16)
        w_lo = st.sb("w0_lo", [P, KC, 3 * D], BF16)
        wo = st.sb("wo0", [P, NG, D], F32)
        maskneg = st.sb("maskneg", [P, P], BF16)
        sel = st.sb("sel0", [P, P], F32)
        stats = st.sb("stats0", [P, G, 6], F32)
        mv = st.sb("mv0", [P, G, 2], F32)
        rstd = st.sb("rstd0", [P, G], F32)
        half = st.sb("half0", [P, G], F32)
        xn = st.sb("xn0", [P, G, D], F32)
        xT_hi = st.sb("xT0_hi", [P, KC, S], BF16)
        xT_lo = st.sb("xT0_lo", [P, KC, S], BF16)
        qk_hi = st.sb("qk_hi", [P, 4, S], BF16)
        qk_lo = st.sb("qk_lo", [P, 4, S], BF16)
        qs = st.sb("qs", [SHIFT + 2, H0, S], BF16)
        ks = st.sb("ks", [SHIFT + 2, H0, S], BF16)
        v = st.sb("v0", [P, G, H0, HB], F32)
        bm = st.sb("bm", [P, H0 // 2, 20], F32)
        mx = st.sb("mx", [P, H0, G], F32)
        mt_f = st.sb("mt_f", [HG * G, P], F32)
        mt_hi = st.sb("mt_hi", [HG * G, P], BF16)
        mt_lo = st.sb("mt_lo", [HG * G, P], BF16)
        pt = [st.sb(f"pt{k}", [P, HG, S - P * k], F32) for k in range(G)]
        o_raw = st.sb("o_raw", [P, S], F32)
        rec = st.sb("rec0", [P, S], F32)
        oT = st.sb("oT", [P, NG, S], F32)

        EQ = EO // B
        w_next = st.sb("w_next0", [P, 2, KC, EQ], F32)
        b_next = st.sb("b_next", [2, EQ], F32)
        b_part = st.sb("b_part", [2, 3, EQ], BF16)
        quarters = [(w[:, :, :].rearrange("p c (q n) -> p q c n", q=B)) for w in
                    (glob["rw_hi"], glob["rw_lo"], glob["ew_hi"], glob["ew_lo"])]
        b3_q = glob["stage"][:, :, :].rearrange("r m (q n) -> r q m n", q=B)

        load_next, load_b, s_next, s_b3 = st.sem("load_next0"), st.sem("load_b0"), st.sem("next0"), st.sem("b3")
        NEXT = 9
        STACKED = 16 * 8
        x_first, x_rest = st.sem("x_first"), st.sem("x_rest")
        load, load_wo = st.sem("load0"), st.sem("load0_wo")
        const, const_v = st.sem("const0"), st.sem("const0v")
        wsplit_hi, wsplit_lo = st.sem("wsplit0_hi"), st.sem("wsplit0_lo")
        s_stat, s_mv, s_rstd = st.sem("stat0"), st.sem("mv0s"), st.sem("rstd0s")
        s_xn, s_xhi, s_xlo, s_qkhi = st.sem("xn0s"), st.sem("xhi0"), st.sem("xlo0"), st.sem("qkhi")
        s_scr, s_stk = st.sem("scr"), [st.sem(f"stack{g}") for g in range(NG)]
        s_work, s_taken, s_mx = st.sem("bank_work"), st.sem("bank_taken"), st.sem("row_max")
        s_mthi, s_shift = st.sem("mthi"), st.sem("shift")
        s_st, s_exp, s_msk, s_pv = st.sem("scoreT"), st.sem("expd"), st.sem("masked"), st.sem("pv0")
        s_raw, s_den, s_rec, s_oT = st.sem("raw0"), st.sem("den0"), st.sem("rec0s"), st.sem("oT0")

        MAXB, STB, PVB, SELB = (0, 1), (2, 4), 6, 7
        BATCH_WORK = sum(map(len, bank_work(False, False)))

        def bank(n, width=BANK, off=0):
            return ps[:, n * BANK + off:n * BANK + off + width]

        ST_UNITS = [(0, (0, 1)), (0, (2, 3)), (1, (0, 1)), (1, (2, 3)), (2, (0, 1, 2, 3)), (3, (0, 1, 2, 3))]

        def st_col(u, n):
            kt, heads = ST_UNITS[u]
            width = S - P * kt
            per = BANK // width
            return STB[u % 2] * BANK + (n // per) * BANK + (n % per) * width, width

        def schedule(b, first, last):
            n = len(START) if first else len(START) - 2 + BATCH_WORK * b
            odd = len(START) % 2
            for g, work in enumerate(bank_work(first, last)):
                yield g, in_group(work, not (first and g == 0)), n, odd
                n, odd = n + len(work), (odd + len(work)) % 2

        LAST_WORK = len(START) - 2 + BATCH_WORK * (B - 1) + sum(map(len, bank_work(False, True)))
        assert BATCH_WORK % 2 == 0, "a batch's work starts in the same bank"

        def all_batches(eng, batch):
            batch(0, True, False)
            with eng.Fori(1, B - 1) as b:
                batch(b, False, False)
            batch(B - 1, False, True)

        with nc.Block() as block:

            @block.sync
            def _(sp):
                for b in range(B):
                    sp.dma_start(X[:, b, :, :], A["x"][b].rearrange("(g p) d -> p g d", p=P)).then_inc(
                        x_rest if b else x_first, 16)
                    if b:
                        continue
                    sp.dma_start(w_f[:, :, :], A["w_project"].rearrange("(c p) n -> p c n", p=P)).then_inc(load, 16)
                sp.wait_ge(const_v, 1)
                for h in range(HG):
                    sp.dma_start(wo[HB * h:HB * h + HD0, :, :],
                                 A["w_out"].rearrange("(g i d) n -> i d g n", i=HG, d=HD0)[h]).then_inc(load_wo, 16)

                def copy_parts(b, qk_work):
                    for g in range(NG):
                        if not (isinstance(b, int) and b == 0):
                            wait_alone(sp, s_stk[g], STACKED * b, passed_sp)
                    for n, scr in enumerate((scratch_q, scratch_k)):
                        for part, buf in enumerate((qk_hi, qk_lo)):
                            sp.wait_ge(s_taken, qk_work[2 * n + 1] + 1)
                            sp.dma_start(scr[part].rearrange("(m p) t -> p m t", p=P),
                                         buf[:, 2 * n:2 * n + 2, :]).then_inc(s_scr, 16)
                    wait_alone(sp, s_scr, 64 * b + 64, passed_sp)

                def stack_group(b, g):
                    reach(sp, s_st, 6 * (NG * (b - 1) + g + 1))
                    heads = slice(HG * g, HG * (g + 1))
                    for scr, dst, hi_lo_rows in ((scratch_q, qs, ((0, 2), (1, 3))), (scratch_k, ks, ((0, 1), (2, 3)))):
                        for part, rows in enumerate(hi_lo_rows):
                            for r in rows:
                                sp.dma_start(dst[HD0 * r:HD0 * (r + 1), heads, :],
                                             scr[part].rearrange("(h d) t -> d h t", d=HD0)[:, heads, :]
                                             ).then_inc(s_stk[g], 16)

                def shift_group(t, g, turned):
                    for part, (buf, done, count) in enumerate(((mt_hi, s_mthi, t + 1), (mt_lo, s_taken, turned + 1))):
                        sp.wait_ge(done, count)
                        sp.dma_start(
                            qs[SHIFT + part:SHIFT + part + 1, HG * g:HG * (g + 1), :].rearrange(
                                "o h (j q) -> o (h j) q", q=P),
                            buf[:, :]).then_inc(s_shift, 16)

                copy_parts(0, [START.index(("qk", m)) for m in range(4)])
                for g in range(NG):
                    stack_group(0, g)
                shift_group(0, 0, START.index(("turn", 0)))

                def batch(b, first, last):
                    reach(sp, s_next, NEXT * b)
                    for n, name in enumerate(("router_w", "expert_w")):
                        sp.dma_start(w_next[:, n, :, :], A[name].rearrange("(c p) (q n) -> q p c n", p=P, q=B)[b]
                                     ).then_inc(load_next, 16)
                    for n, name in enumerate(("router_b", "expert_b")):
                        sp.dma_start(b_next[n:n + 1, :], A[name].rearrange("o (q n) -> q o n", q=B)[b]
                                     ).then_inc(load_b, 16)
                    for g, order, n, odd in schedule(b, first, last):
                        work = [x for kind, x in order if kind == "work"]
                        if not (last and g == NG - 1):
                            g_next = (g + 1) % NG
                            shift_group(NG * b + g + 1, g_next, n + work.index(("turn", g_next)))
                        if not last:
                            if g == 0:
                                copy_parts(b + 1, [n + work.index(("qk", m)) for m in range(4)])
                            stack_group(b + 1, g)
                    wait_alone(sp, s_next, NEXT * b + NEXT, passed_sp)
                    for part in range(3):
                        for m in range(2):
                            sp.dma_start(b3_q[part:part + 1, b, m, :], b_part[m:m + 1, part, :]).then_inc(s_b3, 16)

                all_batches(sp, batch)
                sp.wait_ge(s_b3, 96 * B)

            @block.gpsimd
            def _(pool):
                pool.memset(half[:, :], -0.5).then_inc(const, 1)
                pool.memset(maskneg[:, :], 0.0).then_inc(const, 1)
                pool.memset(sel[:, :], 0.0).then_inc(const, 1)
                pool.wait_ge(const, 3)
                pool.affine_select(out=maskneg[:, :], in_=maskneg[:, :], compare_op=ALU.is_ge, fill=NEG, base=0,
                                   pattern=[[-1, P]], channel_multiplier=1).then_inc(const, 1)
                pool.affine_select(out=sel[:, :].rearrange("p (h r) -> p h r", r=HB),
                                   in_=sel[:, :].rearrange("p (h r) -> p h r", r=HB),
                                   compare_op=ALU.not_equal, fill=1.0, base=-HD0,
                                   pattern=[[-HB, HG], [0, HB]], channel_multiplier=1).then_inc(const, 1)

                def split_next(b):
                    def after(n, ins):
                        def piece():
                            if n is not None:
                                wait_alone(pool, s_next, NEXT * b + n, passed_pool)
                            ins().then_inc(s_next, 1)
                        return piece
                    r_hi, r_lo, e_hi, e_lo = (q[:, b] for q in quarters)

                    def first():
                        wait_alone(pool, load_next, 32 * b + 32, passed_pool)
                        pool.tensor_copy(r_hi, w_next[:, 0, :, :]).then_inc(s_next, 1)

                    def first_bias():
                        wait_alone(pool, load_b, 32 * b + 32, passed_pool)
                        if not (isinstance(b, int) and b == 0):
                            wait_alone(pool, s_b3, 96 * b, passed_pool)
                        pool.tensor_copy(b_part[:, 0, :], b_next[:, :]).then_inc(s_next, 1)
                    return [
                        first,
                        after(None, lambda: pool.tensor_copy(e_hi, w_next[:, 1, :, :])),
                        first_bias,
                        after(1, lambda: pool.tensor_tensor(r_lo, w_next[:, 0, :, :], r_hi.bitcast(F32), ALU.subtract)),
                        after(2, lambda: pool.tensor_tensor(e_lo, w_next[:, 1, :, :], e_hi, ALU.subtract)),
                        after(3, lambda: pool.tensor_tensor(b_next[:, :], b_next[:, :], b_part[:, 0, :], ALU.subtract)),
                        after(6, lambda: pool.tensor_copy(b_part[:, 1, :], b_next[:, :])),
                        after(7, lambda: pool.tensor_tensor(b_next[:, :], b_next[:, :], b_part[:, 1, :], ALU.subtract)),
                        after(8, lambda: pool.tensor_copy(b_part[:, 2, :], b_next[:, :])),
                    ]

                def root(b):
                    wait_alone(pool, s_mv, G * b + G, passed_pool)
                    pool.tensor_scalar(rstd[:, :], mv[:, :, 1], EPS, None, ALU.add).then_inc(s_rstd, 1)
                    wait_alone(pool, s_rstd, 2 * b + 1, passed_pool)
                    pool.tensor_tensor(rstd[:, :], rstd[:, :], half[:, :], ALU.pow).then_inc(s_rstd, 1)

                root(0)
                pool.wait_ge(s_rstd, 2)
                pool.memset(ks[SHIFT:SHIFT + 2, :, :], 1.0).then_inc(const, 1)
                pool.wait_ge(const, 6)
                pool.memset(ks[STK:SHIFT, :, :], 0.0).then_inc(const, 1)
                pool.wait_ge(const, 7)
                pool.memset(qs[STK:SHIFT, :, :], 0.0).then_inc(const, 1)

                def batch(b, first, last):
                    more = work_between(split_next(b))
                    if not last:
                        root(b + 1)
                    for g in range(NG):
                        for u, (kt, heads) in enumerate(ST_UNITS):
                            wait_alone(pool, s_exp, 6 * (NG * b + g) + u + 1, passed_pool)
                            t = pt[kt][:, heads[0]:heads[-1] + 1, 0:P]
                            pool.affine_select(out=t, in_=t, compare_op=ALU.is_ge, fill=0.0, base=0,
                                               pattern=[[0, len(heads)], [1, P]],
                                               channel_multiplier=-1).then_inc(s_msk, 1)
                            if g and u % 2:
                                more()

                all_batches(pool, batch)

            @block.tensor
            def _(pe):
                pe.wait_ge(wsplit_hi, 1)
                pe.wait_ge(wsplit_lo, 1)
                pe.wait_ge(const, 5)
                pe.wait_ge(const_v, 3)
                pe.wait_ge(load_wo, 16 * HG)

                def three(out, lhs, rhs):
                    n = 0
                    for c in range(KC):
                        for a, b_ in ((0, 0), (0, 1), (1, 0)):
                            mm = pe.matmul(out, lhs[a](c), rhs[b_](c), start=(n == 0), stop=(n == 3 * KC - 1))
                            n += 1
                    return mm

                def x_transposed(b, c, out):
                    pe.wait_ge(s_xn, G * b + G)
                    for g in range(G):
                        mm = pe.transpose(out(P, P * g), xn[:, g, P * c:P * (c + 1)], ident[:, :])
                    return mm

                def queries_keys(b, m, out):
                    pe.wait_ge(s_xhi, 2 * b + 2)
                    pe.wait_ge(s_xlo, 2 * b + 2)
                    return three(out(), [lambda c: w_hi[:, c, P * m:P * (m + 1)], lambda c: w_lo[:, c, P * m:P * (m + 1)]],
                                 [lambda c: xT_hi[:, c, :], lambda c: xT_lo[:, c, :]])

                def value_rows(half_, out):
                    for t in (2 * half_, 2 * half_ + 1):
                        mm = three(out(D, D * (t % 2)),
                                   [lambda c: xT_hi[:, c, P * t:P * (t + 1)], lambda c: xT_lo[:, c, P * t:P * (t + 1)]],
                                   [lambda c: w_hi[:, c, 2 * D:], lambda c: w_lo[:, c, 2 * D:]])
                    return mm

                def max_scores(b, g, i, o):
                    if i == 0:
                        pe.wait_ge(s_stk[g], STACKED * (b + 1))
                    blocks = max_units(2 * g + i // 5)[i % 5]
                    i = 0
                    while i < 4:
                        h, j, k0 = blocks[i]
                        w = 1
                        while i + w < 4 and blocks[i + w][:2] == (h, j):
                            w += 1
                        pe.matmul(ps[:, o + P * i:o + P * (i + w)], qs[0:SHIFT, h, P * j:P * (j + 1)],
                                  ks[0:SHIFT, h, P * k0:P * (k0 + w)], start=(i == 0), stop=False, skip_group_check=True)
                        i += w
                        mm = pe.matmul(ps[:, o + P * (i - 1):o + P * i], identb[:, :], maskneg[:, :],
                                       start=False, stop=(i == 4), skip_group_check=True)
                    return mm

                def projection(b, half_, out):
                    pe.wait_ge(s_oT, NG * b + NG)
                    for t in (2 * half_, 2 * half_ + 1):
                        for g in range(NG):
                            mm = pe.matmul(out(D, D * (t % 2)), oT[:, g, P * t:P * (t + 1)], wo[:, g, :],
                                           start=(g == 0), stop=(g == NG - 1))
                    return mm

                def turn_max(t, g, out):
                    pe.wait_ge(s_mx, t + 1)
                    return pe.transpose(out(P)[0:HG * G, :],
                                        mx[:, HG * g:HG * (g + 1), :].rearrange("p h j -> p (h j)"), ident[:, :])

                def work(b, n, parity, kind, arg, ahead, t_next=0):
                    reach(pe, s_taken, n - 1)

                    def out(width=BANK, off=0):
                        return bank(MAXB[parity], width, off)
                    mm = {
                        "xT": lambda: x_transposed(ahead, arg, out),
                        "qk": lambda: queries_keys(ahead, arg, out),
                        "v": lambda: value_rows(arg, out),
                        "max": lambda: max_scores(b if arg[0] >= 2 else ahead, arg[0], arg[1], MAXB[parity] * BANK),
                        "turn": lambda: turn_max(t_next, arg, out),
                        "proj": lambda: projection(b - 1, arg, out),
                    }[kind]()
                    mm.then_inc(s_work, 1)

                def score_unit(b, g, u, first):
                    kt, heads = ST_UNITS[u]
                    t = NG * b + g
                    if u == 0:
                        pe.wait_ge(s_shift, 32 * t + 32)
                    reach(pe, s_exp, 6 * t + u - 1)
                    for i, h in enumerate(heads):
                        c, w = st_col(u, i)
                        h += HG * g
                        mm = pe.matmul(ps[:, c:c + w], ks[:, h, P * kt:P * (kt + 1)], qs[:, h, P * kt:],
                                       start=True, stop=True, skip_group_check=True)
                    mm.then_inc(s_st, 1)

                def values(b, g, kt, values_taken):
                    t = NG * b + g
                    pe.wait_ge(s_msk, 6 * t + (2, 4, 5, 6)[kt])
                    if kt == 0:
                        reach(pe, s_raw, t)
                        if g == 0:
                            pe.wait_ge(s_taken, values_taken)
                    for h in range(HG):
                        mm = pe.matmul(ps[HB * h:HB * (h + 1), PVB * BANK + P * kt:(PVB + 1) * BANK],
                                       v[:, kt, HG * g + h, :], pt[kt][:, h, :],
                                       start=(kt == 0), stop=(kt == G - 1), skip_group_check=True)
                    mm.then_inc(s_pv, 1)

                def denominators(t):
                    pe.wait_ge(s_raw, t + 1)
                    reach(pe, s_rec, G * t)
                    pe.matmul(bank(SELB), sel[:, :], o_raw[:, :], start=True, stop=True).then_inc(s_den, 1)

                for n, (kind, arg) in enumerate(START):
                    if n == len(PREPARE):
                        pe.wait_ge(const, 8)
                    work(0, n, n % 2, kind, arg, 0)

                def batch(b, first, last):
                    for g, order, n, odd in schedule(b, first, last):
                        t, i, first_n = NG * b + g, 0, n
                        for kind, arg in order:
                            if kind == "score":
                                score_unit(b, g, arg, first)
                            elif kind == "den":
                                denominators(t - 1)
                            elif kind == "values":
                                values(b, g, arg, first_n + 2)
                            elif kind == "work":
                                work(b, n + i, (odd + i) % 2, *arg, b + 1, t + 1)
                                i += 1

                all_batches(pe, batch)
                denominators(NG * B - 1)
                for t in range(2):
                    work(B, LAST_WORK + t, (LAST_WORK + t) % 2, "proj", t, None)

            @block.scalar
            def _(act):
                act.wait_ge(load, 16)
                act.activation(w_hi[:, :, :], w_f[:, :, :], ACT.Copy).then_inc(wsplit_hi, 1)
                act.wait_ge(const_v, 3)
                def take(b, n, parity, kind, arg):
                    if kind == "xT":
                        act.wait_ge(s_work, n + 1)
                        act.activation(xT_hi[:, arg, :], bank(MAXB[parity]), ACT.Copy).then_inc(s_xhi, 1)
                    if kind == "qk":
                        act.wait_ge(s_work, n + 1)
                        reach(act, s_scr, 64 * b)
                        act.activation(qk_hi[:, arg, :], bank(MAXB[parity]), ACT.Copy,
                                       scale=(HD0 ** -0.5 if arg < 2 else 1.0)).then_inc(s_qkhi, 1)

                for n, (kind, arg) in enumerate(START):
                    take(0, n, n % 2, kind, arg)

                def exponentials(b, g, u):
                    t, (kt, heads) = NG * b + g, ST_UNITS[u]
                    act.wait_ge(s_st, 6 * t + u + 1)
                    reach(act, s_pv, G * (t - 1) + kt + 1)
                    c, w = st_col(u, 0)
                    per = BANK // w
                    src = ps[:, c:c + len(heads) // per * BANK].rearrange(
                        "p (h q) -> p h q", h=len(heads))[:, :, 0:w]
                    act.activation(pt[kt][:, heads[0]:heads[-1] + 1, :], src, ACT.Exp).then_inc(s_exp, 1)

                def batch(b, first, last):
                    for g, order, n, odd in schedule(b, first, last):
                        i = 0
                        for kind, arg in order:
                            if kind == "score":
                                exponentials(b, g, arg)
                            elif kind == "work":
                                take(b + 1, n + i, (odd + i) % 2, *arg)
                                i += 1
                        t = NG * b + g
                        act.wait_ge(s_pv, G * t + G)
                        reach(act, s_oT, t)
                        act.activation(o_raw[:, :], bank(PVB), ACT.Copy).then_inc(s_raw, 1)

                all_batches(act, batch)

            @block.vector
            def _(dve):
                def statistics(b):
                    dve.wait_ge(*((x_first, 16) if isinstance(b, int) and b == 0 else (x_rest, 16 * (B - 1))))
                    for g in range(G):
                        dve.bn_stats(stats[:, g, :], X[:, b, g, :]).then_inc(s_stat, 1)
                    for g in range(G):
                        wait_alone(dve, s_stat, G * b + g + 1, passed_dve)
                        dve.bn_aggr(mv[:, g, :], stats[:, g, :]).then_inc(s_mv, 1)

                dve.memset(wo[:, :, :], 0.0).then_inc(const_v, 1)
                dve.memset(v[:, :, :, :], 0.0).then_inc(const_v, 1)
                dve.wait_ge(const_v, 2)
                dve.memset(v[:, :, :, HD0:HD0 + 1], 1.0).then_inc(const_v, 1)
                statistics(0)
                dve.wait_ge(load, 16)
                dve.wait_ge(wsplit_hi, 1)
                dve.tensor_tensor(w_lo[:, :, :], w_f[:, :, :], w_hi[:, :, :], ALU.subtract).then_inc(wsplit_lo, 1)

                def normalised(b):
                    dve.wait_ge(s_rstd, 2 * b + 2)
                    for g in range(G):
                        dve.tensor_scalar(xn[:, g, :], X[:, b, g, :], mv[:, g, 0:1], rstd[:, g:g + 1],
                                          ALU.subtract, ALU.mult).then_inc(s_xn, 1)

                def take(b, n, parity, kind, arg, ahead, t_next=0):
                    src = bank(MAXB[parity])
                    if kind == "xT":
                        dve.wait_ge(s_xhi, 2 * ahead + arg + 1)
                        ins = dve.tensor_tensor(xT_lo[:, arg, :], src, xT_hi[:, arg, :], ALU.subtract)
                    elif kind == "qk":
                        dve.wait_ge(s_qkhi, 4 * ahead + arg + 1)
                        reach(dve, s_scr, 64 * ahead)
                        ins = dve.scalar_tensor_tensor(qk_lo[:, arg, :], src, (HD0 ** -0.5 if arg < 2 else 1.0),
                                                       qk_hi[:, arg, :], ALU.mult, ALU.subtract)
                    elif kind == "v":
                        dve.wait_ge(s_work, n + 1)
                        ins = dve.tensor_copy(v[:, 2 * arg:2 * arg + 2, :, 0:HD0],
                                              src.rearrange("p (t h d) -> p t h d", t=2, d=HD0))
                    elif kind == "turn":
                        dve.wait_ge(s_work, n + 1)
                        reach(dve, s_shift, 32 * t_next)
                        dve.tensor_scalar(mt_hi[:, :], src[0:HG * G, 0:P], -1.0, None, ALU.mult).then_inc(s_mthi, 1)
                        dve.wait_ge(s_mthi, t_next + 1)
                        ins = dve.scalar_tensor_tensor(mt_lo[:, :], src[0:HG * G, 0:P], -1.0, mt_hi[:, :], ALU.mult,
                                                       ALU.subtract)
                    elif kind == "proj":
                        dve.wait_ge(s_work, n + 1)
                        xr = X[:, b - 1, 2 * arg:2 * arg + 2, :]
                        ins = dve.tensor_tensor(xr, src.rearrange("p (t n) -> p t n", t=2), xr, ALU.add)
                    else:
                        g, i = arg
                        dve.wait_ge(s_work, n + 1)
                        ins = dve.tensor_reduce(bm[:, 2 * g + i // 5, 4 * (i % 5):4 * (i % 5) + 4],
                                                src.rearrange("p (k q) -> p k q", k=4), AX_X, ALU.max)
                    ins.then_inc(s_taken, 1)
                    if kind == "xT":
                        dve.wait_ge(s_taken, n + 1)
                        dve.sem_inc(s_xlo, 1)
                    if kind == "max" and arg[1] == 9:
                        row_max(arg[0], n)

                def row_max(g, n):
                    pr = slice(2 * g, 2 * g + 2)
                    dve.wait_ge(s_taken, n + 1)
                    m4 = mx[:, HG * g:HG * (g + 1), :].rearrange("p (r h) j -> p r h j", h=2)
                    dve.tensor_reduce(m4[:, :, :, 3], bm[:, pr, 0:8].rearrange("p r (h k) -> p r h k", h=2), AX_X, ALU.max)
                    dve.tensor_reduce(m4[:, :, :, 2], bm[:, pr, 8:16].rearrange("p r (h k) -> p r h k", h=2)[:, :, :, 0:3],
                                      AX_X, ALU.max)
                    dve.tensor_reduce(m4[:, :, :, 1], bm[:, pr, 16:20].rearrange("p r (h k) -> p r h k", h=2), AX_X, ALU.max)
                    dve.tensor_copy(m4[:, :, :, 0], bm[:, pr, 8:16].rearrange("p r (h k) -> p r h k", h=2)[:, :, :, 3])\
                       .then_inc(s_mx, 1)

                def normalise(t, g, q):
                    dve.wait_ge(s_den, t + 1)
                    dve.reciprocal(rec[:, P * q:P * (q + 1)], bank(SELB, P, P * q)).then_inc(s_rec, 1)
                    if q == G - 1:
                        dve.wait_ge(s_rec, G * (t + 1))
                        dve.tensor_tensor(oT[:, g, :], o_raw[:, :], rec[:, :], ALU.mult).then_inc(s_oT, 1)

                normalised(0)
                for n, (kind, arg) in enumerate(START):
                    take(0, n, n % 2, kind, arg, 0)

                def batch(b, first, last):
                    if not last:
                        statistics(b + 1)
                    for g, order, n, odd in schedule(b, first, last):
                        i = 0
                        for kind, arg in order:
                            if kind == "norm":
                                normalise(NG * b + g - 1, (g - 1) % NG, arg)
                            elif kind == "work":
                                take(b, n + i, (odd + i) % 2, *arg, b + 1, NG * b + g + 1)
                                i += 1
                                if g == 0 and i == 4 and not last:
                                    normalised(b + 1)

                all_batches(dve, batch)
                for q in range(G):
                    normalise(NG * B - 1, NG - 1, q)
                for t in range(2):
                    take(B, LAST_WORK + t, (LAST_WORK + t) % 2, "proj", t, None)


NU = EO // BANK
CAP = 60.0


def normalise_ops(b_of, dve, X, stats, mv, rstd, xn, s_stat, s_mv, s_rstd, s_xn, i, passed):
    for j in range(4):
        dve.bn_stats(stats[:, j, :], b_of(j)).then_inc(s_stat, 1)
    for j in range(4):
        wait_alone(dve, s_stat, 4 * i + j + 1, passed)
        dve.bn_aggr(mv[:, j, :], stats[:, j, :]).then_inc(s_mv, 1)
    dve.wait_ge(s_rstd, 2 * i + 2)
    for j in range(4):
        dve.tensor_scalar(xn[:, j, :], b_of(j), mv[:, j, 0:1], rstd[:, j:j + 1],
                          ALU.subtract, ALU.mult).then_inc(s_xn, 1)


def rstd_ops(pool, mv, rstd, half, s_mv, s_rstd, i, passed):
    wait_alone(pool, s_mv, 4 * i + 4, passed)
    pool.tensor_scalar(rstd[:, :], mv[:, :, 1], EPS, None, ALU.add).then_inc(s_rstd, 1)
    wait_alone(pool, s_rstd, 2 * i + 1, passed)
    pool.tensor_tensor(rstd[:, :], rstd[:, :], half[:, :], ALU.pow).then_inc(s_rstd, 1)


def layer0_mixture(nc, glob, A):
    X, ps, ident = glob["X"], glob["ps"], glob["ident"]
    passed_dve, passed_pool, passed_sp = glob["passed"]
    with ExitStack() as stack:
        st = Store(nc, stack)
        rw_hi, rw_lo, ew_hi, ew_lo = (glob[n] for n in ("rw_hi", "rw_lo", "ew_hi", "ew_lo"))
        b3 = glob["stage"][0:3, :, :]
        q_next = st.sb("q_next", [P, KC, NW // B], F32)
        p_next = st.sb("p_next", [P, H1 // B, D], F32)
        wq_q = [w[:, :, :].rearrange("p c (q n) -> p q c n", q=B) for w in (glob["wq_hi"], glob["wq_lo"])]
        wp_q = [w[:, :, :].rearrange("p (q h) n -> p q h n", q=B) for w in (glob["wp_hi"], glob["wp_lo"])]
        ones3 = st.sb("ones3", [3, P], BF16)
        code = st.sb("code", [P, E], I32)
        stats = st.sb("stats1", [P, 4, 6], F32)
        mv = st.sb("mv1", [P, 4, 2], F32)
        rstd = st.sb("rstd1", [P, 4], F32)
        half = st.sb("half1", [P, 4], F32)
        xn = st.sb("xn1", [P, 4, D], F32)
        xr_hi = st.sb("xr_hi", [P, KC, S], F32R)
        xr_lo = st.sb("xr_lo", [P, KC, S], F32R)
        xf = st.sb("xf", [P, KC, S], F32)
        xb_hi = [st.sb(f"xb_hi{n}", [P, KC, P], BF16) for n in range(2)]
        xb_lo = [st.sb(f"xb_lo{n}", [P, KC, P], BF16) for n in range(2)]
        lg = [st.sb(f"lg{n}", [P, E, D], F32) for n in range(2)]
        tmp = [st.sb(f"tmp{n}", [P, E, D], F32) for n in range(2)]
        s4, h4 = st.sb("s4", [P, 4, D], F32), st.sb("h4", [P, 4, D], F32)
        h2, a2, c2 = (st.sb(n, [P, 2, D], F32) for n in ("h2", "a2", "c2"))
        m1, n1, c1, inv = (st.sb(n, [P, D], F32) for n in ("m1", "n1", "c1", "inv"))
        m2, dist, e1 = ([st.sb(f"{n}_{k}", [P, D], F32) for k in range(2)] for n in ("m2", "dist", "e1"))
        cw = [st.sb(f"cw{n}", [P, E], F32) for n in range(2)]

        load_next, s_next, const = st.sem("load_next1"), st.sem("next1"), st.sem("const1")
        NEXT = 4
        s_stat, s_mv, s_rstd = st.sem("stat1"), st.sem("mv1s"), st.sem("rstd1s")
        s_xn, s_tp, s_xhi, s_xlo = st.sem("xn1s"), st.sem("tp1"), st.sem("xhi1"), st.sem("xlo1")
        s_xbhi, s_xblo = st.sem("xb1hi"), st.sem("xb1lo")
        s_rt, s_lg, s_top = st.sem("router"), st.sem("logits"), st.sem("topk")
        s_far, s_ed, s_ez, s_kept = st.sem("distances"), st.sem("exp_first"), st.sem("exp_all"), st.sem("kept")
        s_kept_last = st.sem("kept_last")
        s_inv, s_w, s_c, s_u = st.sem("inverse"), st.sem("weights1"), st.sem("summed"), st.sem("experts")

        TOP = 15
        KEPT = 6

        def bank(n, width=BANK, off=0):
            return ps[:, n * BANK + off:n * BANK + off + width]

        def over_experts(a):
            return a[:, :].rearrange("p (o n) -> p o n", o=1).to_broadcast([P, E, D])

        def all_batches(eng, batch):
            batch(0, True, False)
            with eng.Fori(1, B - 1) as b:
                batch(b, False, False)
            batch(B - 1, False, True)

        def tiles(b, last):
            for t in range(4):
                yield t, 4 * b + t, ((b, t + 1) if t < 3 else None if last else (b + 1, 0))

        with nc.Block() as block:

            @block.sync
            def _(sp):
                def batch(b, first, last):
                    reach(sp, s_next, NEXT * b)
                    sp.dma_start(q_next[:, :, :], A["w_qkv"].rearrange("(c p) (q n) -> q p c n", p=P, q=B)[b]
                                 ).then_inc(load_next, 16)
                    sp.dma_start(p_next[:, :, :], A["w_proj"].rearrange("(q h p) n -> q p h n", p=P, q=B)[b]
                                 ).then_inc(load_next, 16)

                all_batches(sp, batch)

            @block.gpsimd
            def _(pool):
                pool.memset(half[:, :], -0.5).then_inc(const, 1)
                pool.memset(ones3[:, :], 1.0).then_inc(const, 1)
                pool.iota(code[:, :], pattern=[[-1, E]], base=E - 1, channel_multiplier=0).then_inc(const, 1)
                def split_next(b, k):
                    if k < 2:
                        wait_alone(pool, load_next, 32 * b + 32, passed_pool)
                    else:
                        wait_alone(pool, s_next, NEXT * b + k - 1, passed_pool)
                    w, (hi, lo) = ((q_next, wq_q), (p_next, wp_q))[k % 2]
                    if k < 2:
                        ins = pool.tensor_copy(hi[:, b], w[:, :, :])
                    else:
                        ins = pool.tensor_tensor(lo[:, b], w[:, :, :], hi[:, b], ALU.subtract)
                    ins.then_inc(s_next, 1)

                def tile_low(n, t):
                    wait_alone(pool, s_xbhi, n + 1, passed_pool)
                    pool.tensor_tensor(xb_lo[t % 2][:, :, :], xf[:, :, P * t:P * (t + 1)], xb_hi[t % 2][:, :, :],
                                       ALU.subtract).then_inc(s_xblo, 1)

                rstd_ops(pool, mv, rstd, half, s_mv, s_rstd, 0, passed_pool)
                tile_low(0, 0)

                def batch(b, first, last):
                    for t, n, after in tiles(b, last):
                        L, far = lg[t % 2], tmp[t % 2]
                        wait_alone(pool, s_top, TOP * n + TOP, passed_pool)
                        pool.tensor_tensor(far[:, :, :], L[:, :, :], over_experts(m2[t % 2]), ALU.subtract).then_inc(s_far, 1)
                        if t == 1 and not last:
                            rstd_ops(pool, mv, rstd, half, s_mv, s_rstd, b + 1, passed_pool)
                        if after:
                            tile_low(n + 1, after[1])
                        wait_alone(pool, s_ez, n + 1, passed_pool)
                        pool.tensor_scalar(far[:, 0:KEPT, :], far[:, 0:KEPT, :], 0.0, None, ALU.is_ge).then_inc(s_kept, 1)
                        wait_alone(pool, s_kept, 3 * n + 1, passed_pool)
                        pool.tensor_tensor(L[:, 0:KEPT, :], L[:, 0:KEPT, :], far[:, 0:KEPT, :], ALU.mult).then_inc(s_kept, 1)
                        wait_alone(pool, s_kept, 3 * n + 2, passed_pool)
                        wait_alone(pool, s_kept_last, n + 1, passed_pool)
                        wait_alone(pool, s_inv, 2 * n + 2, passed_pool)
                        pool.tensor_tensor(L[:, :, :], L[:, :, :], over_experts(inv), ALU.mult).then_inc(s_kept, 1)
                        split_next(b, t)

                all_batches(pool, batch)

            @block.tensor
            def _(pe):
                pe.wait_ge(const, 3)

                def products(out, x_hi, x_lo, w_hi, w_lo, cols, bias):
                    pe.matmul(out, ones3[:, :], bias, start=True, stop=False)
                    for c in range(KC):
                        pe.matmul(out, x_hi(c), w_hi[:, c, cols], start=False, stop=False)
                        pe.matmul(out, x_hi(c), w_lo[:, c, cols], start=False, stop=False)
                        mm = pe.matmul(out, x_lo(c), w_hi[:, c, cols], start=False, stop=(c == KC - 1))
                    return mm

                def x_transposed(b):
                    pe.wait_ge(s_xn, 4 * b + 4)
                    reach(pe, s_lg, NU * 4 * b)
                    for c in range(KC):
                        for t in range(4):
                            tr = pe.transpose(bank(c, P, P * t), xn[:, t, P * c:P * (c + 1)], ident[:, :])
                        tr.then_inc(s_tp, 1)

                def router(b, n, t):
                    if t == 0:
                        pe.wait_ge(s_xhi, 4 * b + 4)
                        pe.wait_ge(s_xlo, 2 * b + 2)
                    tok = slice(P * t, P * (t + 1))
                    for u in range(NU):
                        reach(pe, s_lg, NU * (n - 1) + u + 1)
                        cols = slice(BANK * u, BANK * (u + 1))
                        products(bank(u), lambda c: xr_hi[:, c, tok], lambda c: xr_lo[:, c, tok], rw_hi, rw_lo, cols,
                                 b3[:, 0, cols]).then_inc(s_rt, 1)

                def experts(n, t):
                    pe.wait_ge(s_xbhi, n + 1)
                    pe.wait_ge(s_xblo, n + 1)
                    for u in range(NU):
                        reach(pe, s_c, E * (n - 1) + 2 * (u + 1))
                        cols = slice(BANK * u, BANK * (u + 1))
                        products(bank(4 + u), lambda c: xb_hi[t % 2][:, c, :], lambda c: xb_lo[t % 2][:, c, :],
                                 ew_hi, ew_lo, cols, b3[:, 1, cols]).then_inc(s_u, 1)

                x_transposed(0)
                router(0, 0, 0)

                def batch(b, first, last):
                    for t, n, after in tiles(b, last):
                        if after:
                            router(after[0], n + 1, after[1])
                        if t == 2 and not last:
                            x_transposed(b + 1)
                        experts(n, t)

                all_batches(pe, batch)

            @block.scalar
            def _(act):
                def x_parts(b):
                    reach(act, s_xblo, 4 * b)
                    for c in range(KC):
                        act.wait_ge(s_tp, 2 * b + c + 1)
                        act.activation(xr_hi[:, c, :], bank(c), ACT.Copy).then_inc(s_xhi, 1)
                        act.activation(xf[:, c, :], bank(c), ACT.Copy).then_inc(s_xhi, 1)

                def tile_high(b, n, t):
                    act.wait_ge(s_xhi, 4 * b + 4)
                    reach(act, s_u, NU * (n - 1))
                    act.activation(xb_hi[t % 2][:, :, :], xf[:, :, P * t:P * (t + 1)], ACT.Copy).then_inc(s_xbhi, 1)

                def logits(n, t):
                    for u in range(NU):
                        act.wait_ge(s_rt, NU * n + u + 1)
                        if u == 0:
                            reach(act, s_w, E * (n - 1))
                        act.activation(lg[t % 2][:, 2 * u:2 * u + 2, :],
                                       bank(u).rearrange("p (e o) -> p e o", e=2), ACT.Copy).then_inc(s_lg, 1)

                x_parts(0)
                tile_high(0, 0, 0)
                logits(0, 0)

                def batch(b, first, last):
                    for t, n, after in tiles(b, last):
                        act.wait_ge(s_top, TOP * n + TOP)
                        act.activation(e1[t % 2][:, :], dist[t % 2][:, :], ACT.Exp).then_inc(s_ed, 1)
                        if after:
                            tile_high(after[0], n + 1, after[1])
                            logits(n + 1, after[1])
                        if t == 2 and not last:
                            x_parts(b + 1)
                        act.wait_ge(s_far, n + 1)
                        act.activation(lg[t % 2][:, :, :], tmp[t % 2][:, :, :], ACT.Exp).then_inc(s_ez, 1)
                        act.wait_ge(s_kept, 3 * n + 3)
                        for e in range(E):
                            act.activation(tmp[t % 2][:, e, :], lg[t % 2][:, e, :], ACT.Copy,
                                           accum_out=cw[t % 2][:, e:e + 1]).then_inc(s_w, 1)

                all_batches(act, batch)

            @block.vector
            def _(dve):
                dve.wait_ge(const, 3)

                def statistics(b):
                    for j in range(4):
                        dve.bn_stats(stats[:, j, :], X[:, b, j, :]).then_inc(s_stat, 1)
                    for j in range(4):
                        wait_alone(dve, s_stat, 4 * b + j + 1, passed_dve)
                        dve.bn_aggr(mv[:, j, :], stats[:, j, :]).then_inc(s_mv, 1)

                def normalised(b):
                    dve.wait_ge(s_rstd, 2 * b + 2)
                    for j in range(4):
                        dve.tensor_scalar(xn[:, j, :], X[:, b, j, :], mv[:, j, 0:1], rstd[:, j:j + 1],
                                          ALU.subtract, ALU.mult).then_inc(s_xn, 1)

                def x_low(b):
                    for c in range(KC):
                        dve.wait_ge(s_xhi, 4 * b + 2 * c + 2)
                        dve.tensor_tensor(xr_lo[:, c, :], xf[:, c, :], xr_hi[:, c, :].bitcast(F32), ALU.subtract).then_inc(s_xlo, 1)

                class Steps:
                    def __init__(self, sem, start):
                        self.sem, self.start, self.done = sem, start, 0

                    def free(self, ins):
                        self.done += 1
                        ins.then_inc(self.sem, 1)

                    def step(self, ins):
                        self.free(ins)
                        dve.wait_ge(self.sem, self.start + self.done)

                def keep_last(n, t):
                    dve.wait_ge(s_ez, n + 1)
                    L = lg[t % 2]
                    dve.scalar_tensor_tensor(L[:, KEPT:, :], tmp[t % 2][:, KEPT:, :], 0.0, L[:, KEPT:, :], ALU.is_ge,
                                             ALU.mult).then_inc(s_kept_last, 1)

                def two_greatest(n, t):
                    L, T = lg[t % 2], tmp[t % 2]
                    second = m2[t % 2]
                    Li, Ti = L[:, :, :].bitcast(I32), T[:, :, :].bitcast(I32)
                    do = Steps(s_top, TOP * n)
                    dve.wait_ge(s_lg, NU * n + NU)
                    do.free(dve.scalar_tensor_tensor(
                        Ti, Li, 31, code[:, :].rearrange("p (e o) -> p e o", o=1).to_broadcast([P, E, D]),
                        ALU.arith_shift_right, ALU.bitwise_xor))
                    do.step(dve.tensor_scalar(Li, Li, -8, None, ALU.bitwise_and))
                    do.step(dve.scalar_tensor_tensor(Li, Ti, 7, Li, ALU.bitwise_and, ALU.bitwise_or))
                    yield
                    do.free(dve.tensor_tensor(h4[:, :, :], L[:, 0:4, :], L[:, 4:8, :], ALU.max))
                    do.step(dve.tensor_tensor(s4[:, :, :], L[:, 0:4, :], L[:, 4:8, :], ALU.min))
                    do.free(dve.tensor_tensor(h2[:, :, :], h4[:, 0:2, :], h4[:, 2:4, :], ALU.max))
                    do.step(dve.tensor_tensor(a2[:, :, :], h4[:, 0:2, :], h4[:, 2:4, :], ALU.min))
                    do.step(dve.tensor_tensor(c2[:, :, :], s4[:, 0:2, :], s4[:, 2:4, :], ALU.max))
                    do.step(dve.tensor_tensor(a2[:, :, :], a2[:, :, :], c2[:, :, :], ALU.max))
                    do.free(dve.tensor_tensor(m1[:, :], h2[:, 0, :], h2[:, 1, :], ALU.max))
                    do.free(dve.tensor_tensor(n1[:, :], h2[:, 0, :], h2[:, 1, :], ALU.min))
                    do.step(dve.tensor_tensor(c1[:, :], a2[:, 0, :], a2[:, 1, :], ALU.max))
                    do.step(dve.tensor_tensor(second[:, :], n1[:, :], c1[:, :], ALU.max))
                    do.step(dve.scalar_tensor_tensor(second[:, :], m1[:, :], -CAP, second[:, :], ALU.add, ALU.max))
                    do.free(dve.tensor_tensor(dist[t % 2][:, :], m1[:, :], second[:, :], ALU.subtract))
                    assert do.done == TOP

                def inverse(n, t):
                    dve.wait_ge(s_ed, n + 1)
                    dve.tensor_scalar(e1[t % 2][:, :], e1[t % 2][:, :], 1.0, None, ALU.add).then_inc(s_inv, 1)
                    dve.wait_ge(s_inv, 2 * n + 1)
                    dve.reciprocal(inv[:, :], e1[t % 2][:, :]).then_inc(s_inv, 1)

                def weigh(b, n, t):
                    c_t = cw[t % 2]
                    dve.wait_ge(s_w, E * n + E)
                    x = X[:, b, t, :]
                    for u in range(NU):
                        dve.wait_ge(s_u, NU * n + u + 1)
                        for e in (0, 1):
                            dve.scalar_tensor_tensor(x, bank(4 + u, D, D * e), c_t[:, 2 * u + e:2 * u + e + 1], x,
                                                     ALU.mult, ALU.add).then_inc(s_c, 1)
                            dve.wait_ge(s_c, E * n + 2 * u + e + 1)

                statistics(0)
                normalised(0)
                x_low(0)
                for _ in two_greatest(0, 0):
                    pass
                inverse(0, 0)

                def batch(b, first, last):
                    for t, n, after in tiles(b, last):
                        if t == 1 and not last:
                            statistics(b + 1)
                        if t == 2 and not last:
                            normalised(b + 1)
                        if after:
                            for _ in two_greatest(n + 1, after[1]):
                                keep_last(n, t)
                        else:
                            keep_last(n, t)
                        if t == 2 and not last:
                            x_low(b + 1)
                        weigh(b, n, t)
                        if after:
                            inverse(n + 1, after[1])

                all_batches(dve, batch)


T8 = 32
OC = 4
NB = S // P
SCALE1 = HD1 ** -0.5


def layer1_attention(nc, glob, A):
    X, ps, ident = glob["X"], glob["ps"], glob["ident"]
    passed_dve, passed_pool, passed_sp = glob["passed"]
    with ExitStack() as stack:
        st = Store(nc, stack)
        wq_hi, wq_lo, wp_hi, wp_lo = (glob[n] for n in ("wq_hi", "wq_lo", "wp_hi", "wp_lo"))
        stats = st.sb("stats2", [P, 4, 6], F32)
        mv = st.sb("mv2", [P, 4, 2], F32)
        rstd = st.sb("rstd2", [P, 4], F32)
        half = st.sb("half2", [P, 4], F32)
        xn = st.sb("xn2", [P, 4, D], F32)
        xT_hi = st.sb("xT2_hi", [P, KC, S], BF16)
        xT_lo = st.sb("xT2_lo", [P, KC, S], BF16)
        qk_hi = st.sb("qk1_hi", [P, KV, HQ + 1, S], BF16)
        qk_lo = st.sb("qk1_lo", [P, KV, HQ + 1, S], BF16)
        v = st.sb("v1", [P, NB, KV, HD1], F32)
        mask = st.sb("mask1", [P, T8], F32)
        sc = [st.sb(f"sc{n}", [P, H1, T8], F32) for n in range(2)]
        mx = [st.sb(f"mx1_{n}", [P, H1], F32) for n in range(2)]
        sm = [st.sb(f"sm1_{n}", [P, H1], F32) for n in range(2)]
        pT = [glob[n][:, :, :].rearrange("p c n -> p (c n)").bitcast(F32).rearrange("p (k o n) -> p k o n", k=KV, o=OC)
              for n in ("ew_hi", "ew_lo")]
        oT_hi = st.sb("oT1_hi", [P, H1, S], BF16)
        oT_lo = st.sb("oT1_lo", [P, H1, S], BF16)
        dq = Dequant(st, glob["stage"], passed_sp, "gu")
        UNITS = [(name, k) for k in range(NC // G) for name in ("gate", "up")]
        NU2 = len(UNITS)

        def unit_of(name, g, k, a):
            return a.rearrange("x (g k n) -> g k x n", g=G, n=UC)[g, k]

        def made_of(name, g, k, part):
            return glob[f"{name}_{part}"][:, :, :].rearrange("p c (g k n) -> p g k c n", g=G, n=UC)[:, g, k]

        def unit_pieces(dve, g, units):
            for i in units:
                name, k = UNITS[i]
                yield from dq.pieces(dve, NU2 * g + i, i % 2, NU2 // 2 * g + i // 2,
                                     made_of(name, g, k, "lo"), made_of(name, g, k, "hi"))

        def unit_high(act, g, i):
            dq.make_high(act, NU2 * g + i, made_of(*UNITS[i][:1], g, UNITS[i][1], "hi"))

        const, const_v = st.sem("const2"), st.sem("const2v")
        s_stat, s_mv, s_rstd = st.sem("stat2"), st.sem("mv2s"), st.sem("rstd2s")
        s_xn, s_tp, s_xhi, s_xlo = st.sem("xn2s"), st.sem("tp2"), st.sem("xhi2"), st.sem("xlo2")
        s_qk, s_qkhi, s_qklo = st.sem("qk1"), st.sem("qk1hi"), st.sem("qk1lo")
        s_v, s_vev, s_sc, s_sma, s_smb, s_ex = (
            st.sem(n) for n in ("v1s", "v1ev", "sc1", "shifted1", "softmax1", "exp1"))
        s_pv, s_ohi, s_olo, s_out, s_res = (st.sem(n) for n in ("pv1", "o1hi", "o1lo", "out1", "res1"))
        NM = KV * (HQ + 1)
        SMA, SMB = 4, 7
        TURNED, MASKED, MAXED, SHIFTED = 1, 2, 3, SMA

        def bank(n, width=BANK, off=0):
            return ps[:, n * BANK + off:n * BANK + off + width]

        def o_tile(a, j, k):
            return a[:, HQ * k:HQ * (k + 1), :].rearrange("p h (b t) -> p (h b) t", b=B)[:, :, T8 * j:T8 * (j + 1)]

        def all_rounds(eng, round_):
            round_(0, False)
            with eng.Fori(1, G - 1) as g:
                round_(g, False)
            round_(G - 1, True)

        QK = NM // NB

        with nc.Block() as block:

            @block.sync
            def _(sp):
                def fetch(g, units):
                    for i in units:
                        name, k = UNITS[i]
                        dq.fetch(sp, NU2 * g + i, i % 2, unit_of(name, g, k, A[f"{name}_W"]), unit_of(name, g, k, A[f"{name}_s"]))
                fetch(0, range(NU2))
                with sp.Fori(1, G) as g:
                    fetch(g, range(NU2))

            @block.gpsimd
            def _(pool):
                pool.memset(half[:, :], -0.5).then_inc(const, 1)
                pool.memset(mask[:, :], -1.0e30).then_inc(const, 1)
                for m in range(P // 8):
                    pool.wait_ge(const, 2 + m)
                    mk = mask[:, :].rearrange("p (b q) -> p b q", q=8)
                    pool.affine_select(out=mk, in_=mk, compare_op=ALU.not_equal, fill=0.0, base=-8 * m,
                                       pattern=[[0, 4], [-1, 8]], channel_multiplier=1).then_inc(const, 1)
                rstd_ops(pool, mv, rstd, half, s_mv, s_rstd, 0, passed_pool)
                with pool.Fori(1, G) as g:
                    rstd_ops(pool, mv, rstd, half, s_mv, s_rstd, g, passed_pool)

            @block.tensor
            def _(pe):
                pe.wait_ge(const, 2 + P // 8)
                pe.wait_ge(const_v, 2)

                def three(out, lhs, rhs, chunks, **kw):
                    n = 0
                    for c in range(chunks):
                        for a, b_ in ((0, 0), (0, 1), (1, 0)):
                            mm = pe.matmul(out, lhs[a](c), rhs[b_](c), start=(n == 0), stop=(n == 3 * chunks - 1), **kw)
                            n += 1
                    return mm

                def turn(g):
                    pe.wait_ge(s_xn, 4 * g + 4)
                    reach(pe, s_vev, NB * g)
                    for c in range(KC):
                        for b in range(B):
                            tr = pe.transpose(bank(4 + c, P, P * b), xn[:, b, P * c:P * (c + 1)], ident[:, :])
                        tr.then_inc(s_tp, 1)

                def queries_keys(g, tiles):
                    pe.wait_ge(s_xhi, 2 * g + 2)
                    pe.wait_ge(s_xlo, 2 * g + 2)
                    for m in tiles:
                        if m >= 2:
                            pe.wait_ge(s_qklo, NM * g + m - 1)
                        elif not (isinstance(g, int) and g == 0):
                            pe.wait_ge(s_sma, SMA * (NB * (g - 1) + m) + TURNED)
                        w = GROUP * (m // (HQ + 1)) + HD1 * (m % (HQ + 1))
                        three(bank(m % 2),
                              [lambda c: wq_hi[:, c, w:w + P], lambda c: wq_lo[:, c, w:w + P]],
                              [lambda c: xT_hi[:, c, :], lambda c: xT_lo[:, c, :]], KC).then_inc(s_qk, 1)

                def values(g):
                    reach(pe, s_res, 2 * g)
                    for j in range(NB):
                        wv = [w[:, :, :].rearrange("p c (k n) -> p c k n", k=KV)[:, :, :, (HQ + 1) * HD1:]
                              for w in (wq_hi, wq_lo)]
                        three(bank(4 + j).rearrange("p (k n) -> p k n", k=KV),
                              [lambda c: xT_hi[:, c, P * j:P * (j + 1)], lambda c: xT_lo[:, c, P * j:P * (j + 1)]],
                              [lambda c: wv[0][:, c, :, :], lambda c: wv[1][:, c, :, :]], KC).then_inc(s_v, 1)

                def scores(g):
                    pe.wait_ge(s_qklo, NM * g + NM)
                    for j in range(NB):
                        for k in range(KV):
                            for i, (a, b_) in enumerate(((qk_hi, qk_hi), (qk_hi, qk_lo), (qk_lo, qk_hi))):
                                for o in range(OC):
                                    t = P * j + T8 * o
                                    mm = pe.matmul(
                                        ps[T8 * o:T8 * (o + 1), BANK * j + P * k:BANK * j + P * (k + 1)]
                                        .rearrange("p (h q) -> p h q", q=T8),
                                        a[:, k, HQ, t:t + T8], b_[:, k, 0:HQ, t:t + T8],
                                        start=(i == 0), stop=(i == 2), skip_group_check=True)
                        mm.then_inc(s_sc, 1)

                def outputs(g, j):
                    n = NB * g + j
                    pe.wait_ge(s_vev, NB * g + NB)
                    pe.wait_ge(s_smb, SMB * n + SMB)
                    for k in range(KV):
                        if j:
                            pe.wait_ge(s_olo, KV * (n - 1) + k + 1)
                        pe.matmul(bank(4 + k).rearrange("p (n o q) -> p n o q", o=OC, q=8), v[:, j, k, :],
                                  pT[j % 2][:, k, :, :].rearrange("p o (n q) -> p n o q", q=8),
                                  start=True, stop=True).then_inc(s_pv, 1)

                def project(g):
                    pe.wait_ge(s_olo, NB * KV * (g + 1))
                    pe.wait_ge(s_ohi, NB * KV * (g + 1))
                    pe.wait_ge(s_vev, NB * g + NB)
                    for b in range(B):
                        def o_of(a):
                            return lambda h: a[:, h, P * b:P * (b + 1)]
                        mm = three(bank(4 + b // 2, D, D * (b % 2)), [o_of(oT_hi), o_of(oT_lo)],
                                   [lambda h: wp_hi[:, h, :], lambda h: wp_lo[:, h, :]], H1)
                        if b % 2:
                            mm.then_inc(s_out, 1)

                turn(0)
                queries_keys(0, range(NM))

                def round_(g, last):
                    scores(g)
                    values(g)
                    if not last:
                        turn(g + 1)
                    for j in range(NB):
                        if not last:
                            queries_keys(g + 1, range(QK * j, QK * (j + 1)))
                        outputs(g, j)
                    project(g)

                all_rounds(pe, round_)

            @block.scalar
            def _(act):
                def x_high(g):
                    for c in range(KC):
                        act.wait_ge(s_tp, 2 * g + c + 1)
                        act.activation(xT_hi[:, c, :].rearrange("p (o b q) -> p b o q", b=B, q=8),
                                       bank(4 + c).rearrange("p (b o q) -> p b o q", b=B, q=8),
                                       ACT.Copy).then_inc(s_xhi, 1)

                def queries_keys_high(g, tiles):
                    for m in tiles:
                        act.wait_ge(s_qk, NM * g + m + 1)
                        act.activation(qk_hi[:, m // (HQ + 1), m % (HQ + 1), :], bank(m % 2),
                                       ACT.Copy).then_inc(s_qkhi, 1)

                def value_rows(g):
                    for j in range(NB):
                        act.wait_ge(s_v, NB * g + j + 1)
                        act.activation(v[:, j, :, :], bank(4 + j).rearrange("p (k n) -> p k n", k=KV),
                                       ACT.Copy).then_inc(s_vev, 1)

                def exponentials(g, j):
                    n = NB * g + j
                    act.wait_ge(s_sma, SMA * n + SHIFTED)
                    act.activation(sc[j % 2][:, :, :], sc[j % 2][:, :, :], ACT.Exp, scale=SCALE1).then_inc(s_ex, 1)

                def outputs_hi(g, j):
                    n = NB * g + j
                    for k in range(KV):
                        act.wait_ge(s_pv, KV * n + k + 1)
                        act.activation(o_tile(oT_hi, j, k), bank(4 + k).rearrange("p (n q) -> p n q", q=T8),
                                       ACT.Copy).then_inc(s_ohi, 1)

                x_high(0)
                queries_keys_high(0, range(NM))

                def round_(g, last):
                    exponentials(g, 0)
                    exponentials(g, 1)
                    value_rows(g)
                    if not last:
                        x_high(g + 1)
                    for j in range(NB):
                        if not last:
                            queries_keys_high(g + 1, range(QK * j, QK * (j + 1)))
                        outputs_hi(g, j)
                        if j + 2 < NB:
                            exponentials(g, j + 2)
                    for i in range(NU2):
                        unit_high(act, g, i)

                all_rounds(act, round_)

            @block.vector
            def _(dve):
                for n in range(2):
                    dve.memset(pT[n][:, :, :, :], 0.0).then_inc(const_v, 1)
                dve.wait_ge(const_v, 2)

                def softmax_a(g, j):
                    n, s, m = NB * g + j, sc[j % 2], mx[j % 2]
                    dve.wait_ge(s_sc, n + 1)
                    reach(dve, s_smb, SMB * (n - 1))
                    dve.transpose(s[:, :, :].rearrange("p h q -> p (h q)"), bank(j)).then_inc(s_sma, 1)
                    yield
                    dve.wait_ge(s_sma, SMA * n + TURNED)
                    dve.tensor_tensor(s[:, :, :], s[:, :, :],
                                      mask[:, :].rearrange("p (o q) -> p o q", o=1).to_broadcast([P, H1, T8]),
                                      ALU.add).then_inc(s_sma, 1)
                    yield
                    dve.wait_ge(s_sma, SMA * n + MASKED)
                    dve.tensor_reduce(m[:, :], s[:, :, :], AX_X, ALU.max).then_inc(s_sma, 1)
                    yield
                    dve.wait_ge(s_sma, SMA * n + MAXED)
                    dve.tensor_tensor(s[:, :, :], s[:, :, :],
                                      m[:, :].rearrange("p (h o) -> p h o", o=1).to_broadcast([P, H1, T8]),
                                      ALU.subtract).then_inc(s_sma, 1)
                    yield

                def softmax_b(g, j):
                    n, s, z = NB * g + j, sc[j % 2], sm[j % 2]
                    dve.wait_ge(s_ex, n + 1)
                    dve.tensor_reduce(z[:, :], s[:, :, :], AX_X, ALU.add).then_inc(s_smb, 1)
                    yield
                    dve.wait_ge(s_smb, SMB * n + 1)
                    dve.reciprocal(z[:, :], z[:, :]).then_inc(s_smb, 1)
                    yield
                    dve.wait_ge(s_smb, SMB * n + 2)
                    dve.tensor_tensor(s[:, :, :], s[:, :, :],
                                      z[:, :].rearrange("p (h o) -> p h o", o=1).to_broadcast([P, H1, T8]),
                                      ALU.mult).then_inc(s_smb, 1)
                    yield
                    dve.wait_ge(s_smb, SMB * n + 3)
                    reach(dve, s_pv, KV * (n - 1))
                    for o in range(OC):
                        rows = slice(T8 * o, T8 * (o + 1))
                        dve.transpose(pT[j % 2][rows, :, o, :],
                                      s[rows, :, :].rearrange("p (k h) q -> p k (h q)", k=KV)).then_inc(s_smb, 1)
                        yield

                def outputs_lo(g, j):
                    n = NB * g + j
                    for k in range(KV):
                        dve.wait_ge(s_ohi, KV * n + k + 1)
                        dve.tensor_tensor(o_tile(oT_lo, j, k), bank(4 + k).rearrange("p (n q) -> p n q", q=T8),
                                          o_tile(oT_hi, j, k), ALU.subtract).then_inc(s_olo, 1)
                        yield

                def queries_keys_low(g):
                    for m in range(NM):
                        dve.wait_ge(s_qkhi, NM * g + m + 1)
                        k, h = m // (HQ + 1), m % (HQ + 1)
                        dve.tensor_tensor(qk_lo[:, k, h, :], bank(m % 2), qk_hi[:, k, h, :],
                                          ALU.subtract).then_inc(s_qklo, 1)
                        yield

                def statistics(g):
                    for b in range(B):
                        dve.bn_stats(stats[:, b, :], X[:, b, g, :]).then_inc(s_stat, 1)
                    for b in range(B):
                        wait_alone(dve, s_stat, 4 * g + b + 1, passed_dve)
                        dve.bn_aggr(mv[:, b, :], stats[:, b, :]).then_inc(s_mv, 1)

                def normalised(g):
                    dve.wait_ge(s_rstd, 2 * g + 2)
                    for b in range(B):
                        dve.tensor_scalar(xn[:, b, :], X[:, b, g, :], mv[:, b, 0:1], rstd[:, b:b + 1],
                                          ALU.subtract, ALU.mult).then_inc(s_xn, 1)

                def x_low(g):
                    for c in range(KC):
                        dve.wait_ge(s_xhi, 2 * g + c + 1)
                        dve.tensor_tensor(xT_lo[:, c, :].rearrange("p (o b q) -> p b o q", b=B, q=8),
                                          bank(4 + c).rearrange("p (b o q) -> p b o q", b=B, q=8),
                                          xT_hi[:, c, :].rearrange("p (o b q) -> p b o q", b=B, q=8),
                                          ALU.subtract).then_inc(s_xlo, 1)

                statistics(0)
                normalised(0)
                x_low(0)
                for _ in queries_keys_low(0):
                    pass

                def round_(g, last):
                    if not last:
                        statistics(g + 1)
                    for _ in chain(softmax_a(g, 0), softmax_a(g, 1)):
                        pass
                    if not last:
                        normalised(g + 1)
                        x_low(g + 1)
                    tiles = iter(()) if last else queries_keys_low(g + 1)
                    for main, steps in (
                            (chain(softmax_b(g, 0), softmax_a(g, 2)), SMB + SMA),
                            (chain(softmax_b(g, 1), outputs_lo(g, 0), softmax_a(g, 3)), SMB + KV + SMA),
                            (chain(softmax_b(g, 2), outputs_lo(g, 1)), SMB + KV),
                            (chain(softmax_b(g, 3), outputs_lo(g, 2)), SMB + KV)):
                        interleave(main, steps, tiles, 0 if last else QK)
                    for _ in outputs_lo(g, NB - 1):
                        pass
                    work_between(unit_pieces(dve, g, range(NU2)))(DQ * NU2)
                    for t in range(2):
                        dve.wait_ge(s_out, 2 * g + t + 1)
                        xr = X[:, 2 * t:2 * t + 2, g, :]
                        dve.tensor_tensor(xr, bank(4 + t).rearrange("p (b n) -> p b n", b=2), xr,
                                          ALU.add).then_inc(s_res, 1)

                all_rounds(dve, round_)


MT = FF // P
GELU_C = 0.7978845608028654
GELU_A = 0.044715


def layer1_mlp(nc, glob, A):
    X, ps, ident = glob["X"], glob["ps"], glob["ident"]
    passed_dve, passed_pool, passed_sp = glob["passed"]
    with ExitStack() as stack:
        st = Store(nc, stack)
        w_hi = [glob[n] for n in ("gate_hi", "up_hi", "ew_hi")]
        w_lo = [glob[n] for n in ("gate_lo", "up_lo", "ew_lo")]
        dq = Dequant(st, glob["stage"], passed_sp, "down")
        down_hi, down_lo = (w[:, :, :].rearrange("p c (u n) -> p u c n", n=UC) for w in (w_hi[2], w_lo[2]))
        stats = st.sb("stats3", [P, 4, 6], F32)
        mv = st.sb("mv3", [P, 4, 2], F32)
        rstd = st.sb("rstd3", [P, 4], F32)
        half = st.sb("half3", [P, 4], F32)
        xn = st.sb("xn3", [P, 4, D], F32)
        xT_hi = st.sb("xT3_hi", [P, 2, S], BF16)
        xT_lo = st.sb("xT3_lo", [P, 2, S], BF16)
        g2 = [st.sb(f"g2_{n}", [P, S], F32) for n in range(2)]
        th = [st.sb(f"th_{n}", [P, S], F32) for n in range(2)]
        it = [st.sb(f"it_{n}", [P, S], F32) for n in range(2)]
        it_hi = [st.sb(f"it_hi{n}", [P, S], BF16) for n in range(2)]
        it_lo = [st.sb(f"it_lo{n}", [P, S], BF16) for n in range(2)]

        const = st.sem("const3")
        s_stat, s_mv, s_rstd = st.sem("stat3"), st.sem("mv3s"), st.sem("rstd3s")
        s_xn, s_tp, s_xhi, s_xlo = st.sem("xn3s"), st.sem("tp3"), st.sem("xhi3"), st.sem("xlo3")
        s_gu, s_sq, s_in, s_th, s_it, s_ihi, s_ilo, s_dn, s_gate, s_res = (
            st.sem(n) for n in ("gateup", "square", "inner", "tanh", "inter", "interhi", "interlo", "down", "gelu", "res3"))

        def bank(n, width=BANK, off=0):
            return ps[:, n * BANK + off:n * BANK + off + width]

        with nc.Block() as block:

            @block.sync
            def _(sp):
                for u in range(NC):
                    dq.fetch(sp, u, u % 2, A["down_W"][P * u:P * (u + 1), :], A["down_s"][8 * u:8 * (u + 1), :])

            @block.gpsimd
            def _(pool):
                pool.memset(half[:, :], -0.5).then_inc(const, 1)
                with pool.Fori(0, B) as b:
                    rstd_ops(pool, mv, rstd, half, s_mv, s_rstd, b, passed_pool)

            @block.tensor
            def _(pe):
                pe.wait_ge(const, 1)

                def turn(b):
                    pe.wait_ge(s_xn, 4 * b + 4)
                    reach(pe, s_it, MT * b)
                    for c in range(2):
                        for t in range(4):
                            tr = pe.transpose(bank(c, P, P * t), xn[:, t, c:D:2], ident[:, :])
                        tr.then_inc(s_tp, 1)

                def gate_up(b, m):
                    if m >= 3:
                        pe.wait_ge(s_it, MT * b + m - 2)
                    else:
                        reach(pe, s_it, MT * b)
                    for k in range(2):
                        n = 0
                        for c in range(2):
                            for w, x in ((w_hi, xT_hi), (w_hi, xT_lo), (w_lo, xT_hi)):
                                mm = pe.matmul(bank(2 * (m % 3) + k), w[k][:, c, P * m:P * (m + 1)], x[:, c, :],
                                               start=(n == 0), stop=(n == 5))
                                n += 1
                        mm.then_inc(s_gu, 1)

                def down(b, m):
                    pe.wait_ge(s_ilo, MT * b + m + 1)
                    pe.wait_ge(s_ihi, MT * b + m + 1)
                    pe.wait_ge(dq.step, DQ * (m // 2 + 1))
                    if m == 0:
                        reach(pe, s_res, 2 * b)
                    for t in range(4):
                        n = 0
                        for a, w in ((it_hi, w_hi), (it_hi, w_lo), (it_lo, w_hi)):
                            mm = pe.matmul(bank(6 + t // 2, D, D * (t % 2)), a[m % 2][:, P * t:P * (t + 1)],
                                           w[2][:, m % 2, D * (m // 2):D * (m // 2 + 1)],
                                           start=(m == 0 and n == 0 and t % 2 == 0), stop=(m == MT - 1 and n == 2),
                                           skip_group_check=True)
                            n += 1
                    mm.then_inc(s_dn, 1)

                with pe.Fori(0, B) as b:
                    turn(b)
                    pe.wait_ge(s_xhi, 2 * b + 2)
                    pe.wait_ge(s_xlo, 2 * b + 2)
                    for m in range(MT + 2):
                        if m < MT:
                            gate_up(b, m)
                        if m >= 2:
                            down(b, m - 2)

            @block.scalar
            def _(act):
                def batch(b, first):
                    for c in range(2):
                        act.wait_ge(s_tp, 2 * b + c + 1)
                        act.activation(xT_hi[:, c, :], bank(c), ACT.Copy).then_inc(s_xhi, 1)

                    def square(m):
                        n = MT * b + m
                        act.wait_ge(s_gu, 2 * n + 2)
                        reach(act, s_in, n - 1 if m >= 2 else MT * b)
                        act.activation(g2[m % 2][:, :], bank(2 * (m % 3)), ACT.Square, scale=GELU_A ** 0.5).then_inc(s_sq, 1)

                    def tanh(m):
                        n = MT * b + m
                        act.wait_ge(s_in, n + 1)
                        reach(act, s_it, n - 1 if m >= 2 else MT * b)
                        act.activation(th[m % 2][:, :], g2[m % 2][:, :], ACT.Tanh, scale=GELU_C).then_inc(s_th, 1)

                    def high(m):
                        n = MT * b + m
                        act.wait_ge(s_it, n + 1)
                        reach(act, s_dn, n - 1 if m >= 2 else MT * b)
                        act.activation(it_hi[m % 2][:, :], it[m % 2][:, :], ACT.Copy).then_inc(s_ihi, 1)

                    square(0)
                    if first:
                        dq.make_high(act, 0, down_hi[:, 0])
                    for m in range(MT):
                        tanh(m)
                        if m + 1 < MT:
                            square(m + 1)
                        high(m)
                        if first and m % 2 and m + 1 < MT:
                            dq.make_high(act, (m + 1) // 2, down_hi[:, (m + 1) // 2])

                batch(0, True)
                with act.Fori(1, B) as b:
                    batch(b, False)

            @block.vector
            def _(dve):
                def batch(b, first):
                    normalise_ops(lambda t: X[:, b, t, :], dve, X, stats, mv, rstd, xn,
                                  s_stat, s_mv, s_rstd, s_xn, b, passed_dve)
                    for c in range(2):
                        dve.wait_ge(s_xhi, 2 * b + c + 1)
                        dve.tensor_tensor(xT_lo[:, c, :], bank(c), xT_hi[:, c, :], ALU.subtract).then_inc(s_xlo, 1)

                    def inner(m):
                        n = MT * b + m
                        dve.wait_ge(s_sq, n + 1)
                        dve.scalar_tensor_tensor(g2[m % 2][:, :], g2[m % 2][:, :], 1.0, bank(2 * (m % 3)),
                                                 ALU.add, ALU.mult).then_inc(s_in, 1)

                    def inter(m):
                        n = MT * b + m
                        dve.wait_ge(s_th, n + 1)
                        dve.scalar_tensor_tensor(th[m % 2][:, :], th[m % 2][:, :], 1.0, bank(2 * (m % 3)),
                                                 ALU.add, ALU.mult).then_inc(s_gate, 1)
                        dve.wait_ge(s_gate, n + 1)
                        dve.scalar_tensor_tensor(it[m % 2][:, :], th[m % 2][:, :], 0.5, bank(2 * (m % 3) + 1),
                                                 ALU.mult, ALU.mult).then_inc(s_it, 1)

                    def low(m):
                        n = MT * b + m
                        dve.wait_ge(s_ihi, n + 1)
                        reach(dve, s_dn, n - 1 if m >= 2 else MT * b)
                        dve.tensor_tensor(it_lo[m % 2][:, :], it[m % 2][:, :], it_hi[m % 2][:, :], ALU.subtract).then_inc(s_ilo, 1)

                    more = work_between(piece for u in range(NC) for piece in dq.pieces(
                        dve, u, u % 2, u // 2, down_lo[:, u], down_hi[:, u]) if first)
                    inner(0)
                    more(DQ)
                    for m in range(MT):
                        inter(m)
                        more(DQ // 2)
                        if m + 1 < MT:
                            inner(m + 1)
                        low(m)
                    for t in range(2):
                        dve.wait_ge(s_dn, MT * b + MT)
                        xr = X[:, b, 2 * t:2 * t + 2, :]
                        dve.tensor_tensor(xr, bank(6 + t).rearrange("p (t n) -> p t n", t=2), xr,
                                          ALU.add).then_inc(s_res, 1)

                batch(0, True)
                with dve.Fori(1, B) as b:
                    batch(b, False)


def build(nc, A, out, phases=(1, 2, 3, 4)):
    with ExitStack() as stack:
        st = Store(nc, stack)
        X = st.sb("X", [P, B, G, D], F32)
        ident = st.sb("ident", [P, P], F32)
        identb = st.sb("identb", [P, P], BF16)
        ps = stack.enter_context(nc.psum_tensor("ps", [P, 8 * BANK], F32))
        made = st.sem("made")
        layer0_stack = stack.enter_context(ExitStack())
        layer0 = Store(nc, layer0_stack)
        glob = {
            "passed": [st.sem(f"passed_{n}") for n in ("dve", "pool", "sp")],
            "rw_hi": layer0.sb("rw_hi", [P, KC, EO], F32R, "right"), "rw_lo": layer0.sb("rw_lo", [P, KC, EO], F32R, "right"),
            "ew_hi": st.sb("ew_hi", [P, KC, EO], BF16), "ew_lo": st.sb("ew_lo", [P, KC, EO], BF16),
            "stage": st.sb("stage", [P, 2, EO], BF16),
            "X": X, "ps": ps, "ident": ident, "identb": identb,
            "scratch_q": nc.dram_tensor("scratch_q", [2, D, S], BF16, kind="Internal").ap(),
            "scratch_k": nc.dram_tensor("scratch_k", [2, D, S], BF16, kind="Internal").ap(),
        }
        with nc.Block() as block:

            @block.gpsimd
            def _(pool):
                pool.memset(ident[:, :], 0.0).then_inc(made, 1)
                pool.wait_ge(made, 1)
                pool.affine_select(out=ident[:, :], in_=ident[:, :], compare_op=ALU.not_equal, fill=1.0, base=0,
                                   pattern=[[-1, P]], channel_multiplier=1).then_inc(made, 1)
                pool.wait_ge(made, 2)
                pool.tensor_copy(identb[:, :], ident[:, :]).then_inc(made, 1)

        if 1 in phases:
            layer0_attention(nc, glob, A)
        glob |= {
            "wq_hi": st.sb("wq_hi", [P, KC, NW], BF16), "wq_lo": st.sb("wq_lo", [P, KC, NW], BF16),
            "wp_hi": st.sb("wp_hi", [P, H1, D], BF16), "wp_lo": st.sb("wp_lo", [P, H1, D], BF16),
        }
        if 2 in phases:
            layer0_mixture(nc, glob, A)
        glob |= {f"{n}_{part}": st.sb(f"{n}_{part}", [P, 2, FF], BF16) for n in ("gate", "up") for part in ("hi", "lo")}
        layer0_stack.close()
        if 3 in phases:
            layer1_attention(nc, glob, A)
        if 4 in phases:
            layer1_mlp(nc, glob, A)

        stored = st.sem("stored")
        with nc.Block() as block:

            @block.sync
            def _(sp):
                for b in range(B):
                    sp.dma_start(out[b].rearrange("(g p) d -> p g d", p=P), X[:, b, :, :]).then_inc(stored, 16)
                sp.wait_ge(stored, 16 * B)


def layouts(L0_attn_x, L0_attn_w_project, L0_attn_w_out, L0_ffn_router_w, L0_ffn_router_b, L0_ffn_expert_w,
            L0_ffn_expert_b, L1_attn_w_qkv, L1_attn_w_proj, L1_ffn_gate_W_packed, L1_ffn_gate_scales,
            L1_ffn_up_W_packed, L1_ffn_up_scales, L1_ffn_down_W_packed, L1_ffn_down_scales):
    E, O = L0_ffn_expert_b.shape
    return {
        "x": L0_attn_x,
        "w_project": L0_attn_w_project.T,
        "w_out": L0_attn_w_out.T,
        "router_w": L0_ffn_router_w.reshape(O, E, D).transpose(2, 1, 0).reshape(D, E * O),
        "router_b": L0_ffn_router_b.reshape(O, E).T.reshape(1, E * O),
        "expert_w": L0_ffn_expert_w.transpose(2, 0, 1).reshape(D, E * O),
        "expert_b": L0_ffn_expert_b.reshape(1, E * O),
        "w_qkv": L1_attn_w_qkv.T,
        "w_proj": L1_attn_w_proj.T,
        "gate_W": hidden_order(L1_ffn_gate_W_packed).T,
        "gate_s": hidden_order(L1_ffn_gate_scales).T,
        "up_W": hidden_order(L1_ffn_up_W_packed).T,
        "up_s": hidden_order(L1_ffn_up_scales).T,
        "down_W": L1_ffn_down_W_packed.T,
        "down_s": L1_ffn_down_scales.T,
    }


def hidden_order(a):
    n, k = a.shape
    return a.reshape(n // 256, 128, 2, k).transpose(0, 2, 1, 3).reshape(n, k)


def kernel(**inputs):
    import concourse.bacc as bacc
    from concourse.bass_utils import run_bass_kernel_spmd

    arrays = {name: np.ascontiguousarray(a) for name, a in layouts(**{k: np.asarray(v) for k, v in inputs.items()}).items()}
    nc = bacc.Bacc("TRN2", target_bir_lowering=False, num_devices=1)
    A = {name: nc.dram_tensor(f"in_{name}", a.shape, mybir.dt.from_np(a.dtype), kind="ExternalInput").ap()
         for name, a in arrays.items()}
    out = nc.dram_tensor("out", arrays["x"].shape, F32, kind="ExternalOutput").ap()
    build(nc, A, out)
    r = run_bass_kernel_spmd(nc, [{f"in_{name}": a for name, a in arrays.items()}], core_ids=[0])
    return r.results[0]["out"]
```
